# Optimizing a Trainium2 kernel written in Bass

```python
import numpy as np
import jax
import jax.numpy as jnp

def _softmax(x, axis=-1):
    return jax.nn.softmax(x, axis=axis)

def _gelu(x):
    return jax.nn.gelu(x, approximate=True)

def _silu(x):
    return jax.nn.silu(x)

def _sigmoid(x):
    return jax.nn.sigmoid(x)

def _layernorm(x, axis=-1, eps=1e-05):
    m = jnp.mean(x, axis=axis, keepdims=True)
    v = jnp.var(x, axis=axis, keepdims=True)
    return (x - m) / jnp.sqrt(v + eps)

def _scatter_add(tgt, idx, src, axis=0):
    return tgt.at[idx].add(src)

def _segment_sum(src, seg, n):
    return jax.ops.segment_sum(src, seg, n)
kernel_name = 'mk_xattn_ffn_d4_seqx_r4_d018c2'

def setup_inputs(seed: int=0):
    np.random.seed(seed)
    _w = jnp.asarray

    def _rec_inputs():
        import jax
        import jax.numpy as jnp
        _rk = jax.random.key(seed)
        x = -1.394e-06 + 0.9999 * jax.random.normal(jax.random.fold_in(_rk, 1), (8, 256, 256), jnp.float32)
        _lenS = 256 - jax.random.randint(jax.random.fold_in(_rk, 7), (8,), 0, max(1, 256 // 4) + 1, jnp.int32)
        _lenS2 = 256 - jax.random.randint(jax.random.fold_in(_rk, 8), (8,), 0, max(1, 256 // 4) + 1, jnp.int32)
        _ctx_1024P = jax.random.normal(jax.random.fold_in(_rk, 11), (8, 16, 256), jnp.float32)
        _ctx_1024c = jax.random.dirichlet(jax.random.fold_in(_rk, 511), 0.3 * jnp.ones((16,), jnp.float32), (8, 256))
        _ctx_1024t = jnp.einsum('bsk,bkd->bsd', _ctx_1024c, _ctx_1024P)
        _ctx_1024t = _ctx_1024t * jax.lax.rsqrt(jnp.mean(jnp.square(_ctx_1024t)) + 1e-12) * 0.953939
        ctx_1024 = -0.000292821 + 1.00034 * (_ctx_1024t + 0.3 * jax.random.normal(jax.random.fold_in(_rk, 611), (8, 256, 256), jnp.float32))
        _validS = jnp.arange(256)[None, :] < _lenS[:, None]
        _validS2 = jnp.arange(256)[None, :] < _lenS2[:, None]
        _causal = jnp.tril(jnp.ones((256, 256), dtype=bool))
        mask_BxS2_bk0 = jnp.logical_not(jnp.broadcast_to(_validS2[:, :], (8, 256)))
        mask_Bx1xSxS2_bf0 = jnp.logical_not(jnp.ones((8, 1, 256, 256), dtype=bool))
        return (x, ctx_1024, mask_BxS2_bk0, mask_Bx1xSxS2_bf0)
    x, ctx_1024, mask_BxS2_bk0, mask_Bx1xSxS2_bf0 = _rec_inputs()

    def _L0_xattn_setup():
        import jax, jax.numpy as jnp
        import numpy as np
        EMBED = 256
        HEADS = 16
        HEAD_DIM = EMBED // HEADS

        def _split_heads(x):
            B, S, _ = x.shape
            return x.reshape(B, S, HEADS, HEAD_DIM).transpose(0, 2, 1, 3)
        key = jax.random.key(seed)
        ks = jax.random.split(key, 7)
        B, S = (2, 512)
        return {'key': jax.random.normal(ks[0], (B, S, EMBED), dtype=jnp.float32), 'query': jax.random.normal(ks[1], (B, S, EMBED), dtype=jnp.float32), 'value': jax.random.normal(ks[2], (B, S, EMBED), dtype=jnp.float32), 'Wk': jax.random.normal(ks[3], (EMBED, EMBED), dtype=jnp.float32) * EMBED ** (-0.5), 'Wq': jax.random.normal(ks[4], (EMBED, EMBED), dtype=jnp.float32) * EMBED ** (-0.5), 'Wv': jax.random.normal(ks[5], (EMBED, EMBED), dtype=jnp.float32) * EMBED ** (-0.5), 'Wo': jax.random.normal(ks[6], (EMBED, EMBED), dtype=jnp.float32) * EMBED ** (-0.5), 'mask': 1}
    _L0_xattn_all = _L0_xattn_setup()
    _L0_xattn_in = {k: v for k, v in _L0_xattn_all.items() if k in ('Wk', 'Wq', 'Wv', 'Wo')}
    del _L0_xattn_all

    def _L0_ffn_setup():
        import jax, jax.numpy as jnp
        import numpy as np
        NUM_EXPERTS = 8
        N_EMBD = 256
        D_FF = 4 * N_EMBD
        B, S = (4, 512)
        key = jax.random.key(seed)
        ks = jax.random.split(key, 6)
        x = jax.random.normal(ks[0], (B, S, N_EMBD), dtype=jnp.float32)
        gate_w = jax.random.normal(ks[1], (N_EMBD, NUM_EXPERTS), dtype=jnp.float32) * 0.02
        w1 = jax.random.normal(ks[2], (NUM_EXPERTS, N_EMBD, D_FF), dtype=jnp.float32) * 0.02
        b1 = jnp.zeros((NUM_EXPERTS, D_FF), dtype=jnp.float32)
        w2 = jax.random.normal(ks[3], (NUM_EXPERTS, D_FF, N_EMBD), dtype=jnp.float32) * 0.02
        b2 = jnp.zeros((NUM_EXPERTS, N_EMBD), dtype=jnp.float32)
        return {'x': x, 'gate_w': gate_w, 'w1': w1, 'b1': b1, 'w2': w2, 'b2': b2}
    _L0_ffn_all = _L0_ffn_setup()
    _L0_ffn_in = {k: v for k, v in _L0_ffn_all.items() if k in ('gate_w', 'w1', 'b1', 'w2', 'b2')}
    del _L0_ffn_all

    def _L1_xattn_setup():
        import jax, jax.numpy as jnp
        import numpy as np
        DIM, DIM_HEAD, HEADS, SCALE = (256, 64, 8, 8.0)
        INNER = DIM_HEAD * HEADS
        LN_EPS = 1e-05
        L2_EPS = 1e-12

        def layer_norm(x, w, b):
            mu = jnp.mean(x, axis=-1, keepdims=True)
            var = jnp.mean(jnp.square(x - mu), axis=-1, keepdims=True)
            return (x - mu) * jax.lax.rsqrt(var + LN_EPS) * w + b

        def l2norm(t):
            n = jnp.sqrt(jnp.sum(jnp.square(t), axis=-1, keepdims=True))
            return t / jnp.maximum(n, L2_EPS)
        key = jax.random.key(seed)
        ks = jax.random.split(key, 8)
        b, n, m = (8, 2048, 64)
        x = jax.random.normal(ks[0], (b, n, DIM), dtype=jnp.float32)
        latents = jax.random.normal(ks[1], (b, m, DIM), dtype=jnp.float32)
        mask = jax.random.randint(ks[2], (b, n), 0, 2) > 0
        Wq = jax.random.normal(ks[3], (DIM, INNER), dtype=jnp.float32) * DIM ** (-0.5)
        Wkv = jax.random.normal(ks[4], (DIM, 2 * INNER), dtype=jnp.float32) * DIM ** (-0.5)
        Wo = jax.random.normal(ks[5], (INNER, DIM), dtype=jnp.float32) * INNER ** (-0.5)
        return {'x': x, 'latents': latents, 'mask': mask, 'ln_x_w': jnp.ones((DIM,)), 'ln_x_b': jnp.zeros((DIM,)), 'ln_l_w': jnp.ones((DIM,)), 'ln_l_b': jnp.zeros((DIM,)), 'Wq': Wq, 'Wkv': Wkv, 'q_scale': jnp.ones((DIM_HEAD,)), 'k_scale': jnp.ones((DIM_HEAD,)), 'Wo': Wo, 'ln_o_w': jnp.ones((DIM,)), 'ln_o_b': jnp.zeros((DIM,))}
    _L1_xattn_all = _L1_xattn_setup()
    _L1_xattn_in = {k: v for k, v in _L1_xattn_all.items() if k in ('ln_x_w', 'ln_x_b', 'ln_l_w', 'ln_l_b', 'Wq', 'Wkv', 'q_scale', 'k_scale', 'Wo', 'ln_o_w', 'ln_o_b')}
    del _L1_xattn_all

    def _L1_ffn_setup():
        import jax, jax.numpy as jnp
        import numpy as np

        def _ste(w, w_q):
            return w + jax.lax.stop_gradient(w_q - w)

        def quantize_w8_per(w, axis):
            amax = jnp.clip(jnp.max(jnp.abs(w), axis=axis, keepdims=True), 1e-08, None)
            scale = 127.0 / amax
            w_q = jnp.clip(jnp.round(w * scale), -128.0, 127.0) / scale
            return _ste(w, w_q)

        def quantize_a16(x):
            amax = jnp.clip(jnp.max(jnp.abs(x)), 1e-08, None)
            scale = 32767.0 / amax
            x_q = jnp.clip(jnp.round(x * scale), -32768.0, 32767.0) / scale
            return _ste(x, x_q)
        key = jax.random.key(seed)
        k1, k2, k3 = jax.random.split(key, 3)
        d_model, d_ff = (256, 1024)
        x = jax.random.normal(k1, (4, 512, d_model), dtype=jnp.float32)
        W_in = jax.random.normal(k2, (d_model, d_ff), dtype=jnp.float32) / np.sqrt(d_model)
        b_in = jnp.zeros((d_ff,), dtype=jnp.float32)
        W_out = jax.random.normal(k3, (d_ff, d_model), dtype=jnp.float32) / np.sqrt(d_ff)
        b_out = jnp.zeros((d_model,), dtype=jnp.float32)
        return {'x': x, 'W_in': W_in, 'b_in': b_in, 'W_out': W_out, 'b_out': b_out}
    _L1_ffn_all = _L1_ffn_setup()
    _L1_ffn_in = {k: v for k, v in _L1_ffn_all.items() if k in ('W_in', 'b_in', 'W_out', 'b_out')}
    del _L1_ffn_all

    def _L2_xattn_setup():
        import jax, jax.numpy as jnp
        import numpy as np
        EPS = 1e-05

        def layer_norm(x, w, b):
            mu = jnp.mean(x, axis=-1, keepdims=True)
            var = jnp.mean((x - mu) ** 2, axis=-1, keepdims=True)
            return (x - mu) * jax.lax.rsqrt(var + EPS) * w + b
        key = jax.random.key(seed)
        ks = jax.random.split(key, 8)
        b, Nx, Nz, D = (16, 1024, 64, 256)
        H, Dh = (8, 64)
        inner = H * Dh
        s = 1.0 / np.sqrt(D)
        return {'x': jax.random.normal(ks[0], (b, Nx, D), jnp.float32), 'latents': jax.random.normal(ks[1], (b, Nz, D), jnp.float32), 'ln_media_w': jnp.ones((D,), jnp.float32), 'ln_media_b': jnp.zeros((D,), jnp.float32), 'ln_lat_w': jnp.ones((D,), jnp.float32), 'ln_lat_b': jnp.zeros((D,), jnp.float32), 'Wq': jax.random.normal(ks[2], (D, inner), jnp.float32) * s, 'Wk': jax.random.normal(ks[3], (D, inner), jnp.float32) * s, 'Wv': jax.random.normal(ks[4], (D, inner), jnp.float32) * s, 'Wout': jax.random.normal(ks[5], (inner, D), jnp.float32) * (1.0 / np.sqrt(inner))}
    _L2_xattn_all = _L2_xattn_setup()
    _L2_xattn_in = {k: v for k, v in _L2_xattn_all.items() if k in ('ln_media_w', 'ln_media_b', 'ln_lat_w', 'ln_lat_b', 'Wq', 'Wk', 'Wv', 'Wout')}
    del _L2_xattn_all

    def _L2_ffn_setup():
        import jax, jax.numpy as jnp
        import numpy as np
        B, S, D, H, E, K = (4, 512, 256, 512, 8, 2)
        TEMP = 5.0
        EPS = 1e-09
        key = jax.random.key(seed)
        k_x, k_wg, k_w1, k_w2 = jax.random.split(key, 4)
        scale = 0.02
        return {'x': jax.random.normal(k_x, (B, S, D), dtype=jnp.float32), 'Wg': jax.random.normal(k_wg, (D, E), dtype=jnp.float32) * scale, 'bg': jnp.zeros((E,), dtype=jnp.float32), 'W1': jax.random.normal(k_w1, (E, D, H), dtype=jnp.float32) * scale, 'b1': jnp.zeros((E, H), dtype=jnp.float32), 'W2': jax.random.normal(k_w2, (E, H, D), dtype=jnp.float32) * scale, 'b2': jnp.zeros((E, D), dtype=jnp.float32)}
    _L2_ffn_all = _L2_ffn_setup()
    _L2_ffn_in = {k: v for k, v in _L2_ffn_all.items() if k in ('Wg', 'bg', 'W1', 'b1', 'W2', 'b2')}
    del _L2_ffn_all

    def _L3_xattn_setup():
        import jax, jax.numpy as jnp
        import numpy as np
        B, S, D, H = (2, 512, 256, 16)
        HD = D // H
        LN_EPS = 1e-05

        def _linear(x, w, b):
            return jnp.einsum('bsd,od->bso', x, w) + b

        def _split_heads(x):
            b, s, _ = x.shape
            return x.reshape(b, s, H, HD).transpose(0, 2, 1, 3)
        key = jax.random.key(seed)
        ks = jax.random.split(key, 14)
        w = 0.02
        return {'q': jax.random.normal(ks[0], (B, S, D), jnp.float32), 'k': jax.random.normal(ks[1], (B, S, D), jnp.float32), 'v': jax.random.normal(ks[2], (B, S, D), jnp.float32), 'mask': jnp.zeros((B, 1, S, S), dtype=bool), 'training': 0, 'wq_w': jax.random.normal(ks[3], (D, D), jnp.float32) * w, 'wq_b': jnp.zeros((D,), jnp.float32), 'wk_w': jax.random.normal(ks[4], (D, D), jnp.float32) * w, 'wk_b': jnp.zeros((D,), jnp.float32), 'wv_w': jax.random.normal(ks[5], (D, D), jnp.float32) * w, 'wv_b': jnp.zeros((D,), jnp.float32), 'wo_w': jax.random.normal(ks[6], (D, D), jnp.float32) * w, 'wo_b': jnp.zeros((D,), jnp.float32), 'ln_g': jnp.ones((D,), jnp.float32), 'ln_b': jnp.zeros((D,), jnp.float32)}
    _L3_xattn_all = _L3_xattn_setup()
    _L3_xattn_in = {k: v for k, v in _L3_xattn_all.items() if k in ('wq_w', 'wq_b', 'wk_w', 'wk_b', 'wv_w', 'wv_b', 'wo_w', 'wo_b', 'ln_g', 'ln_b')}
    del _L3_xattn_all

    def _L3_ffn_setup():
        import jax, jax.numpy as jnp
        import numpy as np
        EPS = 1e-05

        def rmsnorm(x):
            return x * jax.lax.rsqrt(jnp.mean(x * x, axis=-1, keepdims=True) + EPS)

        def act_quant(x):
            scale = 127.0 / jnp.clip(jnp.max(jnp.abs(x), axis=-1, keepdims=True), 1e-05)
            q = jnp.clip(jnp.round(x * scale), -128.0, 127.0) / scale
            return x + jax.lax.stop_gradient(q - x)

        def weight_quant(w):
            scale = 1.0 / jnp.clip(jnp.mean(jnp.abs(w)), 1e-05)
            q = jnp.clip(jnp.round(w * scale), -1.0, 1.0) / scale
            return w + jax.lax.stop_gradient(q - w)

        def bitlinear(x, w, b):
            xq = act_quant(rmsnorm(x))
            wq = weight_quant(w)
            return jnp.einsum('bsd,fd->bsf', xq, wq) + b
        key = jax.random.key(seed)
        k0, k1, k2 = jax.random.split(key, 3)
        B, S, D, F = (2, 2048, 256, 1024)
        x = jax.random.normal(k0, (B, S, D), dtype=jnp.float32)
        w1 = jax.random.normal(k1, (F, D), dtype=jnp.float32) * (1.0 / np.sqrt(D))
        b1 = jnp.zeros((F,), dtype=jnp.float32)
        w2 = jax.random.normal(k2, (D, F), dtype=jnp.float32) * (1.0 / np.sqrt(F))
        b2 = jnp.zeros((D,), dtype=jnp.float32)
        return {'x': x, 'w1': w1, 'b1': b1, 'w2': w2, 'b2': b2}
    _L3_ffn_all = _L3_ffn_setup()
    _L3_ffn_in = {k: v for k, v in _L3_ffn_all.items() if k in ('w1', 'b1', 'w2', 'b2')}
    del _L3_ffn_all
    return {'x': x, 'ctx_1024': ctx_1024, 'mask_BxS2_bk0': mask_BxS2_bk0, 'mask_Bx1xSxS2_bf0': mask_Bx1xSxS2_bf0, 'L0_xattn_Wk': _L0_xattn_in['Wk'], 'L0_xattn_Wq': _L0_xattn_in['Wq'], 'L0_xattn_Wv': _L0_xattn_in['Wv'], 'L0_xattn_Wo': _L0_xattn_in['Wo'], 'L0_ffn_gate_w': _L0_ffn_in['gate_w'], 'L0_ffn_w1': _L0_ffn_in['w1'], 'L0_ffn_b1': _L0_ffn_in['b1'], 'L0_ffn_w2': _L0_ffn_in['w2'], 'L0_ffn_b2': _L0_ffn_in['b2'], 'L1_xattn_ln_x_w': _L1_xattn_in['ln_x_w'], 'L1_xattn_ln_x_b': _L1_xattn_in['ln_x_b'], 'L1_xattn_ln_l_w': _L1_xattn_in['ln_l_w'], 'L1_xattn_ln_l_b': _L1_xattn_in['ln_l_b'], 'L1_xattn_Wq': _L1_xattn_in['Wq'], 'L1_xattn_Wkv': _L1_xattn_in['Wkv'], 'L1_xattn_q_scale': _L1_xattn_in['q_scale'], 'L1_xattn_k_scale': _L1_xattn_in['k_scale'], 'L1_xattn_Wo': _L1_xattn_in['Wo'], 'L1_xattn_ln_o_w': _L1_xattn_in['ln_o_w'], 'L1_xattn_ln_o_b': _L1_xattn_in['ln_o_b'], 'L1_ffn_W_in': _L1_ffn_in['W_in'], 'L1_ffn_b_in': _L1_ffn_in['b_in'], 'L1_ffn_W_out': _L1_ffn_in['W_out'], 'L1_ffn_b_out': _L1_ffn_in['b_out'], 'L2_xattn_ln_media_w': _L2_xattn_in['ln_media_w'], 'L2_xattn_ln_media_b': _L2_xattn_in['ln_media_b'], 'L2_xattn_ln_lat_w': _L2_xattn_in['ln_lat_w'], 'L2_xattn_ln_lat_b': _L2_xattn_in['ln_lat_b'], 'L2_xattn_Wq': _L2_xattn_in['Wq'], 'L2_xattn_Wk': _L2_xattn_in['Wk'], 'L2_xattn_Wv': _L2_xattn_in['Wv'], 'L2_xattn_Wout': _L2_xattn_in['Wout'], 'L2_ffn_Wg': _L2_ffn_in['Wg'], 'L2_ffn_bg': _L2_ffn_in['bg'], 'L2_ffn_W1': _L2_ffn_in['W1'], 'L2_ffn_b1': _L2_ffn_in['b1'], 'L2_ffn_W2': _L2_ffn_in['W2'], 'L2_ffn_b2': _L2_ffn_in['b2'], 'L3_xattn_wq_w': _L3_xattn_in['wq_w'], 'L3_xattn_wq_b': _L3_xattn_in['wq_b'], 'L3_xattn_wk_w': _L3_xattn_in['wk_w'], 'L3_xattn_wk_b': _L3_xattn_in['wk_b'], 'L3_xattn_wv_w': _L3_xattn_in['wv_w'], 'L3_xattn_wv_b': _L3_xattn_in['wv_b'], 'L3_xattn_wo_w': _L3_xattn_in['wo_w'], 'L3_xattn_wo_b': _L3_xattn_in['wo_b'], 'L3_xattn_ln_g': _L3_xattn_in['ln_g'], 'L3_xattn_ln_b': _L3_xattn_in['ln_b'], 'L3_ffn_w1': _L3_ffn_in['w1'], 'L3_ffn_b1': _L3_ffn_in['b1'], 'L3_ffn_w2': _L3_ffn_in['w2'], 'L3_ffn_b2': _L3_ffn_in['b2']}

def reference(x, ctx_1024, mask_BxS2_bk0, mask_Bx1xSxS2_bf0, L0_xattn_Wk, L0_xattn_Wq, L0_xattn_Wv, L0_xattn_Wo, L0_ffn_gate_w, L0_ffn_w1, L0_ffn_b1, L0_ffn_w2, L0_ffn_b2, L1_xattn_ln_x_w, L1_xattn_ln_x_b, L1_xattn_ln_l_w, L1_xattn_ln_l_b, L1_xattn_Wq, L1_xattn_Wkv, L1_xattn_q_scale, L1_xattn_k_scale, L1_xattn_Wo, L1_xattn_ln_o_w, L1_xattn_ln_o_b, L1_ffn_W_in, L1_ffn_b_in, L1_ffn_W_out, L1_ffn_b_out, L2_xattn_ln_media_w, L2_xattn_ln_media_b, L2_xattn_ln_lat_w, L2_xattn_ln_lat_b, L2_xattn_Wq, L2_xattn_Wk, L2_xattn_Wv, L2_xattn_Wout, L2_ffn_Wg, L2_ffn_bg, L2_ffn_W1, L2_ffn_b1, L2_ffn_W2, L2_ffn_b2, L3_xattn_wq_w, L3_xattn_wq_b, L3_xattn_wk_w, L3_xattn_wk_b, L3_xattn_wv_w, L3_xattn_wv_b, L3_xattn_wo_w, L3_xattn_wo_b, L3_xattn_ln_g, L3_xattn_ln_b, L3_ffn_w1, L3_ffn_b1, L3_ffn_w2, L3_ffn_b2):
    import jax
    import jax.numpy as jnp

    def _L0_xattn_ref(key, query, value, Wk, Wq, Wv, Wo, mask):
        import jax, jax.numpy as jnp
        import numpy as np
        EMBED = 256
        HEADS = 16
        HEAD_DIM = EMBED // HEADS

        def _split_heads(x):
            B, S, _ = x.shape
            return x.reshape(B, S, HEADS, HEAD_DIM).transpose(0, 2, 1, 3)
        k = _split_heads(key @ Wk.T)
        q = _split_heads(query @ Wq.T)
        v = _split_heads(value @ Wv.T)
        scale = 1.0 / jnp.sqrt(jnp.float32(EMBED))
        scores = jnp.einsum('bhqd,bhkd->bhqk', q, k) * scale
        S = scores.shape[-1]
        if mask:
            causal = jnp.triu(jnp.full((S, S), -100000.0, dtype=jnp.float32), k=1)
            scores = scores + causal
        attn = jax.nn.softmax(scores, axis=-1)
        out = jnp.einsum('bhqk,bhkd->bhqd', attn, v)
        B = out.shape[0]
        out = out.transpose(0, 2, 1, 3).reshape(B, S, EMBED)
        return out @ Wo.T

    def _L0_ffn_ref(x, gate_w, w1, b1, w2, b2):
        import jax, jax.numpy as jnp
        import numpy as np
        NUM_EXPERTS = 8
        N_EMBD = 256
        D_FF = 4 * N_EMBD
        B, S = (4, 512)
        Bb, Ss, D = x.shape
        x_flat = x.reshape(-1, D)
        router_logits = x_flat @ gate_w
        router_probs = jax.nn.softmax(router_logits, axis=-1)
        expert_idx = jnp.argmax(router_probs, axis=-1)
        expert_w = jnp.take_along_axis(router_probs, expert_idx[:, None], axis=1)[:, 0]
        out = jnp.zeros_like(x_flat)
        for e in range(NUM_EXPERTS):
            h = jax.nn.gelu(x_flat @ w1[e] + b1[e], approximate=False)
            y = h @ w2[e] + b2[e]
            sel = expert_idx == e
            out = out + jnp.where(sel, expert_w, 0.0)[:, None] * y
        return out.reshape(Bb, Ss, D)

    def _L1_xattn_ref(x, latents, mask, ln_x_w, ln_x_b, ln_l_w, ln_l_b, Wq, Wkv, q_scale, k_scale, Wo, ln_o_w, ln_o_b):
        import jax, jax.numpy as jnp
        import numpy as np
        DIM, DIM_HEAD, HEADS, SCALE = (256, 64, 8, 8.0)
        INNER = DIM_HEAD * HEADS
        LN_EPS = 1e-05
        L2_EPS = 1e-12

        def layer_norm(x, w, b):
            mu = jnp.mean(x, axis=-1, keepdims=True)
            var = jnp.mean(jnp.square(x - mu), axis=-1, keepdims=True)
            return (x - mu) * jax.lax.rsqrt(var + LN_EPS) * w + b

        def l2norm(t):
            n = jnp.sqrt(jnp.sum(jnp.square(t), axis=-1, keepdims=True))
            return t / jnp.maximum(n, L2_EPS)
        b, n, _ = x.shape
        m = latents.shape[1]
        x = layer_norm(x, ln_x_w, ln_x_b)
        latents = layer_norm(latents, ln_l_w, ln_l_b)
        q = latents @ Wq
        kv_input = jnp.concatenate([x, latents], axis=1)
        kv = kv_input @ Wkv
        k, v = jnp.split(kv, 2, axis=-1)

        def to_heads(t):
            return t.reshape(t.shape[0], t.shape[1], HEADS, DIM_HEAD).transpose(0, 2, 1, 3)
        q, k, v = map(to_heads, (q, k, v))
        q = l2norm(q) * q_scale
        k = l2norm(k) * k_scale
        sim = jnp.einsum('bhid,bhjd->bhij', q, k) * SCALE
        full_mask = jnp.concatenate([mask, jnp.ones((b, m), dtype=bool)], axis=1)[:, None, None, :]
        max_neg = -jnp.finfo(sim.dtype).max
        sim = jnp.where(full_mask, sim, max_neg)
        attn = jax.nn.softmax(sim.astype(jnp.float32), axis=-1).astype(sim.dtype)
        out = jnp.einsum('bhij,bhjd->bhid', attn, v)
        out = out.transpose(0, 2, 1, 3).reshape(b, m, INNER)
        return layer_norm(out @ Wo, ln_o_w, ln_o_b)

    def _L1_ffn_ref(x, W_in, b_in, W_out, b_out):
        import jax, jax.numpy as jnp
        import numpy as np

        def _ste(w, w_q):
            return w + jax.lax.stop_gradient(w_q - w)

        def quantize_w8_per(w, axis):
            amax = jnp.clip(jnp.max(jnp.abs(w), axis=axis, keepdims=True), 1e-08, None)
            scale = 127.0 / amax
            w_q = jnp.clip(jnp.round(w * scale), -128.0, 127.0) / scale
            return _ste(w, w_q)

        def quantize_a16(x):
            amax = jnp.clip(jnp.max(jnp.abs(x)), 1e-08, None)
            scale = 32767.0 / amax
            x_q = jnp.clip(jnp.round(x * scale), -32768.0, 32767.0) / scale
            return _ste(x, x_q)
        W_in_sim = quantize_w8_per(W_in, axis=0)
        W_out_sim = quantize_w8_per(W_out, axis=1)
        x_sim = quantize_a16(x)
        hidden = jax.nn.gelu(x_sim @ W_in_sim + b_in, approximate=False)
        hidden_sim = quantize_a16(hidden)
        out = hidden_sim @ W_out_sim + b_out
        return out

    def _L2_xattn_ref(x, latents, ln_media_w, ln_media_b, ln_lat_w, ln_lat_b, Wq, Wk, Wv, Wout):
        import jax, jax.numpy as jnp
        import numpy as np
        EPS = 1e-05

        def layer_norm(x, w, b):
            mu = jnp.mean(x, axis=-1, keepdims=True)
            var = jnp.mean((x - mu) ** 2, axis=-1, keepdims=True)
            return (x - mu) * jax.lax.rsqrt(var + EPS) * w + b
        H, Dh = (8, 64)
        scale = Dh ** (-0.5)
        b, Nz, D = latents.shape
        xn = layer_norm(x, ln_media_w, ln_media_b)
        zn = layer_norm(latents, ln_lat_w, ln_lat_b)
        q = (zn @ Wq).reshape(b, Nz, H, Dh).transpose(0, 2, 1, 3)
        kv_in = jnp.concatenate([xn, zn], axis=1)
        F = kv_in.shape[1]
        k = (kv_in @ Wk).reshape(b, F, H, Dh).transpose(0, 2, 1, 3)
        v = (kv_in @ Wv).reshape(b, F, H, Dh).transpose(0, 2, 1, 3)
        sim = jnp.einsum('bhqd,bhfd->bhqf', q * scale, k)
        alphas = jax.nn.softmax(sim, axis=-1)
        out = jnp.einsum('bhqf,bhfd->bhqd', alphas, v)
        out = out.transpose(0, 2, 1, 3).reshape(b, Nz, H * Dh)
        return out @ Wout

    def _L2_ffn_ref(x, Wg, bg, W1, b1, W2, b2):
        import jax, jax.numpy as jnp
        import numpy as np
        B, S, D, H, E, K = (4, 512, 256, 512, 8, 2)
        TEMP = 5.0
        EPS = 1e-09
        logits = jnp.einsum('bsd,de->bse', x, Wg) + bg
        probs = jax.nn.softmax(logits / TEMP, axis=-1)
        vals, idx = jax.lax.top_k(probs, K)
        onehot = jax.nn.one_hot(idx, E, dtype=x.dtype)
        mask = jnp.einsum('bske,bsk->bse', onehot, vals)
        gates = mask / (jnp.sum(mask, axis=-1, keepdims=True) + EPS)
        h = jax.nn.gelu(jnp.einsum('bsd,edh->besh', x, W1) + b1[None, :, None, :], approximate=False)
        out = jnp.einsum('besh,ehd->besd', h, W2) + b2[None, :, None, :]
        y = jnp.einsum('bse,besd->bsd', gates, out)
        return y

    def _L3_xattn_ref(q, k, v, mask, training, wq_w, wq_b, wk_w, wk_b, wv_w, wv_b, wo_w, wo_b, ln_g, ln_b):
        import jax, jax.numpy as jnp
        import numpy as np
        B, S, D, H = (2, 512, 256, 16)
        HD = D // H
        LN_EPS = 1e-05

        def _linear(x, w, b):
            return jnp.einsum('bsd,od->bso', x, w) + b

        def _split_heads(x):
            b, s, _ = x.shape
            return x.reshape(b, s, H, HD).transpose(0, 2, 1, 3)
        residual = q
        Q = _split_heads(_linear(q, wq_w, wq_b))
        K = _split_heads(_linear(k, wk_w, wk_b))
        V = _split_heads(_linear(v, wv_w, wv_b))
        dk = jnp.sqrt(jnp.asarray(HD, jnp.float16)).astype(jnp.float32) + 1e-08
        score = jnp.einsum('bhqd,bhkd->bhqk', Q, K) / dk
        attn = jnp.where(mask, -jnp.inf, score)
        ctx = jnp.einsum('bhqk,bhkd->bhqd', attn, V)
        b, _, s, _ = ctx.shape
        ctx = ctx.transpose(0, 2, 1, 3).reshape(b, s, D)
        o = _linear(ctx, wo_w, wo_b)
        x = residual + o
        mu = jnp.mean(x, axis=-1, keepdims=True)
        var = jnp.mean(jnp.square(x - mu), axis=-1, keepdims=True)
        return ln_g * (x - mu) * jax.lax.rsqrt(var + LN_EPS) + ln_b

    def _L3_ffn_ref(x, w1, b1, w2, b2):
        import jax, jax.numpy as jnp
        import numpy as np
        EPS = 1e-05

        def rmsnorm(x):
            return x * jax.lax.rsqrt(jnp.mean(x * x, axis=-1, keepdims=True) + EPS)

        def act_quant(x):
            scale = 127.0 / jnp.clip(jnp.max(jnp.abs(x), axis=-1, keepdims=True), 1e-05)
            q = jnp.clip(jnp.round(x * scale), -128.0, 127.0) / scale
            return x + jax.lax.stop_gradient(q - x)

        def weight_quant(w):
            scale = 1.0 / jnp.clip(jnp.mean(jnp.abs(w)), 1e-05)
            q = jnp.clip(jnp.round(w * scale), -1.0, 1.0) / scale
            return w + jax.lax.stop_gradient(q - w)

        def bitlinear(x, w, b):
            xq = act_quant(rmsnorm(x))
            wq = weight_quant(w)
            return jnp.einsum('bsd,fd->bsf', xq, wq) + b
        h = bitlinear(x, w1, b1)
        h = jax.nn.gelu(h, approximate=False)
        return bitlinear(h, w2, b2)
    x = x + _L0_xattn_ref(ctx_1024, _layernorm(x, axis=-1), ctx_1024, L0_xattn_Wk, L0_xattn_Wq, L0_xattn_Wv, L0_xattn_Wo, 1)
    x = x + _L0_ffn_ref(_layernorm(x, axis=-1), L0_ffn_gate_w, L0_ffn_w1, L0_ffn_b1, L0_ffn_w2, L0_ffn_b2)
    x = x + _L1_xattn_ref(ctx_1024, _layernorm(x, axis=-1), mask_BxS2_bk0, L1_xattn_ln_x_w, L1_xattn_ln_x_b, L1_xattn_ln_l_w, L1_xattn_ln_l_b, L1_xattn_Wq, L1_xattn_Wkv, L1_xattn_q_scale, L1_xattn_k_scale, L1_xattn_Wo, L1_xattn_ln_o_w, L1_xattn_ln_o_b)
    x = x + _L1_ffn_ref(_layernorm(x, axis=-1), L1_ffn_W_in, L1_ffn_b_in, L1_ffn_W_out, L1_ffn_b_out)
    x = x + _L2_xattn_ref(ctx_1024, _layernorm(x, axis=-1), L2_xattn_ln_media_w, L2_xattn_ln_media_b, L2_xattn_ln_lat_w, L2_xattn_ln_lat_b, L2_xattn_Wq, L2_xattn_Wk, L2_xattn_Wv, L2_xattn_Wout)
    x = x + _L2_ffn_ref(_layernorm(x, axis=-1), L2_ffn_Wg, L2_ffn_bg, L2_ffn_W1, L2_ffn_b1, L2_ffn_W2, L2_ffn_b2)
    x = x + _L3_xattn_ref(_layernorm(x, axis=-1), ctx_1024, ctx_1024, mask_Bx1xSxS2_bf0, 0, L3_xattn_wq_w, L3_xattn_wq_b, L3_xattn_wk_w, L3_xattn_wk_b, L3_xattn_wv_w, L3_xattn_wv_b, L3_xattn_wo_w, L3_xattn_wo_b, L3_xattn_ln_g, L3_xattn_ln_b)
    x = x + _L3_ffn_ref(_layernorm(x, axis=-1), L3_ffn_w1, L3_ffn_b1, L3_ffn_w2, L3_ffn_b2)
    return x

_drawn_inputs = setup_inputs


def setup_inputs(seed=0):
    import zlib

    import numpy as np

    out = dict(_drawn_inputs(seed))
    spreads = {'L0_ffn_b1': (0.0, 0.8),
     'L0_ffn_b2': (0.0, 0.416),
     'L1_xattn_ln_x_w': (1.0, 0.2),
     'L1_xattn_ln_x_b': (0.0, 0.304),
     'L1_xattn_ln_l_w': (1.0, 0.2),
     'L1_xattn_ln_l_b': (0.0, 0.1),
     'L1_xattn_q_scale': (1.0, 0.2),
     'L1_xattn_k_scale': (1.0, 0.2),
     'L1_xattn_ln_o_w': (1.0, 0.2),
     'L1_xattn_ln_o_b': (0.0, 0.1),
     'L1_ffn_b_in': (0.0, 0.1),
     'L1_ffn_b_out': (0.0, 0.1),
     'L2_xattn_ln_media_w': (1.0, 0.2),
     'L2_xattn_ln_media_b': (0.0, 0.1),
     'L2_xattn_ln_lat_w': (1.0, 0.2),
     'L2_xattn_ln_lat_b': (0.0, 0.1),
     'L2_ffn_bg': (0.0, 0.1),
     'L2_ffn_b1': (0.0, 0.694),
     'L2_ffn_b2': (0.0, 0.1),
     'L3_xattn_wq_b': (0.0, 0.1),
     'L3_xattn_wk_b': (0.0, 0.1),
     'L3_xattn_wv_b': (0.0, 0.1),
     'L3_xattn_wo_b': (0.0, 0.267),
     'L3_xattn_ln_g': (1.0, 0.2),
     'L3_xattn_ln_b': (0.0, 0.1),
     'L3_ffn_b1': (0.0, 0.1),
     'L3_ffn_b2': (0.0, 0.1)}
    factors = {'L0_ffn_w1': 3.391, 'L0_ffn_w2': 3.087}
    for name, (base, spread) in spreads.items():
        noise = np.random.default_rng([zlib.crc32(name.encode()), seed]).standard_normal(out[name].shape)
        drawn = base * np.exp(spread * noise) if base else spread * noise
        out[name] = jnp.asarray(drawn.astype(out[name].dtype))
    for name, factor in factors.items():
        out[name] = (out[name] * factor).astype(out[name].dtype)
    return out
```

```python
import numpy as np
import concourse.bass as bass
import concourse.mybir as mybir
from contextlib import ExitStack

ACT = mybir.ActivationFunctionType
ALU = mybir.AluOpType
AX = mybir.AxisListType
F32 = mybir.dt.float32
BF16 = mybir.dt.bfloat16
U8 = mybir.dt.uint8

STAGES = 8
MAGIC = 12582912.0
BIG = float(2.0 ** 123)

COLS = {}
ROWS = {}


def _lay_cols():
    o = 0
    for name, n in (("lxw", 2), ("lxb", 2), ("llw", 2), ("llb", 2), ("ks", 1), ("qs", 1),
                    ("mw", 2), ("mb", 2), ("zw", 2), ("zb", 2), ("bin", 8), ("b1a", 64), ("b1c", 32), ("bq", 2)):
        COLS[name] = (o, n)
        o += n
    return o


def _lay_rows():
    o = 0
    for name, n in (("low", 256), ("lob", 256), ("bout", 256), ("bk", 256), ("bv", 256), ("bo", 256),
                    ("lng", 256), ("lnb", 256), ("fb1", 1024), ("fb2", 256), ("bg", 8)):
        ROWS[name] = (o, n)
        o += n
    return o


NCOL = _lay_cols()
NROW = _lay_rows()


class Mark:

    def __init__(self, queue):
        self.queue, self.used, self.value = queue, False, 0


class Arrival:

    def __init__(self, sem, value):
        self.sem, self.value = sem, value


def flat(after):
    for a in after:
        if a is None:
            continue
        if isinstance(a, (list, tuple)):
            yield from flat(a)
        else:
            yield a


class Queue:

    def __init__(self, sem):
        self.sem, self.items, self.last = sem, [], None

    def do(self, fn, *after):
        after = list(flat(after))
        for a in after:
            if isinstance(a, Mark):
                a.used = True
        m = Mark(self)
        self.items.append((fn, after, m, None))
        self.last = m
        return m

    def dma(self, sem, fn, *after):
        after = list(flat(after))
        for a in after:
            if isinstance(a, Mark):
                a.used = True
        self.items.append((fn, after, None, sem))

    def wait(self, *after):
        after = list(flat(after))
        for a in after:
            if isinstance(a, Mark):
                a.used = True
        self.items.append((None, after, None, None))

    def count(self):
        n = 0
        for _, _, m, _ in self.items:
            if m is not None and m.used:
                n += 1
                m.value = n

    def emit(self, eng):
        seen = {}
        for fn, after, m, dsem in self.items:
            for a in after:
                sem = a.queue.sem if isinstance(a, Mark) else a.sem
                if seen.get(id(sem), 0) < a.value:
                    eng.wait_ge(sem, a.value)
                    seen[id(sem)] = a.value
            if fn is None:
                continue
            ins = fn(eng)
            if dsem is not None:
                ins.then_inc(dsem, 16)
            elif m.used:
                ins.then_inc(self.sem, 1)


class Slot:
    def __init__(self, ap):
        self.ap, self.free = ap, None


class Ring:
    def __init__(self, aps):
        self.slots, self.i = [Slot(a) for a in aps], 0

    def take(self):
        s = self.slots[self.i % len(self.slots)]
        self.i += 1
        return s


def build(nc, io, out):
    ctx = ExitStack()
    with ctx:
        def sb(name, shape, dt=F32):
            return ctx.enter_context(nc.sbuf_tensor(name, shape, dt))

        def sem(name):
            return ctx.enter_context(nc.semaphore(name))

        X = sb("X", [128, 16, 256])
        ctxT = sb("ctxT", [128, 2, 2048])
        chatT = sb("chatT", [128, 2, 2048])
        HT = sb("HT", [128, 2, 2048])
        WA = sb("WA", [128, 8192])
        WB = sb("WB", [128, 8192])
        AR = sb("AR", [128, 14336])
        cols = sb("cols", [128, NCOL])
        rows = sb("rows", [128, NROW])
        ident = sb("ident", [128, 128])
        identb = sb("identb", [128, 128], BF16)
        diagb = sb("diagb", [128, 128], BF16)
        causb = sb("causb", [128, 2, 256], BF16)
        blk = sb("blk", [128, 128])
        onesf = sb("onesf", [128, 128])
        onesb = sb("onesb", [1, 128], BF16)
        nhalf = sb("nhalf", [128, 16])
        st = sb("st", [128, 4, 6])
        mv = sb("mv", [128, 16, 2])
        mv2 = sb("mv2", [128, 16, 2])
        cmv = sb("cmv", [128, 16, 2])
        rs = sb("rs", [128, 16])
        small = sb("small", [128, 704])
        banks = [ctx.enter_context(nc.psum_tensor(f"bank{i}", [128, 512], F32)) for i in range(8)]
        bank_slots = [Slot(b[:, :]) for b in banks]

        def ring_of(*ids):
            r = Ring([])
            r.slots = [bank_slots[i] for i in ids]
            return r

        PE, DV, AC, PO, SP = (Queue(sem(f"s_{n}")) for n in ("pe", "dv", "ac", "po", "sp"))

        def load(name, pairs, *after, q=None):
            s = sem(f"d_{name}")
            for o, i in pairs:
                (q or SP).dma(s, lambda e, o=o, i=i: e.dma_start(o, i), *after)
            return Arrival(s, 16 * len(pairs))

        def col(name, j=0):
            o, _ = COLS[name]
            return cols[:, o + j:o + j + 1]

        def row(name):
            o, n = ROWS[name]
            return rows[:, o:o + n]

        def region(base):
            state = [0]

            def take(words, dt=F32, **dims):
                v = base[:, state[0]:state[0] + words]
                state[0] += words
                assert state[0] <= base.shape[1], (state[0], base.shape)
                if dt is not F32:
                    v = v.bitcast(dt)
                if dims:
                    names = list(dims)
                    v = v.rearrange("p (" + " ".join(names) + ") -> p " + " ".join(names),
                                    **{k: dims[k] for k in names[1:]})
                return v
            return take

        def mm(o, l, r, start, stop, *after):
            return PE.do(lambda e: e.matmul(o, l, r, start=start, stop=stop), *after)

        def tr(o, i, idn, *after):
            return PE.do(lambda e: e.transpose(o, i, idn), *after)

        def tt(o, a, b, op, *after, q=None):
            return (q or DV).do(lambda e: e.tensor_tensor(o, a, b, op), *after)

        def ts(o, a, s1, s2, op0, op1, *after, q=None):
            if op1 is None:
                return (q or DV).do(lambda e: e.tensor_scalar(o, a, s1, None, op0), *after)
            return (q or DV).do(lambda e: e.tensor_scalar(o, a, s1, s2, op0, op1), *after)

        def recip(o, a, *after):
            return DV.do(lambda e: e.reciprocal(o, a), *after)

        def cp(o, a, *after, q=None):
            return (q or DV).do(lambda e: e.tensor_copy(o, a), *after)

        def act(o, a, f, *after, **kw):
            return AC.do(lambda e: e.activation(o, a, f, **kw), *after)

        def red(o, a, op, *after, **kw):
            return DV.do(lambda e: e.tensor_reduce(o, a, AX.X, op, **kw), *after)

        a_cst = load("cst", [(ident[:, :], io["consts"][:, 0:128]), (blk[:, :], io["consts"][:, 640:768]),
                             (small[:, 0:512], io["consts"][:, 128:640]), (cols[:, :], io["cols"])])
        ctx0 = AR[:, 0:4096].rearrange("p (t d) -> p t d", t=16)
        a_ctx = load("ctx", [(ctx0, io["ctx"].rearrange("(t p) d -> p t d", p=128))], q=AC)
        a_x = load("x", [(X[:, :, :], io["x"].rearrange("(t p) d -> p t d", p=128))])

        def wview(dram):
            return dram.rearrange("(k p) n -> p k n", p=128)

        wt = region(WA)
        wq0, wk0 = wt(1024, k=2, n=512), wt(1024, k=2, n=512)
        wv0, wo0 = wt(512, k=2, n=256), wt(512, k=2, n=256)
        a_w0 = load("w0", [(wq0, wview(io["L0wqT"])), (wk0, wview(io["L0wkT"])),
                           (wv0, wview(io["L0wvT"])), (wo0, wview(io["L0woT"]))])
        a_rows = load("rows", [(rows[:, :], io["rows"].to_broadcast([128, NROW]))])

        m_id = [cp(identb[:, :], ident[:, :], a_cst),
                ts(diagb[:, :], ident[:, :], 4000.0, None, ALU.mult, None, a_cst),
                cp(causb[:, :, :], small[:, 0:512].rearrange("p (a b) -> p a b", a=2), a_cst)]
        m_one = DV.do(lambda e: e.memset(onesf[:, :], 1.0))
        m_oneb = DV.do(lambda e: e.memset(onesb[:, :], 1.0))
        m_nh = DV.do(lambda e: e.memset(nhalf[:, :], -0.5))

        def rstd(dst, var, n, *after, eps=1e-5, op=ALU.add):
            m = ts(dst, var, eps, None, op, None, *after, q=PO)
            return PO.do(lambda e: e.tensor_tensor(dst, dst, nhalf[:, 0:n], ALU.pow), m, m_nh)

        def stats(dst, src, t, *after):
            m = DV.do(lambda e: e.bn_stats(st[:, t % 4, :], src), *after)
            return DV.do(lambda e: e.bn_aggr(dst, st[:, t % 4, :]), m)

        Xm = [a_x] * 16

        def norm_T(src, srcm, keep, dst, mvt, ring, evac, *after, second=None, hook=None):
            done = [None] * 16
            tok = [None] * 16
            for g in range(4):
                ms = [stats(mvt[:, t, :], src[:, t, :], t, srcm[t], after) for t in range(4 * g, 4 * g + 4)]
                mr = rstd(rs[:, 4 * g:4 * g + 4], mvt[:, 4 * g:4 * g + 4, 1], 4, ms[-1], tok[:4 * g])
                hs = []
                for t in range(4 * g, 4 * g + 4):
                    s = keep.take()
                    m = ts(s.ap, src[:, t, :], mvt[:, t, 0:1], rs[:, t:t + 1], ALU.subtract, ALU.mult, mr, s.free, ms[-1])
                    hs.append((s, m))
                    tok[t] = m
                if second is not None:
                    ms = [stats(mv2[:, t, :], hs[t % 4][0].ap, t, hs[t % 4][1]) for t in range(4 * g, 4 * g + 4)]
                    mr = rstd(rs[:, 4 * g:4 * g + 4], mv2[:, 4 * g:4 * g + 4, 1], 4, ms[-1])
                    for t in range(4 * g, 4 * g + 4):
                        s, m = hs[t % 4]
                        m = ts(s.ap, s.ap, mv2[:, t, 0:1], rs[:, t:t + 1], ALU.subtract, ALU.mult, mr, ms[-1])
                        hs[t % 4] = (s, m)
                        tok[t] = m
                if hook:
                    for t in range(4 * g, 4 * g + 4):
                        hook(t, *hs[t % 4])
                for c in range(2):
                    b = ring.take()
                    for j in range(4):
                        m = tr(b.ap[:, j * 128:(j + 1) * 128], hs[j][0].ap[:, c * 128:(c + 1) * 128], ident[:, :],
                               hs[j][1], b.free, a_cst)
                        if c == 1:
                            hs[j][0].free = [hs[j][0].free, m] if hook else m
                    m = evac(dst[:, c, g * 512:(g + 1) * 512], b.ap, c, m)
                    b.free = m
                    for t in range(4 * g, 4 * g + 4):
                        done[t] = [done[t], m]
            return done, tok

        def evac_copy(o, i, c, *after):
            return (act(o, i, ACT.Copy, *after) if c == 0 else cp(o, i, *after))

        def evac_affine(w, b):
            def f(o, i, c, *after):
                return act(o, i, ACT.Identity, *after, a_cst, scale=col(w, c), bias=col(b, c)) if c == 0 else \
                    ts(o, i, col(w, c), col(b, c), ALU.mult, ALU.add, *after, a_cst)
            return f

        def tiles_ring(buf, n):
            return Ring([buf[:, i, :] for i in range(n)])

        pre = ring_of(0, 1, 2, 3)
        ctx_m = [None] * 16
        for g in range(4):
            for c in range(2):
                b = pre.take()
                for j in range(4):
                    m = tr(b.ap[:, j * 128:(j + 1) * 128], ctx0[:, 4 * g + j, c * 128:(c + 1) * 128], ident[:, :],
                           a_ctx, a_cst, b.free)
                m = evac_copy(ctxT[:, c, g * 512:(g + 1) * 512], b.ap, c, m)
                b.free = m
                for t in range(4 * g, 4 * g + 4):
                    ctx_m[t] = [ctx_m[t], m]
        keep0 = tiles_ring(AR[:, 4096:6144].rearrange("p (t d) -> p t d", t=8), 8)
        chat_m, _ = norm_T(ctx0, [a_ctx] * 16, keep0, chatT, cmv, pre, evac_copy)

        def residual(t, src, *after):
            Xm[t] = tt(X[:, t, :], src, X[:, t, :], ALU.add, *after, Xm[t])
            return Xm[t]

        def attention(n, nsub, scores, pv, hooks, Pr, PTr, mx, sums, Sr, Tr):
            info = [dict() for _ in range(n)]
            w = 512 // nsub
            for i in range(n + 3):
                if i in hooks:
                    hooks[i]()
                if i < n:
                    u = info[i]
                    u["S"] = Sr.take()
                    u["ms"] = scores(i, u["S"])
                    k = (i % 4) * nsub
                    u["mx"] = red(mx[:, k:k + nsub], u["S"].ap.rearrange("p (a b) -> p a b", a=nsub), ALU.max,
                                  u["ms"], info[i - 4]["exp"] if i >= 4 else None, negate=True)
                    p = u["P"] = Pr.take()
                    for j in range(nsub):
                        m = act(p.ap[:, j * w:(j + 1) * w], u["S"].ap[:, j * w:(j + 1) * w], ACT.Exp,
                                u["mx"], p.free, bias=mx[:, k + j:k + j + 1],
                                accum_out=sums(i, j))
                    u["exp"] = m
                    u["S"].free = m
                if 0 <= i - 2 < n:
                    u = info[i - 2]
                    u["T"] = Tr.take()
                    for j in range(4):
                        m = tr(u["T"].ap[:, j * 128:(j + 1) * 128], u["P"].ap[:, j * 128:(j + 1) * 128], ident[:, :],
                               u["exp"], u["T"].free)
                    u["P"].free = m
                    q = u["PT"] = PTr.take()
                    u["pt"] = cp(q.ap, u["T"].ap, m, q.free)
                    u["T"].free = u["pt"]
                if 0 <= i - 3 < n:
                    u = info[i - 3]
                    u["PT"].free = pv(i - 3, u["PT"].ap, u["pt"], u["exp"])
            return info[n - 1]["PT"].free

        def layer0_attention():
            r = region(AR)
            r(4096)
            keep = tiles_ring(r(2048, t=8, d=256), 8)
            qT = [r(1024, c=4, n=256) for _ in range(2)]
            kT = [r(1024, c=4, n=256) for _ in range(2)]
            V = [r(512, c=2, n=256) for _ in range(2)]
            Pr, PTr = Ring([r(512) for _ in range(3)]), Ring([r(512) for _ in range(2)])
            Ob = [r(512, a=2, n=256)] * 2
            r0 = region(AR)
            OTs = [r0(512, c=2, n=256) for _ in range(2)]
            PTr.slots += [Slot(r0(512))]
            sm = small[:, 512:512 + 64].rearrange("p (s h a) -> p s h a", s=2, h=16)
            rc = small[:, 576:576 + 64].rearrange("p (s h a) -> p s h a", s=2, h=16)
            mx = small[:, 640:648]
            Sr, Tr, Or, Mr = ring_of(0, 1, 2), ring_of(3, 4), ring_of(5, 6), ring_of(7)
            ctx_done = [PE.last, chat_m]
            for s in keep.slots:
                s.free = ctx_done
            hm, _ = norm_T(X, Xm, keep, HT, mv, pre, evac_copy)
            slots = [dict(q=None, k=None, v=None, free=None) for _ in range(2)]
            proj = {}

            def project(b):
                s = b % 2
                lo, hi = b * 256, b * 256 + 256
                ready = [hm[2 * b], hm[2 * b + 1], ctx_m[2 * b], ctx_m[2 * b + 1], a_w0]
                free = proj.get(b - 2)
                ms = []
                for W, src, dst, sc in ((wq0, HT, qT, 0.0625), (wk0, ctxT, kT, None)):
                    for h in range(2):
                        bk = Mr.take()
                        for c in range(2):
                            for k in range(2):
                                m = mm(bk.ap[:, c * 256:(c + 1) * 256], W[:, k, (2 * h + c) * 128:(2 * h + c + 1) * 128],
                                       src[:, k, lo:hi], k == 0, k == 1, ready, bk.free)
                        o = dst[s][:, 2 * h:2 * h + 2, :]
                        i = bk.ap.rearrange("p (c n) -> p c n", c=2)
                        m = act(o, i, ACT.Copy, m, free, scale=sc) if sc else cp(o, i, m, free)
                        bk.free = m
                        ms.append(m)
                bk = Mr.take()
                for t in range(2):
                    for k in range(2):
                        m = mm(bk.ap[:, t * 256:(t + 1) * 256], ctxT[:, k, lo + t * 128:lo + t * 128 + 128],
                               wv0[:, k, :], k == 0, k == 1, ready, bk.free)
                m = act(V[s], bk.ap.rearrange("p (c n) -> p c n", c=2), ACT.Copy, m, free)
                bk.free = m
                ms.append(m)
                slots[s] = dict(ready=ms)

            def scores(i, S):
                b, h = divmod(i, 16)
                s, c, p = b % 2, h // 4, 32 * (h % 4)
                for a in range(2):
                    mm(S.ap[:, a * 256:(a + 1) * 256], qT[s][p:p + 32, c, a * 128:(a + 1) * 128],
                       kT[s][p:p + 32, c, :], True, False, slots[s]["ready"], S.free)
                    m = mm(S.ap[:, a * 256:(a + 1) * 256], diagb[:, :], causb[:, a, :], False, True, m_id)
                return m

            def sums(i, j):
                b, h = divmod(i, 16)
                return sm[:, b % 2, h, j:j + 1]

            O = {}
            fin = {}

            def pv(i, PT, *after):
                b, h = divmod(i, 16)
                if h == 0:
                    O[b] = Or.take()
                for a in range(2):
                    for k in range(2):
                        m = mm(O[b].ap[:, a * 256 + h * 16:a * 256 + h * 16 + 16], PT[:, (2 * a + k) * 128:(2 * a + k + 1) * 128],
                               V[b % 2][:, k, h * 16:(h + 1) * 16], k == 0, k == 1, after, O[b].free)
                if h == 15:
                    proj[b] = m
                    finish(b, m, after)
                return m

            def finish(b, m, after):
                s = b % 2
                r1 = recip(rc[:, s, :, :], sm[:, s, :, :], after)
                mo = None
                for a in range(2):
                    mo = tt(Ob[s][:, a, :].rearrange("p (h d) -> p h d", h=16),
                            O[b].ap[:, a * 256:(a + 1) * 256].rearrange("p (h d) -> p h d", h=16),
                            rc[:, s, :, a:a + 1].to_broadcast([128, 16, 16]), ALU.mult, m, r1, fin.get(b - 1))
                O[b].free = mo
                fin[b] = (mo,)

            def out_proj(b):
                s = b % 2
                mo = fin[b]
                bk = Mr.take()
                for c in range(2):
                    for a in range(2):
                        m = tr(bk.ap[:, c * 256 + a * 128:c * 256 + a * 128 + 128], Ob[s][:, a, c * 128:(c + 1) * 128],
                               ident[:, :], mo, bk.free)
                m2 = act(OTs[s], bk.ap.rearrange("p (c n) -> p c n", c=2), ACT.Copy, m, ctx_done)
                fin[b] = m
                bk.free = m2
                bk = Mr.take()
                for a in range(2):
                    for c in range(2):
                        m = mm(bk.ap[:, a * 256:(a + 1) * 256], OTs[s][:, c, a * 128:(a + 1) * 128], wo0[:, c, :],
                               c == 0, c == 1, m2, bk.free)
                for a in range(2):
                    bk.free = residual(2 * b + a, bk.ap[:, a * 256:(a + 1) * 256], m)

            project(0)
            hooks = {}
            for b in range(7):
                hooks[16 * b + 8] = lambda b=b: project(b + 1)
            for b in range(8):
                hooks.setdefault(16 * b + 16 + 5, None)
                hooks[16 * b + 21] = lambda b=b: out_proj(b)
            PTr.slots[-1].free = ctx_done
            attention(128, 2, scores, pv, hooks, Pr, PTr, mx, sums, Sr, Tr)
            out_proj(7)

        def gates(n_exp, w_sb, wready, temp, topk, hm, bias, r):
            L = r(128, t=16, e=8)
            G = r(128, t=16, e=8)
            M1 = r(128, t=16, e=8)
            M2 = r(128, t=16, e=8)
            E = r(128, t=16, e=8)
            m1 = r(16)
            d = r(16)
            rev = r(8)
            bk = ring_of(7).take()
            for t in range(16):
                for k in range(2):
                    m = mm(bk.ap[:, t * 8:(t + 1) * 8], HT[:, k, t * 128:(t + 1) * 128], w_sb[:, k, :],
                           k == 0, k == 1, hm[t], bk.free, wready)
            lg = bk.ap[:, 0:128].rearrange("p (t e) -> p t e", e=8)

            def bc(v):
                return v.rearrange("p (t o) -> p t o", o=1).to_broadcast([128, 16, 8])

            for e in range(8):
                mrev = DV.do(lambda eng, e=e: eng.memset(rev[:, e:e + 1], float(8 - e)))
            revb = rev.rearrange("p (o e) -> p o e", o=1).to_broadcast([128, 16, 8])
            if bias is not None:
                m = tt(L, lg, bias.rearrange("p (o e) -> p o e", o=1).to_broadcast([128, 16, 8]), ALU.add, m, a_rows)
                bk.free = m
                m = ts(L, L, 1.0 / temp, None, ALU.mult, None, m)
            else:
                m = cp(L, lg, m)
                bk.free = m
            m = red(m1, L, ALU.max, m)
            m = tt(E, L, bc(m1), ALU.subtract, m)
            m = ts(M1, E, 0.0, None, ALU.is_equal, None, m)
            me = act(E, E, ACT.Exp, m)
            md = red(d, E, ALU.add, me)
            m = tt(M1, M1, revb, ALU.mult, m, mrev)
            m = red(m1, M1, ALU.max, m)
            m = tt(M1, M1, bc(m1), ALU.is_equal, m)
            if topk == 2:
                m = ts(M2, M1, -3.0e38, None, ALU.mult, None, m)
                m = tt(L, L, M2, ALU.add, m)
                m = red(m1, L, ALU.max, m)
                m = tt(M2, L, bc(m1), ALU.is_equal, m)
                m = tt(M2, M2, revb, ALU.mult, m)
                m = red(m1, M2, ALU.max, m)
                m = tt(M2, M2, bc(m1), ALU.is_equal, m)
                m = tt(M1, M1, M2, ALU.add, m)
            md = recip(d, d, md)
            md = tt(E, E, bc(d), ALU.mult, md)
            m = tt(G, E, M1, ALU.mult, md, m)
            if topk == 2:
                m = red(d, G, ALU.add, m)
                m = ts(d, d, 1e-9, None, ALU.add, None, m)
                m = recip(d, d, m)
                m = tt(G, G, bc(d), ALU.mult, m)
            return G, m

        def experts(ff, w1d, w2d, b1name, b2d, G, gm, hm, gbufs, wbufs, first_free, tag, r):
            nf = ff // 128
            b2 = r(256)
            GT = r(2048)
            a_b2 = load(tag + "b2", [(b2[0:8, :], b2d)])
            Hr, Yr = ring_of(0, 1, 2, 3), ring_of(4, 5, 6)
            sems = [sem(f"d_{tag}e{i}") for i in range(2)]
            wfree = [first_free, first_free]

            def load_expert(e):
                w1, w2 = wbufs[e % 2]
                s = sems[e % 2]
                SP.dma(s, lambda q: q.dma_start(w1, w1d[e].rearrange("(k p) n -> p k n", p=128)), wfree[e % 2])
                SP.dma(s, lambda q: q.dma_start(w2, w2d[e].rearrange("(k p) n -> p k n", p=128)))
                return Arrival(s, 32 * (e // 2 + 1))

            arr = {0: load_expert(0), 1: load_expert(1)}
            bk = ring_of(7).take()
            for t in range(16):
                if t % 4 == 0:
                    bk = ring_of(7).take()
                m = tr(bk.ap[0:8, (t % 4) * 128:(t % 4 + 1) * 128], G[:, t, :], ident[:, :], gm, bk.free)
                if t % 4 == 3:
                    gtm = cp(GT[0:8, (t - 3) * 128:(t + 1) * 128], bk.ap[0:8, :], m)
                    bk.free = gtm
            for t in range(0, 16, 2):
                bk = Yr.take()
                for a in range(2):
                    m = mm(bk.ap[:, a * 256:(a + 1) * 256], GT[0:8, (t + a) * 128:(t + a + 1) * 128], b2[0:8, :],
                           True, True, gtm, a_b2, bk.free)
                for a in range(2):
                    bk.free = residual(t + a, bk.ap[:, a * 256:(a + 1) * 256], m)
            gfree = [None, None]
            units = [(e, n) for e in range(8) for n in range(4)]
            ready = {}
            for i in range(len(units) + 1):
                up, down = [], []
                if i < len(units):
                    e, n = units[i]
                    w1, w2 = wbufs[e % 2]
                    gb = gbufs[i % 2]
                    ms = []
                if i > 0:
                    pe_, pn = units[i - 1]
                    pw2 = wbufs[pe_ % 2][1]
                    pg = gbufs[(i - 1) % 2]
                for f in range(nf):
                    if i < len(units):
                        bk = Hr.take()
                        for k in range(2):
                            m = mm(bk.ap, w1[:, k, f * 128:(f + 1) * 128], HT[:, k, n * 512:(n + 1) * 512],
                                   k == 0, k == 1, arr[e], [hm[t] for t in range(4 * n, 4 * n + 4)], bk.free)
                        m = act(gb[:, f, :], bk.ap, ACT.Gelu, m, gfree[i % 2], a_cst, bias=col(b1name, e * nf + f))
                        bk.free = m
                        ms.append(m)
                    if i > 0 and f % (nf // 4) == nf // 4 - 1:
                        j = f // (nf // 4)
                        t = 4 * pn + j
                        bk = Yr.take()
                        for k in range(nf):
                            m = mm(bk.ap[:, 0:256], pg[:, k, j * 128:(j + 1) * 128], pw2[:, k, :], k == 0, k == nf - 1,
                                   ready[i - 1], bk.free)
                        if j == 3:
                            last = m
                        Xm[t] = DV.do(lambda q, t=t, b=bk.ap, g=G[:, t, pe_:pe_ + 1]: q.scalar_tensor_tensor(
                            out=X[:, t, :], in0=b[:, 0:256], scalar=g, in1=X[:, t, :], op0=ALU.mult, op1=ALU.add),
                            m, Xm[t], gm)
                        bk.free = Xm[t]
                if i < len(units):
                    ready[i] = ms
                if i > 0:
                    gfree[(i - 1) % 2] = last
                    if pn == 3 and pe_ + 2 < 8:
                        wfree[pe_ % 2] = last
                        arr[pe_ + 2] = load_expert(pe_ + 2)

        def fence():
            f = [PE.last, DV.last, AC.last, PO.last]
            for q in (DV, AC, PO):
                q.wait(f)
            return f

        def layer0_ffn():
            f = fence()
            r = region(AR)
            keep = tiles_ring(r(2048, t=8, d=256), 8)
            for s in keep.slots:
                s.free = f
            hm, _ = norm_T(X, Xm, keep, HT, mv, pre, evac_copy)
            gw = r(16, k=2, n=8)
            a_g = load("gw", [(gw, wview(io["L0gate"]))], f)
            G, gm = gates(8, gw, a_g, 1.0, 1, hm, None, r)
            gb = [r(4096, f=8, n=512) for _ in range(2)]
            wt = region(WB)
            wb = [(wt(2048, k=2, n=1024), wt(2048, k=8, n=256)) for _ in range(2)]
            experts(1024, io["L0w1"], io["L0w2"], "b1a", io["L0b2"], G, gm, hm, gb, wb, None, "l0", r)

        def layer2_ffn(wfree):
            f = fence()
            r = region(AR)
            keep = tiles_ring(r(2048, t=8, d=256), 8)
            for s in keep.slots:
                s.free = f
            hm, _ = norm_T(X, Xm, keep, HT, mv, pre, evac_copy)
            gw = r(16, k=2, n=8)
            a_g = load("gw2", [(gw, wview(io["L2Wg"]))], f)
            G, gm = gates(8, gw, a_g, 5.0, 2, hm, row("bg"), r)
            gb = [r(2048, f=4, n=512) for _ in range(2)]
            wt = region(WB)
            wt(4096)
            wb = [(wt(1024, k=2, n=512), wt(1024, k=4, n=256)) for _ in range(2)]
            experts(512, io["L2W1"], io["L2W2"], "b1c", io["L2b2"], G, gm, hm, gb, wb, wfree, "l2", r)

        def perceiver(which, W, a_w, xw, xb, zw, zb):
            f = fence()
            r = region(AR)
            keep = tiles_ring(r(2048, t=8, d=256), 8)
            for s in keep.slots:
                s.free = f
            wbh = region(WB)
            wbh(4096)
            kT = [r(2048, c=4, n=512), wbh(2048, c=4, n=512)]
            V = [r(2048, t=4, n=512), wbh(2048, t=4, n=512)]
            qT = [r(1024, c=4, n=256) for _ in range(2)]
            xT = [r(512, c=2, n=256) for _ in range(2)]
            Pr, PTr = Ring([r(512) for _ in range(3)]), Ring([r(512) for _ in range(2)])
            r2 = region(AR)
            Obs = [r2(512) for _ in range(1)]
            OTs = [r2(512, c=4, n=128) for _ in range(1)]
            sq, kn = Ring([r(512)]), Ring([r2(512), r2(512)])
            yb = r(256)
            sm = small[:, 512:512 + 32].rearrange("p (s h) -> p s h", s=4)
            rc = small[:, 544:544 + 32].rearrange("p (s h) -> p s h", s=4)
            mx = small[:, 640:648]
            ss = Ring([small[:, 656:664], small[:, 664:672]])
            Sr, Tr, Or, Mr = ring_of(0, 1, 2), ring_of(3, 4), ring_of(5, 6), ring_of(7)
            hm, _ = norm_T(X, Xm, keep, HT, mv, pre, evac_affine(zw, zb), second=True)
            f2 = fence()
            for s in kn.slots:
                s.free = f2
            obfree, otfree = f2, f2
            proj_free = {}
            ready = {}

            def project(b):
                s = b % 2
                lo = b * 256
                free = [proj_free.get(b - 2), f2]
                done = []
                pieces = []
                xs = []

                def affine():
                    for c in range(2):
                        xs.append(ts(xT[s][:, c, :], chatT[:, c, lo:lo + 256], col(xw, c), col(xb, c), ALU.mult, ALU.add,
                                     chat_m[2 * b], chat_m[2 * b + 1], free, a_cst, q=DV))
                pieces.append(affine)

                def src(t):
                    return (xT[s], t * 128, xs) if t < 2 else (HT, lo + (t - 2) * 128, hm[2 * b + t - 2])

                def value(t):
                    sr, o, dep = src(t)
                    bk = Mr.take()
                    for k in range(2):
                        m = mm(bk.ap, sr[:, k, o:o + 128], wv[:, k, :], k == 0, k == 1, dep, a_w, bk.free)
                    m = act(V[s][:, t, :], bk.ap, ACT.Copy, m, free)
                    bk.free = m
                    done.append(m)

                def normed(t, w, dst, at, scale_col):
                    sr, o, dep = src(t)
                    bk = Mr.take()
                    for k in range(2):
                        m = mm(bk.ap, sr[:, k, o:o + 128], w[:, k, :], k == 0, k == 1, dep, a_w, bk.free)
                    q = sq.take()
                    m1 = act(q.ap, bk.ap, ACT.Square, m, q.free)
                    v = ss.take()
                    m2 = red(v.ap, q.ap.rearrange("p (h d) -> p h d", h=8), ALU.add, m1, v.free)
                    q.free = m2
                    m3 = rstd(v.ap, v.ap, 8, m2, eps=1e-24, op=ALU.max)
                    z = kn.take()
                    m4 = tt(z.ap.rearrange("p (h d) -> p h d", h=8), bk.ap.rearrange("p (h d) -> p h d", h=8),
                            v.ap.rearrange("p (h o) -> p h o", o=1).to_broadcast([128, 8, 64]), ALU.mult, m3, z.free)
                    v.free = m4
                    bk.free = m4

                    def second():
                        T = Tr.take()
                        for c in range(4):
                            m5 = tr(T.ap[:, c * 128:(c + 1) * 128], z.ap[:, c * 128:(c + 1) * 128], ident[:, :], m4, T.free)
                        z.free = m5
                        m6 = act(dst[:, :, at:at + 128], T.ap.rearrange("p (c n) -> p c n", c=4), ACT.Copy, m5, free, m_qs,
                                 scale=scale_col)
                        T.free = m6
                        done.append(m6)
                    return second

                def plain(w, sr, o, n, dst, at, sc, dep):
                    per = 512 // n
                    for c0 in range(0, 4, per):
                        bk = Mr.take()
                        for c in range(per):
                            for k in range(2):
                                m = mm(bk.ap[:, c * n:(c + 1) * n], w[:, k, (c0 + c) * 128:(c0 + c + 1) * 128],
                                       sr[:, k, o:o + n], k == 0, k == 1, dep, a_w, bk.free)
                        m = act(dst[:, c0:c0 + per, at:at + n], bk.ap.rearrange("p (c n) -> p c n", c=per), ACT.Copy, m, free,
                                scale=sc)
                        bk.free = m
                        done.append(m)

                if which == 1:
                    later = []
                    for t in range(4):
                        pieces.append(lambda t=t: later.append(normed(t, wk, kT[s], t * 128, col("ks"))))
                        pieces.append(lambda t=t: (later.pop()(), value(t)))
                        if t >= 2:
                            pieces.append(lambda t=t: later.append(normed(t, wq, qT[s], (t - 2) * 128, qs8)))
                            pieces.append(lambda t=t: later.pop()())
                else:
                    pieces.append(lambda: plain(wk, xT[s], 0, 256, kT[s], 0, 1.0, xs))
                    for t in range(4):
                        pieces.append(lambda t=t: value(t))
                    hd = [hm[2 * b], hm[2 * b + 1]]
                    pieces.append(lambda: plain(wk, HT, lo, 256, kT[s], 256, 1.0, hd))
                    pieces.append(lambda: plain(wq, HT, lo, 256, qT[s], 0, 0.125, hd))
                ready[b] = done
                return pieces

            wq, wk, wv, wo = W
            qs8 = small[:, 650:651]
            m_qs = ts(qs8, col("qs"), 8.0, None, ALU.mult, None, a_cst, f)
            neg = None
            if which == 1:
                nb = r(1024, dt=BF16)[0:1, :]
                mk = r(512, dt=U8)[0:1, :]
                a_mk = load("mk", [(mk, io["mask1"])], f)
                neg = ts(nb, mk, 1.0, BIG, ALU.subtract, ALU.mult, a_mk)

            def scores(i, S):
                b, rest = divmod(i, 16)
                a, h = divmod(rest, 8)
                s, c, p = b % 2, h // 2, 64 * (h % 2)
                m = mm(S.ap, qT[s][p:p + 64, c, a * 128:(a + 1) * 128], kT[s][p:p + 64, c, :], True, which != 1,
                       ready[b], S.free)
                if which == 1:
                    m = mm(S.ap[:, 0:256], onesb[:, :], nb[:, b * 256:(b + 1) * 256], False, True, neg, m_oneb)
                return m

            def sums(i, j):
                g, h = divmod(i, 8)
                return sm[:, g % 4, h:h + 1]

            O, fin = {}, {}

            def pv(i, PT, *after):
                g, h = divmod(i, 8)
                b = g // 2
                if h == 0:
                    O[g] = Or.take()
                for k in range(4):
                    m = mm(O[g].ap[:, h * 64:(h + 1) * 64], PT[:, k * 128:(k + 1) * 128],
                           V[b % 2][:, k, h * 64:(h + 1) * 64], k == 0, k == 3, after, O[g].free)
                if h == 7:
                    if g % 2 == 1:
                        proj_free[b] = m
                    s = g % 4
                    r1 = recip(rc[:, s, :], sm[:, s, :], after)
                    fin[g] = tt(Obs[0].rearrange("p (h d) -> p h d", h=8),
                                O[g].ap.rearrange("p (h d) -> p h d", h=8),
                                rc[:, s, :].rearrange("p (h o) -> p h o", o=1).to_broadcast([128, 8, 64]),
                                ALU.mult, m, r1, obf[0])
                    O[g].free = fin[g]
                return m

            obf, otf, ybf = [obfree], [otfree], [f2]

            def out_proj(g):
                T = Mr.take()
                for c in range(4):
                    m = tr(T.ap[:, c * 128:(c + 1) * 128], Obs[0][:, c * 128:(c + 1) * 128], ident[:, :], fin[g], T.free)
                obf[0] = m
                m = act(OTs[0], T.ap.rearrange("p (c n) -> p c n", c=4), ACT.Copy, m, otf[0])
                T.free = m
                T = Mr.take()
                for c in range(4):
                    m = mm(T.ap[:, 0:256], OTs[0][:, c, :], wo[:, c, :], c == 0, c == 3, m, T.free)
                otf[0] = m
                if which == 2:
                    T.free = residual(g, T.ap[:, 0:256], m)
                    return
                ms = stats(mv2[:, g, :], T.ap[:, 0:256], g, m)
                mr = rstd(rs[:, g:g + 1], mv2[:, g, 1:2], 1, ms)
                m = ts(yb, T.ap[:, 0:256], mv2[:, g, 0:1], rs[:, g:g + 1], ALU.subtract, ALU.mult, mr, ms, ybf[0])
                T.free = m
                m = tt(yb, yb, row("low"), ALU.mult, m, a_rows, q=PO)
                m = tt(yb, yb, row("lob"), ALU.add, m, q=PO)
                ybf[0] = residual(g, yb, m)

            for p in project(0):
                p()
            hooks = {}

            def add(i, fn):
                old = hooks.get(i)
                hooks[i] = (lambda: (old(), fn())) if old else fn

            for b in range(7):
                def start(b=b):
                    pc = project(b + 1)
                    state[b] = pc
                    pc[0]()
                state = {}
                n = 13 if which == 1 else 8
                add(16 * b + 3, lambda b=b: state.__setitem__(b, project(b + 1)) or state[b][0]())
                for j in range(1, n):
                    add(16 * b + 3 + j, lambda b=b, j=j: state[b][j]())
            for g in range(15):
                add(8 * g + 8 + 4, lambda g=g: out_proj(g))
            attention(128, 1, scores, pv, hooks, Pr, PTr, mx, sums, Sr, Tr)
            out_proj(15)

        def all_max(dst, src, n, ring, *after):
            m = red(dst, src, ALU.max, *after)
            b = ring.take()
            m = tr(b.ap[0:1, 0:128], dst, ident[:, :], m, b.free)
            m = red(dst[0:1, :], b.ap[0:1, 0:128], ALU.max, m)
            m = mm(b.ap[:, 256:257], onesf[0:1, :], dst[0:1, :], True, True, m, m_one)
            m = cp(dst, b.ap[:, 256:257], m)
            b.free = m
            return m

        def layer1_ffn(WI, WO, a_w):
            f = fence()
            r = region(AR)
            am = small[:, 0:64]
            sc = small[:, 64:72]
            keep = tiles_ring(r(2048, t=8, d=256), 8)
            for s in keep.slots:
                s.free = f
            hid3 = AR[:, 0:12288].rearrange("p (g f n) -> p g f n", g=3, f=8)
            W1 = AR[:, 12288:14336].rearrange("p (k n) -> p k n", k=2)
            hid1 = WB[:, 4096:8192].rearrange("p (f n) -> p f n", f=8)

            def hid(n):
                return hid3[:, n, :, :] if n < 3 else hid1
            aw = small[:, 80:96]
            sw = small[:, 96:112]
            iw = small[:, 112:128]
            wm = []
            for j, Wt in ((0, WI), (8, WO)):
                m = red(aw[:, j:j + 8], Wt, ALU.max, a_w, f, apply_absolute_value=True)
                wm.append(m)
            m = ts(aw, aw, 1e-8, None, ALU.max, None, wm)
            m = recip(sw, aw, m)
            m = ts(sw, sw, 127.0, None, ALU.mult, None, m)
            mi = ts(iw, aw, 1.0 / 127.0, None, ALU.mult, None, m)
            w_ready = []
            for j, Wt in ((0, WI), (8, WO)):
                for k in range(8):
                    m1 = ts(Wt[:, k, :], Wt[:, k, :], sw[:, j + k:j + k + 1], MAGIC, ALU.mult, ALU.add, m, mi)
                    m1 = ts(Wt[:, k, :], Wt[:, k, :], MAGIC, iw[:, j + k:j + k + 1], ALU.subtract, ALU.mult, m1)
                    w_ready.append(m1)
            t1 = []
            rr = ring_of(4, 5)
            for k in range(2):
                for q in range(2):
                    b = rr.take()
                    for j in range(4):
                        m = tr(b.ap[:, j * 128:(j + 1) * 128], WI[:, 4 * q + j, k * 128:(k + 1) * 128], ident[:, :],
                               w_ready, b.free)
                    m = act(W1[:, k, q * 512:(q + 1) * 512], b.ap, ACT.Copy, m, f)
                    b.free = m
                    t1.append(m)

            def hook(t, s, m):
                s.free = red(am[:, t:t + 1], s.ap, ALU.max, m, f, apply_absolute_value=True)

            hm, _ = norm_T(X, Xm, keep, HT, mv, pre, evac_copy, hook=hook)
            m = all_max(sc[:, 0:1], am[:, 0:16], 16, ring_of(7), DV.last)
            m = ts(sc[:, 0:1], sc[:, 0:1], 1e-8, None, ALU.max, None, m)
            m = recip(sc[:, 1:2], sc[:, 0:1], m)
            m = ts(sc[:, 1:2], sc[:, 1:2], 32767.0, None, ALU.mult, None, m)
            m = ts(sc[:, 2:3], sc[:, 0:1], 1.0 / 32767.0, None, ALU.mult, None, m)
            hq = []
            for n in range(4):
                v = HT[:, :, n * 512:(n + 1) * 512]
                m1 = ts(v, v, sc[:, 1:2], MAGIC, ALU.mult, ALU.add, m, hm[4 * n:4 * n + 4])
                hq.append(ts(v, v, MAGIC, sc[:, 2:3], ALU.subtract, ALU.mult, m1))
            f3 = [hm, w_ready, t1]
            Hr, Yr = ring_of(0, 1, 2, 3), ring_of(4, 5, 6)
            gm = []
            for n in range(4):
                for k in range(8):
                    b = Hr.take()
                    for c in range(2):
                        m = mm(b.ap, W1[:, c, k * 128:(k + 1) * 128], HT[:, c, n * 512:(n + 1) * 512], c == 0, c == 1,
                               hq[n], t1, b.free)
                    m = act(hid(n)[:, k, :], b.ap, ACT.Gelu, m, f3, a_cst, bias=col("bin", k))
                    b.free = m
                    u = small[:, 160 + 8 * n + k:161 + 8 * n + k]
                    gm.append(red(u, hid(n)[:, k, :], ALU.max, m, apply_absolute_value=True))
            m = all_max(sc[:, 3:4], small[:, 160:192], 32, ring_of(7), gm)
            m = ts(sc[:, 3:4], sc[:, 3:4], 1e-8, None, ALU.max, None, m)
            m = recip(sc[:, 4:5], sc[:, 3:4], m)
            m = ts(sc[:, 4:5], sc[:, 4:5], 32767.0, None, ALU.mult, None, m)
            ms = ts(sc[:, 5:6], sc[:, 3:4], 1.0 / 32767.0, None, ALU.mult, None, m)
            for n in range(4):
                qs = []
                for k in range(0, 8, 2):
                    v = hid(n)[:, k:k + 2, :]
                    m1 = ts(v, v, sc[:, 4:5], MAGIC, ALU.mult, ALU.add, ms)
                    qs.append(ts(v, v, MAGIC, sc[:, 5:6], ALU.subtract, ALU.mult, m1))
                for j in range(4):
                    t = 4 * n + j
                    b = Yr.take()
                    for k in range(8):
                        m = mm(b.ap[:, 0:256], hid(n)[:, k, j * 128:(j + 1) * 128], WO[:, k, :], k == 0, k == 7,
                               qs, b.free)
                    Xm[t] = tt(X[:, t, :], X[:, t, :], row("bout"), ALU.add, Xm[t], a_rows)
                    b.free = residual(t, b.ap[:, 0:256], m)

        def layer3_attention(wq, wk, wv, wo, a_w):
            f = fence()
            r = region(AR)
            Hn = r(4096, t=16, d=256)
            keep = tiles_ring(Hn, 16)
            for s in keep.slots:
                s.free = f
            hm, tok = norm_T(X, Xm, keep, HT, mv, pre, evac_copy)
            mk = r(1024, dt=U8, t=16, n=256)
            a_m = load("mask0", [(mk, io["mask0"].rearrange("(t p) n -> p t n", p=128))], f)
            pen = small[:, 0:16]
            m = red(pen, mk, ALU.max, a_m, f)
            m_pen = ts(pen, pen, -3.0e38, 3.0e38, ALU.mult, ALU.mult, m)
            Ks, Vs, Qs, As, Cs = (Ring([r(512, a=2, n=256) for _ in range(2)]) for _ in range(5))
            Qs.slots.append(Slot(r(512, a=2, n=256)))
            ys = Ring([r(256) for _ in range(4)])
            R = ring_of(0, 1, 2, 3, 4, 5, 6, 7)

            def first(b):
                lo = b * 256
                kv = []
                for w, rg, bias in ((wk, Ks, "bk"), (wv, Vs, "bv")):
                    bk = R.take()
                    for a in range(2):
                        for k in range(2):
                            m = mm(bk.ap[:, a * 256:(a + 1) * 256], ctxT[:, k, lo + a * 128:lo + (a + 1) * 128], w[:, k, :],
                                   k == 0, k == 1, a_w, bk.free, ctx_m[2 * b + a])
                    s = rg.take()
                    m = tt(s.ap, bk.ap.rearrange("p (a n) -> p a n", a=2),
                           row(bias).rearrange("p (o n) -> p o n", o=1).to_broadcast([128, 2, 256]), ALU.add, m, s.free, a_rows, f)
                    bk.free = m
                    kv.append((s, m))
                bk = R.take()
                for c in range(2):
                    for k in range(2):
                        m = mm(bk.ap[:, c * 256:(c + 1) * 256], wq[:, k, c * 128:(c + 1) * 128], HT[:, k, lo:lo + 256],
                               k == 0, k == 1, a_w, bk.free, hm[2 * b], hm[2 * b + 1])
                q = Qs.take()
                for c in range(2):
                    m2 = act(q.ap[:, c, :], bk.ap[:, c * 256:(c + 1) * 256], ACT.Identity, m, q.free, a_cst, f, bias=col("bq", c))
                bk.free = m2
                return kv, (q, m2)

            def second(b, kv, q):
                (K, mk_), (V, mv_) = kv
                bk = R.take()
                for c in range(2):
                    for a in range(2):
                        m = mm(bk.ap[:, c * 128:(c + 1) * 128], K.ap[:, a, c * 128:(c + 1) * 128],
                               V.ap[:, a, c * 128:(c + 1) * 128], a == 0, a == 1, mk_, mv_, bk.free)
                K.free = V.free = m
                A = As.take()
                m = tt(A.ap[:, 0, :].rearrange("p (c n) -> p c n", c=2), bk.ap[:, 0:256].rearrange("p (c n) -> p c n", c=2),
                       blk[:, :].rearrange("p (o n) -> p o n", o=1).to_broadcast([128, 2, 128]), ALU.mult, m, A.free, a_cst, f)
                bk.free = m
                return A, m

            def third(b, q, A, am_):
                bk = R.take()
                for c in range(2):
                    m = mm(bk.ap[:, c * 256:(c + 1) * 256], A.ap[:, 0, c * 128:(c + 1) * 128], q[0].ap[:, c, :], True, True,
                           am_, q[1], bk.free)
                q[0].free = A.free = m
                C = Cs.take()
                m = act(C.ap, bk.ap.rearrange("p (c n) -> p c n", c=2), ACT.Copy, m, C.free, f)
                bk.free = m
                return C, m

            def fourth(b, C, cm):
                bk = R.take()
                for a in range(2):
                    for c in range(2):
                        m = mm(bk.ap[:, a * 256:(a + 1) * 256], C.ap[:, c, a * 128:(a + 1) * 128], wo[:, c, :],
                               c == 0, c == 1, cm, bk.free)
                C.free = m
                mms = []
                yy = []
                for a in range(2):
                    t = 2 * b + a
                    y = ys.take()
                    m1 = tt(y.ap, bk.ap[:, a * 256:(a + 1) * 256], row("bo"), ALU.add, m, y.free, a_rows, f)
                    bk.free = m1
                    m1 = DV.do(lambda e, y=y, t=t: e.scalar_tensor_tensor(out=y.ap, in0=Hn[:, t, :], scalar=pen[:, t:t + 1],
                               in1=y.ap, op0=ALU.add, op1=ALU.add), m1, m_pen, tok[t])
                    mms.append(stats(mv2[:, t, :], y.ap, t, m1))
                    yy.append(y)
                mr = rstd(rs[:, 2 * b:2 * b + 2], mv2[:, 2 * b:2 * b + 2, 1], 2, mms, tok[2 * b], tok[2 * b + 1])
                for a in range(2):
                    t = 2 * b + a
                    y = yy[a]
                    m1 = ts(y.ap, y.ap, mv2[:, t, 0:1], rs[:, t:t + 1], ALU.subtract, ALU.mult, mr, mms)
                    m1 = tt(y.ap, y.ap, row("lng"), ALU.mult, m1, q=PO)
                    m1 = tt(y.ap, y.ap, row("lnb"), ALU.add, m1, q=PO)
                    y.free = residual(t, y.ap, m1)

            s1, s2, s3 = {}, {}, {}
            for i in range(8 + 3):
                if i < 8:
                    s1[i] = first(i)
                if 0 <= i - 1 < 8:
                    s2[i - 1] = second(i - 1, *s1[i - 1])
                if 0 <= i - 2 < 8:
                    s3[i - 2] = third(i - 2, s1[i - 2][1], *s2[i - 2])
                if 0 <= i - 3 < 8:
                    fourth(i - 3, *s3[i - 3])

        def layer3_ffn(w1, w2, a_w):
            f = fence()
            r = region(AR)
            wq1 = r(1024, dt=BF16, k=2, n=1024)
            wq2 = r(1024, dt=BF16, k=8, n=256)
            sc = small[:, 0:8]
            R = ring_of(6, 7)
            iws = []
            wr = []
            for j, (w, wq, n) in enumerate(((w1, wq1, 262144.0), (w2, wq2, 262144.0))):
                v = sc[:, 4 * j:4 * j + 1]
                s = sc[:, 4 * j + 1:4 * j + 2]
                i = sc[:, 4 * j + 2:4 * j + 3]
                m = red(v, w.rearrange("p k n -> p (k n)"), ALU.add, a_w, f, apply_absolute_value=True)
                b = R.take()
                m = mm(b.ap[:, 0:1], onesf[:, :], v, True, True, m, b.free, m_one)
                m = ts(i, b.ap[:, 0:1], 1.0 / n, 1e-5, ALU.mult, ALU.max, m)
                b.free = m
                m = recip(s, i, m)
                iws.append(i)
                m = ts(w, w, s, MAGIC, ALU.mult, ALU.add, m)
                m = ts(w, w, MAGIC, 1.0, ALU.subtract, ALU.min, m)
                wr.append(ts(wq, w, -1.0, None, ALU.max, None, m))
            hs = Ring([r(1024) for _ in range(3)])
            hb = Ring([r(512, dt=BF16) for _ in range(2)])
            hT = Ring([r(512, dt=BF16, k=8, n=128) for _ in range(2)])
            xs = Ring([r(256) for _ in range(3)])
            xb = Ring([r(128, dt=BF16) for _ in range(2)])
            xT = Ring([r(128, dt=BF16, k=2, n=128) for _ in range(2)])
            ys = Ring([r(256) for _ in range(3)])
            scr = Ring([r(1024), r(1024)])
            stt = small[:, 128:128 + 16 * 16].rearrange("p (t s) -> p t s", t=16)
            Hr, Tr, Yr = ring_of(0, 1, 2, 3), ring_of(4, 5), ring_of(6, 7)

            def quant(t, src, srcm, n, base, dst, dstm, wi):
                c = [stt[:, t, base + k:base + k + 1] for k in range(6)]
                q = scr.take()
                m1 = act(q.ap[:, 0:n], src, ACT.Square, srcm, q.free, f, accum_out=c[0])
                q.free = m1
                m2 = red(c[1], src, ALU.max, srcm, f, apply_absolute_value=True)
                m3 = ts(c[0], c[0], 1.0 / n, 1e-5, ALU.mult, ALU.add, m1, q=PO)
                m3 = PO.do(lambda e: e.tensor_tensor(c[0], c[0], nhalf[:, 0:1], ALU.pow), m3, m_nh)
                m4 = ts(c[1], c[1], c[0], 1e-5, ALU.mult, ALU.max, m3, m2)
                m5 = recip(c[2], c[1], m4)
                m6 = ts(c[2], c[2], 127.0, None, ALU.mult, None, m5)
                m7 = ts(c[3], c[1], iws[wi], 1.0 / 127.0, ALU.mult, ALU.mult, m6)
                m8 = ts(src, src, c[0], c[2], ALU.mult, ALU.mult, m7, m1)
                m8 = ts(src, src, MAGIC, None, ALU.add, None, m8)
                m9 = ts(dst, src, MAGIC, None, ALU.subtract, None, m8, dstm)
                return m9, c[3]

            S = {}
            rs_m = []
            for g in range(4):
                ms = [stats(mv[:, t, :], X[:, t, :], t, Xm[t]) for t in range(4 * g, 4 * g + 4)]
                rs_m.append(rstd(rs[:, 4 * g:4 * g + 4], mv[:, 4 * g:4 * g + 4, 1], 4, ms, f))

            def s1(t):
                x = xs.take()
                m = ts(x.ap, X[:, t, :], mv[:, t, 0:1], rs[:, t:t + 1], ALU.subtract, ALU.mult, rs_m[t // 4], x.free, Xm[t])
                d = xb.take()
                m, sx = quant(t, x.ap, m, 256, 0, d.ap, d.free, 0)
                x.free = m
                T = Tr.take()
                tv = T.ap.bitcast(BF16)
                for k in range(2):
                    m = tr(tv[:, k * 128:(k + 1) * 128], d.ap[:, k * 128:(k + 1) * 128], identb[:, :], m, T.free, m_id)
                d.free = m
                xt = xT.take()
                m = cp(xt.ap, tv[:, 0:256].rearrange("p (k n) -> p k n", k=2), m, xt.free, f)
                T.free = m
                h = hs.take()
                ms = []
                for q in range(2):
                    b = Hr.take()
                    for k in range(2):
                        mp = mm(b.ap, xt.ap[:, k, :], wq1[:, k, q * 512:(q + 1) * 512], k == 0, k == 1, m, wr, b.free)
                    fb = row("fb1")[:, q * 512:(q + 1) * 512]
                    m1 = DV.do(lambda e, b=b, q=q, fb=fb: e.scalar_tensor_tensor(
                        out=h.ap[:, q * 512:(q + 1) * 512], in0=b.ap, scalar=sx, in1=fb, op0=ALU.mult, op1=ALU.add),
                        mp, h.free, a_rows, f)
                    b.free = m1
                    ms.append(m1)
                xt.free = mp
                m = act(h.ap, h.ap, ACT.Gelu, ms)
                S[t] = (h, m)

            def s2(t):
                h, m = S[t]
                d = hb.take()
                m, sx = quant(t, h.ap, m, 1024, 8, d.ap, d.free, 1)
                h.free = m
                T = Tr.take()
                tv = T.ap.bitcast(BF16)
                for k in range(8):
                    m = tr(tv[:, k * 128:(k + 1) * 128], d.ap[:, k * 128:(k + 1) * 128], identb[:, :], m, T.free)
                d.free = m
                xt = hT.take()
                m = cp(xt.ap, tv.rearrange("p (k n) -> p k n", k=8), m, xt.free, f)
                T.free = m
                b = Yr.take()
                for k in range(8):
                    mp = mm(b.ap[:, 0:256], xt.ap[:, k, :], wq2[:, k, :], k == 0, k == 7, m, wr, b.free)
                xt.free = mp
                y = ys.take()
                m = DV.do(lambda e: e.scalar_tensor_tensor(out=y.ap, in0=b.ap[:, 0:256], scalar=sx, in1=row("fb2"),
                                                           op0=ALU.mult, op1=ALU.add), mp, y.free, a_rows, f)
                b.free = m
                m = tt(X[:, t, :], X[:, t, :], y.ap, ALU.add, m, Xm[t])
                y.free = m
                Xm[t] = m

            for t in range(17):
                if t < 16:
                    s1(t)
                if t > 0:
                    s2(t - 1)

        def weights(name, views, *after):
            return load(name, views, *after)

        if STAGES >= 1:
            layer0_attention()
            e0 = PE.last
            wt = region(WA)
            W1 = (wt(1024, k=2, n=512), wt(1024, k=2, n=512), wt(1024, k=2, n=512), wt(1024, k=4, n=256))
            WI, WO = wt(2048, f=8, n=256), wt(2048, f=8, n=256)
        if STAGES >= 3:
            a_w1 = load("w1", [(W1[0], wview(io["L1Wq"])), (W1[1], wview(io["L1Wkv"])[:, :, 0:512]),
                               (W1[2], wview(io["L1Wkv"])[:, :, 512:1024]), (W1[3], wview(io["L1Wo"]))], e0)
        if STAGES >= 4:
            a_wf1 = load("wf1", [(WI, wview(io["L1WinT"])), (WO, wview(io["L1Wout"]))], e0)
        if STAGES >= 2:
            layer0_ffn()
            e1 = PE.last
        if STAGES >= 5:
            wt = region(WB)
            W2 = (wt(1024, k=2, n=512), wt(1024, k=2, n=512), wt(1024, k=2, n=512), wt(1024, k=4, n=256))
            a_w2 = load("w2", [(W2[0], wview(io["L2Wq"])), (W2[1], wview(io["L2Wk"])),
                               (W2[2], wview(io["L2Wv"])), (W2[3], wview(io["L2Wout"]))], e1)
        if STAGES >= 3:
            perceiver(1, W1, a_w1, "lxw", "lxb", "llw", "llb")
        if STAGES >= 4:
            layer1_ffn(WI, WO, a_wf1)
            e3 = PE.last
        if STAGES >= 7:
            wt = region(WA)
            W3 = [wt(512, k=2, n=256) for _ in range(4)]
            F1, F2 = wt(2048, k=2, n=1024), wt(2048, k=8, n=256)
            a_w3 = load("w3", [(W3[0], wview(io["L3wqT"])), (W3[1], wview(io["L3wkT"])),
                               (W3[2], wview(io["L3wvT"])), (W3[3], wview(io["L3woT"]))], e3)
            a_f3 = load("f3", [(F1, wview(io["L3w1T"])), (F2, wview(io["L3w2T"]))], e3)
        if STAGES >= 5:
            perceiver(2, W2, a_w2, "mw", "mb", "zw", "zb")
            e4 = PE.last
        if STAGES >= 6:
            layer2_ffn(e4)
        if STAGES >= 7:
            layer3_attention(*W3, a_w3)
        if STAGES >= 8:
            layer3_ffn(F1, F2, a_f3)
        s_out = sem("s_out")
        ov = out.rearrange("(t p) d -> p t d", p=128)
        for g in range(4):
            SP.dma(s_out, lambda e, g=g: e.dma_start(ov[:, 4 * g:4 * g + 4, :], X[:, 4 * g:4 * g + 4, :]),
                   Xm[4 * g:4 * g + 4])
        SP.wait(Arrival(s_out, 64))

        for q in (PE, DV, AC, PO, SP):
            q.count()
        block = ctx.enter_context(nc.Block())

        @block.tensor
        def _(eng):
            PE.emit(eng)

        @block.vector
        def _(eng):
            DV.emit(eng)

        @block.scalar
        def _(eng):
            AC.emit(eng)

        @block.gpsimd
        def _(eng):
            PO.emit(eng)

        @block.sync
        def _(eng):
            SP.emit(eng)


def _constants():
    c = np.zeros((128, 768), np.float32)
    c[:, 0:128] = np.eye(128, dtype=np.float32)
    q = np.arange(128)[:, None]
    k = np.arange(256)[None, :]
    c[:, 128:384] = np.where(k > q, -25.0, 0.0)
    c[:, 384:640] = np.where(k > q + 128, -25.0, 0.0)
    i = np.arange(128)
    c[:, 640:768] = np.where(i[:, None] // 16 == i[None, :] // 16, 0.25, 0.0)
    return c


def kernel(**inputs):
    import concourse.bacc as bacc
    from concourse.bass_utils import run_bass_kernel_spmd as run
    a = {k: np.asarray(v) for k, v in inputs.items()}

    def pc(v):
        return v.reshape(-1, 128).T

    def pad_heads(w):
        z = np.zeros((256, 16, 32), np.float32)
        z[:, :, 0:16] = w.T.reshape(256, 16, 16)
        return z.reshape(256, 512)

    cols = np.concatenate([
        pc(a["L1_xattn_ln_x_w"]), pc(a["L1_xattn_ln_x_b"]), pc(a["L1_xattn_ln_l_w"]), pc(a["L1_xattn_ln_l_b"]),
        pc(np.tile(a["L1_xattn_k_scale"], 2)), pc(np.tile(a["L1_xattn_q_scale"], 2)),
        pc(a["L2_xattn_ln_media_w"]), pc(a["L2_xattn_ln_media_b"]), pc(a["L2_xattn_ln_lat_w"]), pc(a["L2_xattn_ln_lat_b"]),
        pc(a["L1_ffn_b_in"]), pc(a["L0_ffn_b1"].reshape(-1)), pc(a["L2_ffn_b1"].reshape(-1)), pc(a["L3_xattn_wq_b"])], axis=1)
    rows = np.concatenate([
        a["L1_xattn_ln_o_w"], a["L1_xattn_ln_o_b"], a["L1_ffn_b_out"], a["L3_xattn_wk_b"], a["L3_xattn_wv_b"],
        a["L3_xattn_wo_b"], a["L3_xattn_ln_g"], a["L3_xattn_ln_b"], a["L3_ffn_b1"], a["L3_ffn_b2"], a["L2_ffn_bg"]])[None, :]
    data = {
        "x": a["x"].reshape(2048, 256), "ctx": a["ctx_1024"].reshape(2048, 256),
        "mask1": a["mask_BxS2_bk0"].reshape(1, 2048),
        "mask0": a["mask_Bx1xSxS2_bf0"].reshape(2048, 256),
        "cols": cols, "rows": rows, "consts": _constants(),
        "L0wqT": pad_heads(a["L0_xattn_Wq"]), "L0wkT": pad_heads(a["L0_xattn_Wk"]),
        "L0wvT": a["L0_xattn_Wv"].T, "L0woT": a["L0_xattn_Wo"].T,
        "L0gate": a["L0_ffn_gate_w"], "L0w1": a["L0_ffn_w1"], "L0w2": a["L0_ffn_w2"], "L0b2": a["L0_ffn_b2"],
        "L1Wq": a["L1_xattn_Wq"], "L1Wkv": a["L1_xattn_Wkv"], "L1Wo": a["L1_xattn_Wo"],
        "L1WinT": a["L1_ffn_W_in"].T, "L1Wout": a["L1_ffn_W_out"],
        "L2Wq": a["L2_xattn_Wq"], "L2Wk": a["L2_xattn_Wk"], "L2Wv": a["L2_xattn_Wv"], "L2Wout": a["L2_xattn_Wout"],
        "L2Wg": a["L2_ffn_Wg"], "L2W1": a["L2_ffn_W1"], "L2W2": a["L2_ffn_W2"], "L2b2": a["L2_ffn_b2"],
        "L3wqT": a["L3_xattn_wq_w"].T, "L3wkT": a["L3_xattn_wk_w"].T, "L3wvT": a["L3_xattn_wv_w"].T,
        "L3woT": a["L3_xattn_wo_w"].T, "L3w1T": a["L3_ffn_w1"].T, "L3w2T": a["L3_ffn_w2"].T,
    }
    nc = bacc.Bacc("TRN2", target_bir_lowering=False, num_devices=1)
    arrays, io = {}, {}
    for name, v in data.items():
        v = np.ascontiguousarray(v)
        arrays["in_" + name] = v
        io[name] = nc.dram_tensor("in_" + name, v.shape, mybir.dt.from_np(v.dtype), kind="ExternalInput").ap()
    out = nc.dram_tensor("out_0", (2048, 256), F32, kind="ExternalOutput").ap()
    build(nc, io, out)
    r = run(nc, [arrays], core_ids=[0])
    return r.results[0]["out_0"].reshape(8, 256, 256)
```

```python
import numpy as np
import concourse.bass as bass
import concourse.mybir as mybir
from contextlib import ExitStack

ACT = mybir.ActivationFunctionType
ALU = mybir.AluOpType
AX = mybir.AxisListType
F32 = mybir.dt.float32
BF16 = mybir.dt.bfloat16
U8 = mybir.dt.uint8

STAGES = 8
MAGIC = 12582912.0
BIG = float(2.0 ** 123)

COLS = {}
ROWS = {}


def _lay_cols():
    o = 0
    for name, n in (("lxw", 2), ("lxb", 2), ("llw", 2), ("llb", 2), ("ks", 1), ("qs", 1),
                    ("mw", 2), ("mb", 2), ("zw", 2), ("zb", 2), ("bin", 8), ("bq", 2)):
        COLS[name] = (o, n)
        o += n
    return o


def _lay_rows():
    o = 0
    for name, n in (("low", 256), ("lob", 256), ("bout", 256), ("bk", 256), ("bv", 256), ("bo", 256),
                    ("lng", 256), ("lnb", 256), ("fb1", 1024), ("fb2", 256), ("bg", 8)):
        ROWS[name] = (o, n)
        o += n
    return o


NCOL = _lay_cols()
NROW = _lay_rows()


class Mark:

    def __init__(self, queue):
        self.queue, self.used, self.value = queue, False, 0


class Arrival:

    def __init__(self, sem, value):
        self.sem, self.value = sem, value


def flat(after):
    for a in after:
        if a is None:
            continue
        if isinstance(a, (list, tuple)):
            yield from flat(a)
        else:
            yield a


class Queue:

    def __init__(self, sem):
        self.sem, self.items, self.last = sem, [], None

    def do(self, fn, *after):
        after = list(flat(after))
        for a in after:
            if isinstance(a, Mark):
                a.used = True
        m = Mark(self)
        self.items.append((fn, after, m, None))
        self.last = m
        return m

    def dma(self, sem, fn, *after):
        after = list(flat(after))
        for a in after:
            if isinstance(a, Mark):
                a.used = True
        self.items.append((fn, after, None, sem))

    def wait(self, *after):
        after = list(flat(after))
        for a in after:
            if isinstance(a, Mark):
                a.used = True
        self.items.append((None, after, None, None))

    def count(self):
        n = 0
        for _, _, m, _ in self.items:
            if m is not None and m.used:
                n += 1
                m.value = n

    def emit(self, eng):
        seen = {}
        for fn, after, m, dsem in self.items:
            for a in after:
                sem = a.queue.sem if isinstance(a, Mark) else a.sem
                if seen.get(id(sem), 0) < a.value:
                    eng.wait_ge(sem, a.value)
                    seen[id(sem)] = a.value
            if fn is None:
                continue
            ins = fn(eng)
            if dsem is not None:
                ins.then_inc(dsem, 16)
            elif m.used:
                ins.then_inc(self.sem, 1)


class Slot:
    def __init__(self, ap):
        self.ap, self.free = ap, None


class Ring:
    def __init__(self, aps):
        self.slots, self.i = [Slot(a) for a in aps], 0

    def take(self):
        s = self.slots[self.i % len(self.slots)]
        self.i += 1
        return s


def build(nc, io, out):
    ctx = ExitStack()
    with ctx:
        def sb(name, shape, dt=F32):
            return ctx.enter_context(nc.sbuf_tensor(name, shape, dt))

        def sem(name):
            return ctx.enter_context(nc.semaphore(name))

        X = sb("X", [128, 16, 256])
        ctxT = sb("ctxT", [128, 2, 2048])
        chatT = sb("chatT", [128, 2, 2048])
        HT = sb("HT", [128, 2, 2048])
        WA = sb("WA", [128, 8192])
        WB = sb("WB", [128, 8208])
        AR = sb("AR", [128, 14336])
        cols = sb("cols", [128, NCOL])
        rows = sb("rows", [128, NROW])
        ident = sb("ident", [128, 128])
        identb = sb("identb", [128, 128], BF16)
        diagb = sb("diagb", [128, 128], BF16)
        causb = sb("causb", [128, 2, 256], BF16)
        blk = sb("blk", [128, 128])
        onesf = sb("onesf", [128, 128])
        onesb = sb("onesb", [1, 128], BF16)
        onesbb = sb("onesbb", [128, 128], BF16)
        trib = sb("trib", [128, 128], BF16)
        iota = sb("iota", [128, 48])
        rev = sb("rev", [128, 8])
        nhalf = sb("nhalf", [128, 16])
        st = sb("st", [128, 8, 6])
        mv = sb("mv", [128, 16, 2])
        mv2 = sb("mv2", [128, 16, 2])
        cmv = sb("cmv", [128, 16, 2])
        rs = sb("rs", [128, 16])
        small = sb("small", [128, 704])
        banks = [ctx.enter_context(nc.psum_tensor(f"bank{i}", [128, 512], F32)) for i in range(8)]
        bank_slots = [Slot(b[:, :]) for b in banks]

        def ring_of(*ids):
            r = Ring([])
            r.slots = [bank_slots[i] for i in ids]
            return r

        PE, DV, AC, PO, SP = (Queue(sem(f"s_{n}")) for n in ("pe", "dv", "ac", "po", "sp"))

        def load(name, pairs, *after, q=None):
            s = sem(f"d_{name}")
            for o, i in pairs:
                (q or SP).dma(s, lambda e, o=o, i=i: e.dma_start(o, i), *after)
            return Arrival(s, 16 * len(pairs))

        def col(name, j=0):
            o, _ = COLS[name]
            return cols[:, o + j:o + j + 1]

        def row(name):
            o, n = ROWS[name]
            return rows[:, o:o + n]

        def region(base):
            state = [0]

            def take(words, dt=F32, **dims):
                v = base[:, state[0]:state[0] + words]
                state[0] += words
                assert state[0] <= base.shape[1], (state[0], base.shape)
                if dt is not F32:
                    v = v.bitcast(dt)
                if dims:
                    names = list(dims)
                    v = v.rearrange("p (" + " ".join(names) + ") -> p " + " ".join(names),
                                    **{k: dims[k] for k in names[1:]})
                return v
            return take

        def mm(o, l, r, start, stop, *after):
            return PE.do(lambda e: e.matmul(o, l, r, start=start, stop=stop), *after)

        def tr(o, i, idn, *after):
            return PE.do(lambda e: e.transpose(o, i, idn), *after)

        def tt(o, a, b, op, *after, q=None):
            return (q or DV).do(lambda e: e.tensor_tensor(o, a, b, op), *after)

        def ts(o, a, s1, s2, op0, op1, *after, q=None):
            if op1 is None:
                return (q or DV).do(lambda e: e.tensor_scalar(o, a, s1, None, op0), *after)
            return (q or DV).do(lambda e: e.tensor_scalar(o, a, s1, s2, op0, op1), *after)

        def recip(o, a, *after):
            return DV.do(lambda e: e.reciprocal(o, a), *after)

        def cp(o, a, *after, q=None):
            return (q or DV).do(lambda e: e.tensor_copy(o, a), *after)

        def act(o, a, f, *after, **kw):
            return AC.do(lambda e: e.activation(o, a, f, **kw), *after)

        def red(o, a, op, *after, **kw):
            return DV.do(lambda e: e.tensor_reduce(o, a, AX.X, op, **kw), *after)

        a_cst = load("cst", [(ident[:, :], io["consts"][:, 0:128]), 
                             (small[:, 0:640], io["consts"][:, 128:768]), (iota[:, :], io["consts"][:, 896:944]),
                             (blk[:, :], io["consts"][:, 768:896]), (cols[:, :], io["cols"])])
        ctx0 = AR[:, 0:4096].rearrange("p (t d) -> p t d", t=16)
        a_ctx = load("ctx", [(ctx0, io["ctx"].rearrange("(t p) d -> p t d", p=128))], q=AC)
        a_x = load("x", [(X[:, :, :], io["x"].rearrange("(t p) d -> p t d", p=128))])

        sorted_h0, sorted_y0, sorted_h2, sorted_y2 = (
            nc.dram_tensor(n, (k * 128, 256), F32, kind="Internal").ap()
            for n, k in (("sorted_h0", 23), ("sorted_y0", 23), ("sorted_h2", 39), ("sorted_y2", 39)))

        def clear(dram, n, name, *after):
            s = sem("d_" + name)
            for i in range(n):
                PO.dma(s, lambda e, i=i: e.dma_start(dram[i * 1024:min((i + 1) * 1024, dram.shape[0]), :].rearrange(
                    "(k p) n -> p k n", p=128),
                    zero[:, 0:(min((i + 1) * 1024, dram.shape[0]) - i * 1024) * 2].rearrange("p (k n) -> p k n", n=256)), *after)
            return Arrival(s, 16 * n)

        zero = WA[:, 4096:6144]
        m_zero = PO.do(lambda e: e.memset(zero, 0.0))
        cleared0 = clear(sorted_h0, 3, "z0", m_zero)
        cleared2 = clear(sorted_h2, 5, "z2", m_zero)

        def wview(dram):
            return dram.rearrange("(k p) n -> p k n", p=128)

        wt = region(WA)
        wq0, wk0 = wt(1024, k=2, n=512), wt(1024, k=2, n=512)
        wv0, wo0 = wt(512, k=2, n=256), wt(512, k=2, n=256)
        a_w0 = load("w0", [(wq0, wview(io["L0wqT"])), (wk0, wview(io["L0wkT"])),
                           (wv0, wview(io["L0wvT"])), (wo0, wview(io["L0woT"]))])
        a_rows = load("rows", [(rows[:, :], io["rows"].to_broadcast([128, NROW]))])

        m_id = [cp(identb[:, :], ident[:, :], a_cst),
                ts(diagb[:, :], ident[:, :], 4000.0, None, ALU.mult, None, a_cst),
                cp(causb[:, :, :], small[:, 0:512].rearrange("p (a b) -> p a b", a=2), a_cst)]
        m_id.append(cp(trib[:, :], small[:, 512:640], a_cst))
        m_rev = ts(rev[:, :], iota[:, 0:8], -1.0, 8.0, ALU.mult, ALU.add, a_cst)
        DV.do(lambda e: e.memset(onesbb[:, :], 1.0))
        m_one = DV.do(lambda e: e.memset(onesf[:, :], 1.0))
        m_oneb = DV.do(lambda e: e.memset(onesb[:, :], 1.0))
        m_nh = DV.do(lambda e: e.memset(nhalf[:, :], -0.5))

        def rstd(dst, var, n, *after, eps=1e-5, op=ALU.add):
            m = ts(dst, var, eps, None, op, None, *after, q=PO)
            return PO.do(lambda e: e.tensor_tensor(dst, dst, nhalf[:, 0:n], ALU.pow), m, m_nh)

        def stats(dst, src, t, *after):
            m = DV.do(lambda e: e.bn_stats(st[:, t % 8, :], src), *after)
            return DV.do(lambda e: e.bn_aggr(dst, st[:, t % 8, :]), m)

        Xm = [a_x] * 16

        def norm_T(src, srcm, keep, dst, mvt, ring, evac, *after, second=None, hook=None):
            done = [None] * 16
            tok = [None] * 16
            hs = [None] * 16
            r1, r2 = {}, {}

            def stat(g, dst, source):
                T = range(4 * g, 4 * g + 4)
                ms = [stats(dst[:, t, :], *source(t)) for t in T]
                return rstd(rs[:, 4 * g:4 * g + 4], dst[:, 4 * g:4 * g + 4, 1], 4, ms[-1], tok[4 * g:4 * g + 4])

            def normalise(g):
                for t in range(4 * g, 4 * g + 4):
                    s = keep.take()
                    tok[t] = ts(s.ap, src[:, t, :], mvt[:, t, 0:1], rs[:, t:t + 1], ALU.subtract, ALU.mult, r1[g], s.free)
                    hs[t] = s

            def again(g):
                for t in range(4 * g, 4 * g + 4):
                    tok[t] = ts(hs[t].ap, hs[t].ap, mv2[:, t, 0:1], rs[:, t:t + 1], ALU.subtract, ALU.mult, r2[g])

            def turn(g):
                if hook:
                    for t in range(4 * g, 4 * g + 4):
                        hook(t, hs[t], tok[t])
                for c in range(2):
                    b = ring.take()
                    for j in range(4):
                        s = hs[4 * g + j]
                        m = tr(b.ap[:, j * 128:(j + 1) * 128], s.ap[:, c * 128:(c + 1) * 128], ident[:, :],
                               tok[4 * g + j], b.free, a_cst)
                        if c == 1:
                            s.free = [s.free, m] if hook else m
                    m = evac(dst[:, c, g * 512:(g + 1) * 512], b.ap, c, m)
                    b.free = m
                    for t in range(4 * g, 4 * g + 4):
                        done[t] = [done[t], m]

            for i in range(6):
                if i < 4:
                    r1[i] = stat(i, mvt, lambda t: (src[:, t, :], t, srcm[t], after))
                if 0 <= i - 2 < 4 and second is not None:
                    again(i - 2)
                    turn(i - 2)
                if 0 <= i - 1 < 4:
                    normalise(i - 1)
                    if second is None:
                        turn(i - 1)
                    else:
                        r2[i - 1] = stat(i - 1, mv2, lambda t: (hs[t].ap, t, tok[t]))
            return done, tok

        def evac_copy(o, i, c, *after):
            return (act(o, i, ACT.Copy, *after) if c == 0 else cp(o, i, *after))

        def evac_affine(w, b):
            def f(o, i, c, *after):
                return act(o, i, ACT.Identity, *after, a_cst, scale=col(w, c), bias=col(b, c)) if c == 0 else \
                    ts(o, i, col(w, c), col(b, c), ALU.mult, ALU.add, *after, a_cst)
            return f

        def tiles_ring(buf, n):
            return Ring([buf[:, i, :] for i in range(n)])

        pre = ring_of(0, 1, 2, 3)
        ctx_m = [None] * 16
        for g in range(4):
            for c in range(2):
                b = pre.take()
                for j in range(4):
                    m = tr(b.ap[:, j * 128:(j + 1) * 128], ctx0[:, 4 * g + j, c * 128:(c + 1) * 128], ident[:, :],
                           a_ctx, a_cst, b.free)
                m = evac_copy(ctxT[:, c, g * 512:(g + 1) * 512], b.ap, c, m)
                b.free = m
                for t in range(4 * g, 4 * g + 4):
                    ctx_m[t] = [ctx_m[t], m]
        keep0 = tiles_ring(AR[:, 4096:6144].rearrange("p (t d) -> p t d", t=8), 8)
        chat_m, _ = norm_T(ctx0, [a_ctx] * 16, keep0, chatT, cmv, pre, evac_copy)

        def residual(t, src, *after):
            Xm[t] = tt(X[:, t, :], src, X[:, t, :], ALU.add, *after, Xm[t])
            return Xm[t]

        def attention(n, nsub, scores, pv, hooks, Pr, PTr, mx, sums, Sr, Tr):
            info = [dict() for _ in range(n)]
            w = 512 // nsub
            for i in range(n + 3):
                if i in hooks:
                    hooks[i]()
                if i < n:
                    u = info[i]
                    u["S"] = Sr.take()
                    u["ms"] = scores(i, u["S"])
                    k = (i % 4) * nsub
                    u["mx"] = red(mx[:, k:k + nsub], u["S"].ap.rearrange("p (a b) -> p a b", a=nsub), ALU.max,
                                  u["ms"], info[i - 4]["exp"] if i >= 4 else None, negate=True)
                    p = u["P"] = Pr.take()
                    for j in range(nsub):
                        m = act(p.ap[:, j * w:(j + 1) * w], u["S"].ap[:, j * w:(j + 1) * w], ACT.Exp,
                                u["mx"], p.free, bias=mx[:, k + j:k + j + 1],
                                accum_out=sums(i, j))
                    u["exp"] = m
                    u["S"].free = m
                if 0 <= i - 2 < n:
                    u = info[i - 2]
                    u["T"] = Tr.take()
                    for j in range(4):
                        m = tr(u["T"].ap[:, j * 128:(j + 1) * 128], u["P"].ap[:, j * 128:(j + 1) * 128], ident[:, :],
                               u["exp"], u["T"].free)
                    u["P"].free = m
                    q = u["PT"] = PTr.take()
                    u["pt"] = cp(q.ap, u["T"].ap, m, q.free)
                    u["T"].free = u["pt"]
                if 0 <= i - 3 < n:
                    u = info[i - 3]
                    u["PT"].free = pv(i - 3, u["PT"].ap, u["pt"], u["exp"])
            return info[n - 1]["PT"].free

        def layer0_attention():
            r = region(AR)
            r(4096)
            keep = tiles_ring(r(2048, t=8, d=256), 8)
            qT = [r(1024, c=4, n=256) for _ in range(2)]
            kT = [r(1024, c=4, n=256) for _ in range(2)]
            V = [r(512, c=2, n=256) for _ in range(2)]
            Pr, PTr = Ring([r(512) for _ in range(3)]), Ring([r(512) for _ in range(2)])
            Ob = [r(512, a=2, n=256)] * 2
            r0 = region(AR)
            OTs = [r0(512, c=2, n=256) for _ in range(2)]
            PTr.slots += [Slot(r0(512))]
            sm = small[:, 512:512 + 64].rearrange("p (s h a) -> p s h a", s=2, h=16)
            rc = small[:, 576:576 + 64].rearrange("p (s h a) -> p s h a", s=2, h=16)
            mx = small[:, 640:648]
            Sr, Tr, Or, Mr = ring_of(0, 1), ring_of(2, 3), ring_of(4, 5), ring_of(6, 7)
            ctx_done = [PE.last, chat_m]
            for s in keep.slots:
                s.free = ctx_done
            hm, _ = norm_T(X, Xm, keep, HT, mv, pre, evac_copy)
            slots = [dict(q=None, k=None, v=None, free=None) for _ in range(2)]
            proj = {}

            def project(b):
                s = b % 2
                lo, hi = b * 256, b * 256 + 256
                ready = [hm[2 * b], hm[2 * b + 1], ctx_m[2 * b], ctx_m[2 * b + 1], a_w0]
                free = proj.get(b - 2)
                ms = []
                for W, src, dst, sc in ((wq0, HT, qT, 0.0625), (wk0, ctxT, kT, None)):
                    for h in range(2):
                        bk = Mr.take()
                        for c in range(2):
                            for k in range(2):
                                m = mm(bk.ap[:, c * 256:(c + 1) * 256], W[:, k, (2 * h + c) * 128:(2 * h + c + 1) * 128],
                                       src[:, k, lo:hi], k == 0, k == 1, ready, bk.free)
                        o = dst[s][:, 2 * h:2 * h + 2, :]
                        i = bk.ap.rearrange("p (c n) -> p c n", c=2)
                        m = act(o, i, ACT.Copy, m, free, scale=sc) if sc else cp(o, i, m, free)
                        bk.free = m
                        ms.append(m)
                bk = Mr.take()
                for t in range(2):
                    for k in range(2):
                        m = mm(bk.ap[:, t * 256:(t + 1) * 256], ctxT[:, k, lo + t * 128:lo + t * 128 + 128],
                               wv0[:, k, :], k == 0, k == 1, ready, bk.free)
                m = act(V[s], bk.ap.rearrange("p (c n) -> p c n", c=2), ACT.Copy, m, free)
                bk.free = m
                ms.append(m)
                slots[s] = dict(ready=ms)

            def scores(i, S):
                b, h = divmod(i, 16)
                s, c, p = b % 2, h // 4, 32 * (h % 4)
                for a in range(2):
                    mm(S.ap[:, a * 256:(a + 1) * 256], qT[s][p:p + 32, c, a * 128:(a + 1) * 128],
                       kT[s][p:p + 32, c, :], True, False, slots[s]["ready"], S.free)
                    m = mm(S.ap[:, a * 256:(a + 1) * 256], diagb[:, :], causb[:, a, :], False, True, m_id)
                return m

            def sums(i, j):
                b, h = divmod(i, 16)
                return sm[:, b % 2, h, j:j + 1]

            O = {}
            fin = {}

            def pv(i, PT, *after):
                b, h = divmod(i, 16)
                if h == 0:
                    O[b] = Or.take()
                for a in range(2):
                    for k in range(2):
                        m = mm(O[b].ap[:, a * 256 + h * 16:a * 256 + h * 16 + 16], PT[:, (2 * a + k) * 128:(2 * a + k + 1) * 128],
                               V[b % 2][:, k, h * 16:(h + 1) * 16], k == 0, k == 1, after, O[b].free)
                if h == 15:
                    proj[b] = m
                    finish(b, m, after)
                return m

            def finish(b, m, after):
                s = b % 2
                r1 = recip(rc[:, s, :, :], sm[:, s, :, :], after)
                mo = None
                for a in range(2):
                    mo = tt(Ob[s][:, a, :].rearrange("p (h d) -> p h d", h=16),
                            O[b].ap[:, a * 256:(a + 1) * 256].rearrange("p (h d) -> p h d", h=16),
                            rc[:, s, :, a:a + 1].to_broadcast([128, 16, 16]), ALU.mult, m, r1, fin.get(b - 1))
                O[b].free = mo
                fin[b] = (mo,)

            def out_proj(b):
                s = b % 2
                mo = fin[b]
                bk = Mr.take()
                for c in range(2):
                    for a in range(2):
                        m = tr(bk.ap[:, c * 256 + a * 128:c * 256 + a * 128 + 128], Ob[s][:, a, c * 128:(c + 1) * 128],
                               ident[:, :], mo, bk.free)
                m2 = act(OTs[s], bk.ap.rearrange("p (c n) -> p c n", c=2), ACT.Copy, m, ctx_done)
                fin[b] = m
                bk.free = m2
                bk = Mr.take()
                for a in range(2):
                    for c in range(2):
                        m = mm(bk.ap[:, a * 256:(a + 1) * 256], OTs[s][:, c, a * 128:(a + 1) * 128], wo0[:, c, :],
                               c == 0, c == 1, m2, bk.free)
                for a in range(2):
                    bk.free = residual(2 * b + a, bk.ap[:, a * 256:(a + 1) * 256], m)

            project(0)
            hooks = {}
            for b in range(7):
                hooks[16 * b + 8] = lambda b=b: project(b + 1)
            for b in range(8):
                hooks.setdefault(16 * b + 16 + 5, None)
                hooks[16 * b + 21] = lambda b=b: out_proj(b)
            PTr.slots[-1].free = ctx_done
            attention(128, 2, scores, pv, hooks, Pr, PTr, mx, sums, Sr, Tr)
            out_proj(7)

        def gates(w_sb, wready, temp, topk, hm, bias, r):
            L = r(128, t=16, e=8)
            G = r(128, t=16, e=8)
            E = r(128, t=16, e=8)
            M = r(128 * topk, c=topk, t=16, e=8)
            S = r(128 * topk, c=topk, t=16, e=8)
            gv = r(16 * topk, c=topk, t=16)
            m1 = r(16)
            d = r(16)
            bk = ring_of(7).take()
            for t in range(16):
                for k in range(2):
                    m = mm(bk.ap[:, t * 8:(t + 1) * 8], HT[:, k, t * 128:(t + 1) * 128], w_sb[:, k, :],
                           k == 0, k == 1, hm[t], bk.free, wready)
            lg = bk.ap[:, 0:128].rearrange("p (t e) -> p t e", e=8)

            def bc(v):
                return v.rearrange("p (t o) -> p t o", o=1).to_broadcast([128, 16, 8])

            revb = rev[:, :].rearrange("p (o e) -> p o e", o=1).to_broadcast([128, 16, 8])
            if bias is not None:
                m = tt(L, lg, bias.rearrange("p (o e) -> p o e", o=1).to_broadcast([128, 16, 8]), ALU.add, m, a_rows)
                bk.free = m
                m = ts(L, L, 1.0 / temp, None, ALU.mult, None, m)
            else:
                m = cp(L, lg, m)
                bk.free = m
            m = red(m1, L, ALU.max, m)
            m = tt(E, L, bc(m1), ALU.subtract, m)
            me = act(E, E, ACT.Exp, m)
            sel = []
            for c in range(topk):
                if c:
                    m = ts(S[:, 0, :, :], M[:, c - 1, :, :], -3.0e38, None, ALU.mult, None, m)
                    m = tt(L, L, S[:, 0, :, :], ALU.add, m)
                    m = red(m1, L, ALU.max, m)
                m = tt(M[:, c, :, :], L, bc(m1), ALU.is_equal, m)
                m = tt(M[:, c, :, :], M[:, c, :, :], revb, ALU.mult, m, m_rev)
                m = red(m1, M[:, c, :, :], ALU.max, m)
                m = tt(M[:, c, :, :], M[:, c, :, :], bc(m1), ALU.is_equal, m)
                sel.append(m)
            md = red(d, E, ALU.add, me)
            md = recip(d, d, md)
            md = tt(E, E, bc(d), ALU.mult, md)
            for c in range(topk):
                md = tt(S[:, c, :, :], E, M[:, c, :, :], ALU.mult, md, sel)
                md = red(gv[:, c, :], S[:, c, :, :], ALU.add, md)
            if topk == 2:
                m = tt(d, gv[:, 0, :], gv[:, 1, :], ALU.add, md)
                m = ts(d, d, 1e-9, None, ALU.add, None, m)
                m = recip(d, d, m)
                for c in range(2):
                    md = tt(gv[:, c, :], gv[:, c, :], d, ALU.mult, m)
                m = tt(S[:, 0, :, :], S[:, 0, :, :], S[:, 1, :, :], ALU.add, md)
                md2 = tt(G, S[:, 0, :, :], bc(d), ALU.mult, m)
            else:
                md2 = cp(G, S[:, 0, :, :], md)
            return G, M, gv, md2, [md2, md], sel

        def route(M, sel, topk, nt, r):
            n = 16 * topk
            selb = r(64 * topk, dt=BF16)
            I = [r(8 * n, t=n, e=8) for _ in range(2)]
            Mf = M.rearrange("p c t e -> p (c t) e")
            nb = [r(8) for _ in range(3)]
            pos = r(n, dt=mybir.dt.int32)
            ex = r(nt, dt=mybir.dt.int32)
            posf = r(n)
            cmpb = r(8 * nt, i=nt, e=8)
            exf = r(nt)
            bk = ring_of(7).take()
            m = cp(selb, Mf.rearrange("p t e -> p (t e)"), sel)
            mm(bk.ap[:, 0:8 * n], trib[:, :], selb, True, True, m, bk.free, m_id)
            m = mm(bk.ap[:, 256:256 + 8 * n], onesbb[:, :], selb, True, True, m_one)
            pre_v = bk.ap[:, 0:8 * n].rearrange("p (t e) -> p t e", e=8)
            tot = bk.ap[:, 256:256 + 8 * n].rearrange("p (t e) -> p t e", e=8)
            m = cp(I[0], tot, m)
            cur, st_ = 0, 1
            while st_ < n:
                o, i = I[1 - cur], I[cur]
                m1 = tt(o[:, st_:n, :], i[:, st_:n, :], i[:, 0:n - st_, :], ALU.add, m)
                m2 = cp(o[:, 0:st_, :], i[:, 0:st_, :], m)
                m = [m1, m2]
                cur, st_ = 1 - cur, st_ * 2
            inc, exc = I[cur], I[1 - cur]
            m = tt(exc, inc, tot, ALU.subtract, m)
            ma = tt(exc, exc, pre_v, ALU.add, m)
            bk.free = ma
            m = ts(nb[0], inc[:, n - 1, :], 63.5, 1.0 / 128, ALU.add, ALU.mult, m)
            m = ts(nb[0], nb[0], MAGIC, MAGIC, ALU.add, ALU.subtract, m)
            m = cp(nb[1], nb[0], m)
            cur, st_ = 1, 1
            while st_ < 8:
                o, i = nb[3 - cur], nb[cur]
                m1 = tt(o[:, st_:8], i[:, st_:8], i[:, 0:8 - st_], ALU.add, m)
                m2 = cp(o[:, 0:st_], i[:, 0:st_], m)
                m = [m1, m2]
                cur, st_ = 3 - cur, st_ * 2
            T = nb[cur]
            mt = m
            m = tt(nb[0], T, nb[0], ALU.subtract, mt)
            m = ts(nb[0], nb[0], 128.0, None, ALU.mult, None, m)
            m = tt(exc, exc, nb[0].rearrange("p (o e) -> p o e", o=1).to_broadcast([128, n, 8]), ALU.add, m, ma)
            m = tt(exc, exc, Mf, ALU.mult, m)
            m = red(posf, exc, ALU.add, m)
            m_pos = cp(pos, posf, m)
            m = tt(cmpb[0:1, :, :], T[0:1, :].rearrange("p (o e) -> p o e", o=1).to_broadcast([1, nt, 8]),
                   iota[0:1, 0:nt].rearrange("p (i o) -> p i o", o=1).to_broadcast([1, nt, 8]), ALU.is_le, mt, a_cst)
            m = red(exf[0:1, :], cmpb[0:1, :, :], ALU.add, m)
            m = ts(ex[0:1, :], exf[0:1, :], 7.0, None, ALU.min, None, m)
            return pos, ex, m_pos, m

        def experts(tag, ff, topk, nt, pack, b2d, gate_d, temp, bias, wbufs, sorted_h, sorted_y, cleared):
            f = fence()
            r = region(AR)
            Hn = r(4096, t=16, d=256)
            keep = tiles_ring(Hn, 16)
            for s in keep.slots:
                s.free = f
            gw = r(16, k=2, n=8)
            a_g = load(tag + "gw", [(gw, wview(gate_d))], f)
            hm, tok = norm_T(X, Xm, keep, HT, mv, pre, evac_copy)
            nf = ff // 128
            nw = 4 * ff + nf
            G, M, gv, gm, gvm, sel = gates(gw, a_g, temp, topk, hm, bias, r)
            pos, ex, m_pos, m_ex = route(M, sel, topk, nt, r)
            b2 = r(256)
            a_b2 = load(tag + "b2", [(b2[0:8, :], b2d)], f)
            xs = Ring([r(256) for _ in range(3)])
            xT = Ring([r(256, k=2, n=128) for _ in range(2)])
            gb = Ring([r(ff, f=nf, n=128) for _ in range(2)])
            ys = Ring([r(256) for _ in range(3)])
            wbufs = [w for w in wbufs(r)]
            wr = Ring(wbufs)
            for g in (xs, wr, ys):
                for i, s in enumerate(g.slots):
                    s.sem, s.n = sem(f"d_{tag}{'x' if g is xs else 'w' if g is wr else 'y'}{i}"), 0
            s_sc = sem(f"d_{tag}sc")
            for c in range(topk):
                for t in range(16):
                    i = c * 16 + t
                    PO.dma(s_sc, lambda e, i=i, t=t: e.indirect_dma_start(
                        out=sorted_h, out_offset=bass.IndirectOffsetOnAxis(ap=pos[:, i:i + 1], axis=0),
                        in_=Hn[:, t, :], in_offset=None), m_pos, tok[t], cleared)
            scattered = Arrival(s_sc, 256 * topk)

            def arrival(s):
                s.n += 16
                return Arrival(s.sem, s.n)

            regs = {}

            def load_w(i):
                s = wr.take()
                SP.wait(m_ex, f, s.free)

                def fn(e, i=i, s=s):
                    v = e.value_load(ex[0:1, i:i + 1], min_val=0, max_val=7)
                    return e.dma_start(s.ap[:, 0:nw].rearrange("p (o n) -> p o n", o=1),
                                       pack[bass.ds(v, 1), :, :].rearrange("o p n -> p o n"))
                SP.dma(s.sem, fn)
                return s, arrival(s)

            def load_x(i):
                s = xs.take()
                SP.dma(s.sem, lambda e: e.dma_start(s.ap, sorted_h[i * 128:(i + 1) * 128, :]), s.free, scattered, f)
                return s, arrival(s)

            GT = gb.slots[0].ap.rearrange("p f n -> p (f n)")
            Yr = ring_of(4, 5)
            for h in range(0, 16, nf):
                for t in range(h, h + nf):
                    if t % 4 == 0:
                        bk = ring_of(7).take()
                    m = tr(bk.ap[0:8, (t % 4) * 128:(t % 4 + 1) * 128], G[:, t, :], ident[:, :], gm, bk.free)
                    if t % 4 == 3:
                        gtm = cp(GT[0:8, (t - 3 - h) * 128:(t + 1 - h) * 128], bk.ap[0:8, :], m, gb.slots[0].free)
                        bk.free = gtm
                for t in range(h, h + nf, 2):
                    bk = Yr.take()
                    for a in range(2):
                        m = mm(bk.ap[:, a * 256:(a + 1) * 256], GT[0:8, (t + a - h) * 128:(t + a + 1 - h) * 128], b2[0:8, :],
                               True, True, gtm, a_b2, bk.free)
                    gb.slots[0].free = m
                    for a in range(2):
                        bk.free = residual(t + a, bk.ap[:, a * 256:(a + 1) * 256], m)

            Tr, Hr = ring_of(6, 7), ring_of(0, 1, 2, 3)
            lw, lx, xt, gt = {}, {}, {}, {}
            nwb = len(wbufs)
            for i in range(min(nwb, nt)):
                lw[i] = load_w(i)
            for i in range(3):
                lx[i] = load_x(i)

            def turn(i):
                s, a = lx[i]
                T = Tr.take()
                for k in range(2):
                    m = tr(T.ap[:, k * 128:(k + 1) * 128], s.ap[:, k * 128:(k + 1) * 128], ident[:, :], a, T.free)
                s.free = m
                o = xT.take()
                m = cp(o.ap, T.ap[:, 0:256].rearrange("p (k n) -> p k n", k=2), m, o.free)
                T.free = m
                xt[i] = (o, m)
                if i + 3 < nt:
                    lx[i + 3] = load_x(i + 3)

            def up(i):
                o, mx_ = xt[i]
                w, aw = lw[i]
                g = gb.take()
                ms = []
                for q in range(nf // 4):
                    bk = Hr.take()
                    for j in range(4):
                        ft = 4 * q + j
                        for k in range(2):
                            m = mm(bk.ap[:, j * 128:(j + 1) * 128], w.ap[:, k * ff + ft * 128:k * ff + ft * 128 + 128],
                                   o.ap[:, k, :], k == 0, k == 1, aw, mx_, bk.free)
                    for j in range(4):
                        ft = 4 * q + j
                        m2 = act(g.ap[:, ft, :], bk.ap[:, j * 128:(j + 1) * 128], ACT.Gelu, m, g.free,
                                 bias=w.ap[:, 4 * ff + ft:4 * ff + ft + 1])
                        ms.append(m2)
                    bk.free = m2
                o.free = m
                gt[i] = (g, ms)

            def down(i):
                g, ms = gt[i]
                w, aw = lw[i]
                bk = Yr.take()
                for k in range(nf):
                    m = mm(bk.ap[:, 0:256], g.ap[:, k, :], w.ap[:, 2 * ff + k * 256:2 * ff + (k + 1) * 256],
                           k == 0, k == nf - 1, ms[k], bk.free)
                g.free = w.free = m
                y = ys.take()
                m = cp(y.ap, bk.ap[:, 0:256], m, y.free)
                bk.free = m
                if i + nwb < nt:
                    lw[i + nwb] = load_w(i + nwb)
                SP.dma(y.sem, lambda e: e.dma_start(sorted_y[i * 128:(i + 1) * 128, :], y.ap), m)
                y.free = arrival(y)

            turn(0)
            up(0)
            turn(1)
            for i in range(nt):
                if i + 1 < nt:
                    up(i + 1)
                if i + 2 < nt:
                    turn(i + 2)
                down(i)
            stored = [y.free for y in ys.slots]
            back = keep
            for s in back.slots:
                s.free = scattered
            for i, s in enumerate(back.slots):
                s.sem, s.n = sem(f"d_{tag}g{i}"), 0
            for t in range(16):
                for c in range(topk):
                    i = c * 16 + t
                    s = back.take()
                    PO.dma(s.sem, lambda e, i=i, s=s: e.indirect_dma_start(
                        out=s.ap, out_offset=None, in_=sorted_y,
                        in_offset=bass.IndirectOffsetOnAxis(ap=pos[:, i:i + 1], axis=0)), stored, s.free)
                    a = arrival(s)
                    Xm[t] = DV.do(lambda q, t=t, s=s, g=gv[:, c, t:t + 1]: q.scalar_tensor_tensor(
                        out=X[:, t, :], in0=s.ap, scalar=g, in1=X[:, t, :], op0=ALU.mult, op1=ALU.add), a, Xm[t], gvm)
                    s.free = Xm[t]

        def fence():
            f = [PE.last, DV.last, AC.last, PO.last]
            for q in (DV, AC, PO):
                q.wait(f)
            return f

        def layer0_ffn():
            def wbufs(r):
                return [WB[:, 0:4104], WB[:, 4104:8208], r(4104)]
            experts("e0", 1024, 1, 23, io["L0pack"], io["L0b2"], io["L0gate"], 1.0, None, wbufs,
                    sorted_h0, sorted_y0, cleared0)

        def layer2_ffn():
            def wbufs(r):
                return [WB[:, i * 2052:(i + 1) * 2052] for i in range(4)]
            experts("e2", 512, 2, 39, io["L2pack"], io["L2b2"], io["L2Wg"], 5.0, row("bg"), wbufs,
                    sorted_h2, sorted_y2, cleared2)

        def perceiver(which, W, a_w, xw, xb, zw, zb):
            f = fence()
            r = region(AR)
            keep = tiles_ring(r(2048, t=8, d=256), 8)
            for s in keep.slots:
                s.free = f
            wbh = region(WB)
            wbh(4096)
            kT = [r(2048, c=4, n=512), wbh(2048, c=4, n=512)]
            V = [r(2048, t=4, n=512), wbh(2048, t=4, n=512)]
            qT = [r(1024, c=4, n=256) for _ in range(2)]
            xT = [r(512, c=2, n=256) for _ in range(2)]
            Pr, PTr = Ring([r(512) for _ in range(3)]), Ring([r(512) for _ in range(2)])
            r2 = region(AR)
            Obs = [r2(512) for _ in range(1)]
            OTs = [r2(512, c=4, n=128) for _ in range(1)]
            sq, kn = Ring([r(512)]), Ring([r2(512), r2(512)])
            yb = r(256)
            sm = small[:, 512:512 + 32].rearrange("p (s h) -> p s h", s=4)
            rc = small[:, 544:544 + 32].rearrange("p (s h) -> p s h", s=4)
            mx = small[:, 640:648]
            ss = Ring([small[:, 656:664], small[:, 664:672]])
            Sr, Tr, Or, Mr = ring_of(0, 1), ring_of(2, 3), ring_of(4, 5), ring_of(6, 7)
            hm, _ = norm_T(X, Xm, keep, HT, mv, pre, evac_affine(zw, zb), second=True)
            f2 = fence()
            for s in kn.slots:
                s.free = f2
            obfree, otfree = f2, f2
            proj_free = {}
            ready = {}

            def project(b):
                s = b % 2
                lo = b * 256
                free = [proj_free.get(b - 2), f2]
                done = []
                pieces = []
                xs = []

                def affine():
                    for c in range(2):
                        xs.append(ts(xT[s][:, c, :], chatT[:, c, lo:lo + 256], col(xw, c), col(xb, c), ALU.mult, ALU.add,
                                     chat_m[2 * b], chat_m[2 * b + 1], free, a_cst, q=DV))
                pieces.append(affine)

                def src(t):
                    return (xT[s], t * 128, xs) if t < 2 else (HT, lo + (t - 2) * 128, hm[2 * b + t - 2])

                def value(t):
                    sr, o, dep = src(t)
                    bk = Mr.take()
                    for k in range(2):
                        m = mm(bk.ap, sr[:, k, o:o + 128], wv[:, k, :], k == 0, k == 1, dep, a_w, bk.free)
                    m = act(V[s][:, t, :], bk.ap, ACT.Copy, m, free)
                    bk.free = m
                    done.append(m)

                def normed(t, w, dst, at, scale_col):
                    sr, o, dep = src(t)
                    bk = Mr.take()
                    for k in range(2):
                        m = mm(bk.ap, sr[:, k, o:o + 128], w[:, k, :], k == 0, k == 1, dep, a_w, bk.free)
                    q = sq.take()
                    m1 = act(q.ap, bk.ap, ACT.Square, m, q.free)
                    v = ss.take()
                    m2 = red(v.ap, q.ap.rearrange("p (h d) -> p h d", h=8), ALU.add, m1, v.free)
                    q.free = m2
                    m3 = rstd(v.ap, v.ap, 8, m2, eps=1e-24, op=ALU.max)
                    z = kn.take()
                    m4 = tt(z.ap.rearrange("p (h d) -> p h d", h=8), bk.ap.rearrange("p (h d) -> p h d", h=8),
                            v.ap.rearrange("p (h o) -> p h o", o=1).to_broadcast([128, 8, 64]), ALU.mult, m3, z.free)
                    v.free = m4
                    bk.free = m4

                    def second():
                        T = Tr.take()
                        for c in range(4):
                            m5 = tr(T.ap[:, c * 128:(c + 1) * 128], z.ap[:, c * 128:(c + 1) * 128], ident[:, :], m4, T.free)
                        z.free = m5
                        m6 = act(dst[:, :, at:at + 128], T.ap.rearrange("p (c n) -> p c n", c=4), ACT.Copy, m5, free, m_qs,
                                 scale=scale_col)
                        T.free = m6
                        done.append(m6)
                    return second

                def plain(w, sr, o, n, dst, at, sc, dep):
                    per = 512 // n
                    for c0 in range(0, 4, per):
                        bk = Mr.take()
                        for c in range(per):
                            for k in range(2):
                                m = mm(bk.ap[:, c * n:(c + 1) * n], w[:, k, (c0 + c) * 128:(c0 + c + 1) * 128],
                                       sr[:, k, o:o + n], k == 0, k == 1, dep, a_w, bk.free)
                        m = act(dst[:, c0:c0 + per, at:at + n], bk.ap.rearrange("p (c n) -> p c n", c=per), ACT.Copy, m, free,
                                scale=sc)
                        bk.free = m
                        done.append(m)

                if which == 1:
                    later = []
                    for t in range(4):
                        pieces.append(lambda t=t: later.append(normed(t, wk, kT[s], t * 128, col("ks"))))
                        pieces.append(lambda t=t: (later.pop()(), value(t)))
                        if t >= 2:
                            pieces.append(lambda t=t: later.append(normed(t, wq, qT[s], (t - 2) * 128, qs8)))
                            pieces.append(lambda t=t: later.pop()())
                else:
                    pieces.append(lambda: plain(wk, xT[s], 0, 256, kT[s], 0, 1.0, xs))
                    for t in range(4):
                        pieces.append(lambda t=t: value(t))
                    hd = [hm[2 * b], hm[2 * b + 1]]
                    pieces.append(lambda: plain(wk, HT, lo, 256, kT[s], 256, 1.0, hd))
                    pieces.append(lambda: plain(wq, HT, lo, 256, qT[s], 0, 0.125, hd))
                ready[b] = done
                return pieces

            wq, wk, wv, wo = W
            qs8 = small[:, 650:651]
            m_qs = ts(qs8, col("qs"), 8.0, None, ALU.mult, None, a_cst, f)
            neg = None
            if which == 1:
                nb = r(1024, dt=BF16)[0:1, :]
                mk = r(512, dt=U8)[0:1, :]
                a_mk = load("mk", [(mk, io["mask1"])], f)
                neg = ts(nb, mk, 1.0, BIG, ALU.subtract, ALU.mult, a_mk)

            def scores(i, S):
                b, rest = divmod(i, 16)
                a, h = divmod(rest, 8)
                s, c, p = b % 2, h // 2, 64 * (h % 2)
                m = mm(S.ap, qT[s][p:p + 64, c, a * 128:(a + 1) * 128], kT[s][p:p + 64, c, :], True, which != 1,
                       ready[b], S.free)
                if which == 1:
                    m = mm(S.ap[:, 0:256], onesb[:, :], nb[:, b * 256:(b + 1) * 256], False, True, neg, m_oneb)
                return m

            def sums(i, j):
                g, h = divmod(i, 8)
                return sm[:, g % 4, h:h + 1]

            O, fin = {}, {}

            def pv(i, PT, *after):
                g, h = divmod(i, 8)
                b = g // 2
                if h == 0:
                    O[g] = Or.take()
                for k in range(4):
                    m = mm(O[g].ap[:, h * 64:(h + 1) * 64], PT[:, k * 128:(k + 1) * 128],
                           V[b % 2][:, k, h * 64:(h + 1) * 64], k == 0, k == 3, after, O[g].free)
                if h == 7:
                    if g % 2 == 1:
                        proj_free[b] = m
                    s = g % 4
                    r1 = recip(rc[:, s, :], sm[:, s, :], after)
                    fin[g] = tt(Obs[0].rearrange("p (h d) -> p h d", h=8),
                                O[g].ap.rearrange("p (h d) -> p h d", h=8),
                                rc[:, s, :].rearrange("p (h o) -> p h o", o=1).to_broadcast([128, 8, 64]),
                                ALU.mult, m, r1, obf[0])
                    O[g].free = fin[g]
                return m

            obf, otf, ybf = [obfree], [otfree], [f2]

            def out_proj(g):
                T = Mr.take()
                for c in range(4):
                    m = tr(T.ap[:, c * 128:(c + 1) * 128], Obs[0][:, c * 128:(c + 1) * 128], ident[:, :], fin[g], T.free)
                obf[0] = m
                m = act(OTs[0], T.ap.rearrange("p (c n) -> p c n", c=4), ACT.Copy, m, otf[0])
                T.free = m
                T = Mr.take()
                for c in range(4):
                    m = mm(T.ap[:, 0:256], OTs[0][:, c, :], wo[:, c, :], c == 0, c == 3, m, T.free)
                otf[0] = m
                if which == 2:
                    T.free = residual(g, T.ap[:, 0:256], m)
                    return
                ms = stats(mv2[:, g, :], T.ap[:, 0:256], g, m)
                mr = rstd(rs[:, g:g + 1], mv2[:, g, 1:2], 1, ms)
                m = ts(yb, T.ap[:, 0:256], mv2[:, g, 0:1], rs[:, g:g + 1], ALU.subtract, ALU.mult, mr, ms, ybf[0])
                T.free = m
                m = tt(yb, yb, row("low"), ALU.mult, m, a_rows, q=PO)
                m = tt(yb, yb, row("lob"), ALU.add, m, q=PO)
                ybf[0] = residual(g, yb, m)

            for p in project(0):
                p()
            hooks = {}

            def add(i, fn):
                old = hooks.get(i)
                hooks[i] = (lambda: (old(), fn())) if old else fn

            for b in range(7):
                def start(b=b):
                    pc = project(b + 1)
                    state[b] = pc
                    pc[0]()
                state = {}
                n = 13 if which == 1 else 8
                add(16 * b + 3, lambda b=b: state.__setitem__(b, project(b + 1)) or state[b][0]())
                for j in range(1, n):
                    add(16 * b + 3 + j, lambda b=b, j=j: state[b][j]())
            for g in range(15):
                add(8 * g + 8 + 4, lambda g=g: out_proj(g))
            attention(128, 1, scores, pv, hooks, Pr, PTr, mx, sums, Sr, Tr)
            out_proj(15)

        def all_max(dst, src, n, ring, *after):
            m = red(dst, src, ALU.max, *after)
            b = ring.take()
            m = tr(b.ap[0:1, 0:128], dst, ident[:, :], m, b.free)
            m = red(dst[0:1, :], b.ap[0:1, 0:128], ALU.max, m)
            m = mm(b.ap[:, 256:257], onesf[0:1, :], dst[0:1, :], True, True, m, m_one)
            m = cp(dst, b.ap[:, 256:257], m)
            b.free = m
            return m

        def layer1_ffn(WI, WO, a_w):
            f = fence()
            r = region(AR)
            am = small[:, 0:64]
            sc = small[:, 64:72]
            keep = tiles_ring(r(2048, t=8, d=256), 8)
            for s in keep.slots:
                s.free = f
            hid3 = AR[:, 0:12288].rearrange("p (g f n) -> p g f n", g=3, f=8)
            W1 = AR[:, 12288:14336].rearrange("p (k n) -> p k n", k=2)
            hid1 = WB[:, 4096:8192].rearrange("p (f n) -> p f n", f=8)

            def hid(n):
                return hid3[:, n, :, :] if n < 3 else hid1
            aw = small[:, 80:96]
            sw = small[:, 96:112]
            iw = small[:, 112:128]
            wm = []
            for j, Wt in ((0, WI), (8, WO)):
                m = red(aw[:, j:j + 8], Wt, ALU.max, a_w, f, apply_absolute_value=True)
                wm.append(m)
            m = ts(aw, aw, 1e-8, None, ALU.max, None, wm)
            m = recip(sw, aw, m)
            m = ts(sw, sw, 127.0, None, ALU.mult, None, m)
            mi = ts(iw, aw, 1.0 / 127.0, None, ALU.mult, None, m)
            w_ready = []
            for j, Wt in ((0, WI), (8, WO)):
                for k in range(8):
                    m1 = ts(Wt[:, k, :], Wt[:, k, :], sw[:, j + k:j + k + 1], MAGIC, ALU.mult, ALU.add, m, mi)
                    m1 = ts(Wt[:, k, :], Wt[:, k, :], MAGIC, iw[:, j + k:j + k + 1], ALU.subtract, ALU.mult, m1)
                    w_ready.append(m1)
            t1 = []
            rr = ring_of(4, 5)
            for k in range(2):
                for q in range(2):
                    b = rr.take()
                    for j in range(4):
                        m = tr(b.ap[:, j * 128:(j + 1) * 128], WI[:, 4 * q + j, k * 128:(k + 1) * 128], ident[:, :],
                               w_ready, b.free)
                    m = act(W1[:, k, q * 512:(q + 1) * 512], b.ap, ACT.Copy, m, f)
                    b.free = m
                    t1.append(m)

            def hook(t, s, m):
                s.free = red(am[:, t:t + 1], s.ap, ALU.max, m, f, apply_absolute_value=True)

            hm, _ = norm_T(X, Xm, keep, HT, mv, pre, evac_copy, hook=hook)
            m = all_max(sc[:, 0:1], am[:, 0:16], 16, ring_of(7), DV.last)
            m = ts(sc[:, 0:1], sc[:, 0:1], 1e-8, None, ALU.max, None, m)
            m = recip(sc[:, 1:2], sc[:, 0:1], m)
            m = ts(sc[:, 1:2], sc[:, 1:2], 32767.0, None, ALU.mult, None, m)
            m = ts(sc[:, 2:3], sc[:, 0:1], 1.0 / 32767.0, None, ALU.mult, None, m)
            hq = []
            for n in range(4):
                v = HT[:, :, n * 512:(n + 1) * 512]
                m1 = ts(v, v, sc[:, 1:2], MAGIC, ALU.mult, ALU.add, m, hm[4 * n:4 * n + 4])
                hq.append(ts(v, v, MAGIC, sc[:, 2:3], ALU.subtract, ALU.mult, m1))
            f3 = [hm, w_ready, t1]
            Hr, Yr = ring_of(0, 1, 2, 3), ring_of(4, 5, 6)
            gm = []
            for n in range(4):
                for k in range(8):
                    b = Hr.take()
                    for c in range(2):
                        m = mm(b.ap, W1[:, c, k * 128:(k + 1) * 128], HT[:, c, n * 512:(n + 1) * 512], c == 0, c == 1,
                               hq[n], t1, b.free)
                    m = act(hid(n)[:, k, :], b.ap, ACT.Gelu, m, f3, a_cst, bias=col("bin", k))
                    b.free = m
                    u = small[:, 160 + 8 * n + k:161 + 8 * n + k]
                    gm.append(red(u, hid(n)[:, k, :], ALU.max, m, apply_absolute_value=True))
            m = all_max(sc[:, 3:4], small[:, 160:192], 32, ring_of(7), gm)
            m = ts(sc[:, 3:4], sc[:, 3:4], 1e-8, None, ALU.max, None, m)
            m = recip(sc[:, 4:5], sc[:, 3:4], m)
            m = ts(sc[:, 4:5], sc[:, 4:5], 32767.0, None, ALU.mult, None, m)
            ms = ts(sc[:, 5:6], sc[:, 3:4], 1.0 / 32767.0, None, ALU.mult, None, m)
            for n in range(4):
                qs = []
                for k in range(0, 8, 2):
                    v = hid(n)[:, k:k + 2, :]
                    m1 = ts(v, v, sc[:, 4:5], MAGIC, ALU.mult, ALU.add, ms)
                    qs.append(ts(v, v, MAGIC, sc[:, 5:6], ALU.subtract, ALU.mult, m1))
                for j in range(4):
                    t = 4 * n + j
                    b = Yr.take()
                    for k in range(8):
                        m = mm(b.ap[:, 0:256], hid(n)[:, k, j * 128:(j + 1) * 128], WO[:, k, :], k == 0, k == 7,
                               qs, b.free)
                    Xm[t] = tt(X[:, t, :], X[:, t, :], row("bout"), ALU.add, Xm[t], a_rows)
                    b.free = residual(t, b.ap[:, 0:256], m)

        def layer3_attention(wq, wk, wv, wo, a_w):
            f = fence()
            r = region(AR)
            Hn = r(4096, t=16, d=256)
            keep = tiles_ring(Hn, 16)
            for s in keep.slots:
                s.free = f
            hm, tok = norm_T(X, Xm, keep, HT, mv, pre, evac_copy)
            mk = r(1024, dt=U8, t=16, n=256)
            a_m = load("mask0", [(mk, io["mask0"].rearrange("(t p) n -> p t n", p=128))], f)
            pen = small[:, 0:16]
            m = red(pen, mk, ALU.max, a_m, f)
            m_pen = ts(pen, pen, -3.0e38, 3.0e38, ALU.mult, ALU.mult, m)
            Ks, Vs, Qs, As, Cs = (Ring([r(512, a=2, n=256) for _ in range(2)]) for _ in range(5))
            Qs.slots.append(Slot(r(512, a=2, n=256)))
            ys = Ring([r(256) for _ in range(4)])
            R = ring_of(0, 1, 2, 3, 4, 5, 6, 7)

            def first(b):
                lo = b * 256
                kv = []
                for w, rg, bias in ((wk, Ks, "bk"), (wv, Vs, "bv")):
                    bk = R.take()
                    for a in range(2):
                        for k in range(2):
                            m = mm(bk.ap[:, a * 256:(a + 1) * 256], ctxT[:, k, lo + a * 128:lo + (a + 1) * 128], w[:, k, :],
                                   k == 0, k == 1, a_w, bk.free, ctx_m[2 * b + a])
                    s = rg.take()
                    m = tt(s.ap, bk.ap.rearrange("p (a n) -> p a n", a=2),
                           row(bias).rearrange("p (o n) -> p o n", o=1).to_broadcast([128, 2, 256]), ALU.add, m, s.free, a_rows, f)
                    bk.free = m
                    kv.append((s, m))
                bk = R.take()
                for c in range(2):
                    for k in range(2):
                        m = mm(bk.ap[:, c * 256:(c + 1) * 256], wq[:, k, c * 128:(c + 1) * 128], HT[:, k, lo:lo + 256],
                               k == 0, k == 1, a_w, bk.free, hm[2 * b], hm[2 * b + 1])
                q = Qs.take()
                for c in range(2):
                    m2 = act(q.ap[:, c, :], bk.ap[:, c * 256:(c + 1) * 256], ACT.Identity, m, q.free, a_cst, f, bias=col("bq", c))
                bk.free = m2
                return kv, (q, m2)

            def second(b, kv, q):
                (K, mk_), (V, mv_) = kv
                bk = R.take()
                for c in range(2):
                    for a in range(2):
                        m = mm(bk.ap[:, c * 128:(c + 1) * 128], K.ap[:, a, c * 128:(c + 1) * 128],
                               V.ap[:, a, c * 128:(c + 1) * 128], a == 0, a == 1, mk_, mv_, bk.free)
                K.free = V.free = m
                A = As.take()
                m = tt(A.ap[:, 0, :].rearrange("p (c n) -> p c n", c=2), bk.ap[:, 0:256].rearrange("p (c n) -> p c n", c=2),
                       blk[:, :].rearrange("p (o n) -> p o n", o=1).to_broadcast([128, 2, 128]), ALU.mult, m, A.free, a_cst, f)
                bk.free = m
                return A, m

            def third(b, q, A, am_):
                bk = R.take()
                for c in range(2):
                    m = mm(bk.ap[:, c * 256:(c + 1) * 256], A.ap[:, 0, c * 128:(c + 1) * 128], q[0].ap[:, c, :], True, True,
                           am_, q[1], bk.free)
                q[0].free = A.free = m
                C = Cs.take()
                m = act(C.ap, bk.ap.rearrange("p (c n) -> p c n", c=2), ACT.Copy, m, C.free, f)
                bk.free = m
                return C, m

            def fourth(b, C, cm):
                bk = R.take()
                for a in range(2):
                    for c in range(2):
                        m = mm(bk.ap[:, a * 256:(a + 1) * 256], C.ap[:, c, a * 128:(a + 1) * 128], wo[:, c, :],
                               c == 0, c == 1, cm, bk.free)
                C.free = m
                mms = []
                yy = []
                for a in range(2):
                    t = 2 * b + a
                    y = ys.take()
                    m1 = tt(y.ap, bk.ap[:, a * 256:(a + 1) * 256], row("bo"), ALU.add, m, y.free, a_rows, f)
                    bk.free = m1
                    m1 = DV.do(lambda e, y=y, t=t: e.scalar_tensor_tensor(out=y.ap, in0=Hn[:, t, :], scalar=pen[:, t:t + 1],
                               in1=y.ap, op0=ALU.add, op1=ALU.add), m1, m_pen, tok[t])
                    mms.append(stats(mv2[:, t, :], y.ap, t, m1))
                    yy.append(y)
                mr = rstd(rs[:, 2 * b:2 * b + 2], mv2[:, 2 * b:2 * b + 2, 1], 2, mms, tok[2 * b], tok[2 * b + 1])
                for a in range(2):
                    t = 2 * b + a
                    y = yy[a]
                    m1 = ts(y.ap, y.ap, mv2[:, t, 0:1], rs[:, t:t + 1], ALU.subtract, ALU.mult, mr, mms)
                    m1 = tt(y.ap, y.ap, row("lng"), ALU.mult, m1, q=PO)
                    m1 = tt(y.ap, y.ap, row("lnb"), ALU.add, m1, q=PO)
                    y.free = residual(t, y.ap, m1)

            s1, s2, s3 = {}, {}, {}
            for i in range(8 + 3):
                if i < 8:
                    s1[i] = first(i)
                if 0 <= i - 1 < 8:
                    s2[i - 1] = second(i - 1, *s1[i - 1])
                if 0 <= i - 2 < 8:
                    s3[i - 2] = third(i - 2, s1[i - 2][1], *s2[i - 2])
                if 0 <= i - 3 < 8:
                    fourth(i - 3, *s3[i - 3])

        def layer3_ffn(w1, w2, a_w):
            f = fence()
            r = region(AR)
            wq1 = r(1024, dt=BF16, k=2, n=1024)
            wq2 = r(1024, dt=BF16, k=8, n=256)
            sc = small[:, 0:8]
            R = ring_of(6, 7)
            iws = []
            wr = []
            for j, (w, wq, n) in enumerate(((w1, wq1, 262144.0), (w2, wq2, 262144.0))):
                v = sc[:, 4 * j:4 * j + 1]
                s = sc[:, 4 * j + 1:4 * j + 2]
                i = sc[:, 4 * j + 2:4 * j + 3]
                m = red(v, w.rearrange("p k n -> p (k n)"), ALU.add, a_w, f, apply_absolute_value=True)
                b = R.take()
                m = mm(b.ap[:, 0:1], onesf[:, :], v, True, True, m, b.free, m_one)
                m = ts(i, b.ap[:, 0:1], 1.0 / n, 1e-5, ALU.mult, ALU.max, m)
                b.free = m
                m = recip(s, i, m)
                iws.append(i)
                m = ts(w, w, s, MAGIC, ALU.mult, ALU.add, m)
                m = ts(w, w, MAGIC, 1.0, ALU.subtract, ALU.min, m)
                wr.append(ts(wq, w, -1.0, None, ALU.max, None, m))
            hs = Ring([r(1024) for _ in range(3)])
            hb = Ring([r(512, dt=BF16) for _ in range(2)])
            hT = Ring([r(512, dt=BF16, k=8, n=128) for _ in range(2)])
            xs = Ring([r(256) for _ in range(3)])
            xb = Ring([r(128, dt=BF16) for _ in range(2)])
            xT = Ring([r(128, dt=BF16, k=2, n=128) for _ in range(2)])
            ys = Ring([r(256) for _ in range(3)])
            scr = Ring([r(1024), r(1024)])
            stt = small[:, 128:128 + 16 * 16].rearrange("p (t s) -> p t s", t=16)
            Hr, Tr, Yr = ring_of(0, 1, 2, 3), ring_of(4, 5), ring_of(6, 7)

            def quant(t, src, srcm, n, base, dst, dstm, wi):
                c = [stt[:, t, base + k:base + k + 1] for k in range(6)]
                q = scr.take()
                m1 = act(q.ap[:, 0:n], src, ACT.Square, srcm, q.free, f, accum_out=c[0])
                q.free = m1
                m2 = red(c[1], src, ALU.max, srcm, f, apply_absolute_value=True)
                m3 = ts(c[0], c[0], 1.0 / n, 1e-5, ALU.mult, ALU.add, m1, q=PO)
                m3 = PO.do(lambda e: e.tensor_tensor(c[0], c[0], nhalf[:, 0:1], ALU.pow), m3, m_nh)
                m4 = ts(c[1], c[1], c[0], 1e-5, ALU.mult, ALU.max, m3, m2)
                m5 = recip(c[2], c[1], m4)
                m6 = ts(c[2], c[2], 127.0, None, ALU.mult, None, m5)
                m7 = ts(c[3], c[1], iws[wi], 1.0 / 127.0, ALU.mult, ALU.mult, m6)
                m8 = ts(src, src, c[0], c[2], ALU.mult, ALU.mult, m7, m1)
                m8 = ts(src, src, MAGIC, None, ALU.add, None, m8)
                m9 = ts(dst, src, MAGIC, None, ALU.subtract, None, m8, dstm)
                return m9, c[3]

            S = {}
            rs_m = []
            for g in range(4):
                ms = [stats(mv[:, t, :], X[:, t, :], t, Xm[t]) for t in range(4 * g, 4 * g + 4)]
                rs_m.append(rstd(rs[:, 4 * g:4 * g + 4], mv[:, 4 * g:4 * g + 4, 1], 4, ms, f))

            def s1(t):
                x = xs.take()
                m = ts(x.ap, X[:, t, :], mv[:, t, 0:1], rs[:, t:t + 1], ALU.subtract, ALU.mult, rs_m[t // 4], x.free, Xm[t])
                d = xb.take()
                m, sx = quant(t, x.ap, m, 256, 0, d.ap, d.free, 0)
                x.free = m
                T = Tr.take()
                tv = T.ap.bitcast(BF16)
                for k in range(2):
                    m = tr(tv[:, k * 128:(k + 1) * 128], d.ap[:, k * 128:(k + 1) * 128], identb[:, :], m, T.free, m_id)
                d.free = m
                xt = xT.take()
                m = cp(xt.ap, tv[:, 0:256].rearrange("p (k n) -> p k n", k=2), m, xt.free, f)
                T.free = m
                h = hs.take()
                ms = []
                for q in range(2):
                    b = Hr.take()
                    for k in range(2):
                        mp = mm(b.ap, xt.ap[:, k, :], wq1[:, k, q * 512:(q + 1) * 512], k == 0, k == 1, m, wr, b.free)
                    fb = row("fb1")[:, q * 512:(q + 1) * 512]
                    m1 = DV.do(lambda e, b=b, q=q, fb=fb: e.scalar_tensor_tensor(
                        out=h.ap[:, q * 512:(q + 1) * 512], in0=b.ap, scalar=sx, in1=fb, op0=ALU.mult, op1=ALU.add),
                        mp, h.free, a_rows, f)
                    b.free = m1
                    ms.append(m1)
                xt.free = mp
                m = act(h.ap, h.ap, ACT.Gelu, ms)
                S[t] = (h, m)

            def s2(t):
                h, m = S[t]
                d = hb.take()
                m, sx = quant(t, h.ap, m, 1024, 8, d.ap, d.free, 1)
                h.free = m
                T = Tr.take()
                tv = T.ap.bitcast(BF16)
                for k in range(8):
                    m = tr(tv[:, k * 128:(k + 1) * 128], d.ap[:, k * 128:(k + 1) * 128], identb[:, :], m, T.free)
                d.free = m
                xt = hT.take()
                m = cp(xt.ap, tv.rearrange("p (k n) -> p k n", k=8), m, xt.free, f)
                T.free = m
                b = Yr.take()
                for k in range(8):
                    mp = mm(b.ap[:, 0:256], xt.ap[:, k, :], wq2[:, k, :], k == 0, k == 7, m, wr, b.free)
                xt.free = mp
                y = ys.take()
                m = DV.do(lambda e: e.scalar_tensor_tensor(out=y.ap, in0=b.ap[:, 0:256], scalar=sx, in1=row("fb2"),
                                                           op0=ALU.mult, op1=ALU.add), mp, y.free, a_rows, f)
                b.free = m
                m = tt(X[:, t, :], X[:, t, :], y.ap, ALU.add, m, Xm[t])
                y.free = m
                Xm[t] = m

            for t in range(17):
                if t < 16:
                    s1(t)
                if t > 0:
                    s2(t - 1)

        def weights(name, views, *after):
            return load(name, views, *after)

        if STAGES >= 1:
            layer0_attention()
            e0 = PE.last
            wt = region(WA)
            W1 = (wt(1024, k=2, n=512), wt(1024, k=2, n=512), wt(1024, k=2, n=512), wt(1024, k=4, n=256))
            WI, WO = wt(2048, f=8, n=256), wt(2048, f=8, n=256)
            e0 = [e0, cleared0, cleared2]
        if STAGES >= 3:
            a_w1 = load("w1", [(W1[0], wview(io["L1Wq"])), (W1[1], wview(io["L1Wkv"])[:, :, 0:512]),
                               (W1[2], wview(io["L1Wkv"])[:, :, 512:1024]), (W1[3], wview(io["L1Wo"]))], e0)
        if STAGES >= 4:
            a_wf1 = load("wf1", [(WI, wview(io["L1WinT"])), (WO, wview(io["L1Wout"]))], e0)
        if STAGES >= 2:
            layer0_ffn()
            e1 = PE.last
        if STAGES >= 5:
            wt = region(WB)
            W2 = (wt(1024, k=2, n=512), wt(1024, k=2, n=512), wt(1024, k=2, n=512), wt(1024, k=4, n=256))
            a_w2 = load("w2", [(W2[0], wview(io["L2Wq"])), (W2[1], wview(io["L2Wk"])),
                               (W2[2], wview(io["L2Wv"])), (W2[3], wview(io["L2Wout"]))], e1)
        if STAGES >= 3:
            perceiver(1, W1, a_w1, "lxw", "lxb", "llw", "llb")
        if STAGES >= 4:
            layer1_ffn(WI, WO, a_wf1)
            e3 = PE.last
        if STAGES >= 7:
            wt = region(WA)
            W3 = [wt(512, k=2, n=256) for _ in range(4)]
            F1, F2 = wt(2048, k=2, n=1024), wt(2048, k=8, n=256)
            a_w3 = load("w3", [(W3[0], wview(io["L3wqT"])), (W3[1], wview(io["L3wkT"])),
                               (W3[2], wview(io["L3wvT"])), (W3[3], wview(io["L3woT"]))], e3)
            a_f3 = load("f3", [(F1, wview(io["L3w1T"])), (F2, wview(io["L3w2T"]))], e3)
        if STAGES >= 5:
            perceiver(2, W2, a_w2, "mw", "mb", "zw", "zb")
        if STAGES >= 6:
            layer2_ffn()
        if STAGES >= 7:
            layer3_attention(*W3, a_w3)
        if STAGES >= 8:
            layer3_ffn(F1, F2, a_f3)
        s_out = sem("s_out")
        ov = out.rearrange("(t p) d -> p t d", p=128)
        for g in range(4):
            SP.dma(s_out, lambda e, g=g: e.dma_start(ov[:, 4 * g:4 * g + 4, :], X[:, 4 * g:4 * g + 4, :]),
                   Xm[4 * g:4 * g + 4])
        SP.wait(Arrival(s_out, 64))

        for q in (PE, DV, AC, PO, SP):
            q.count()
        block = ctx.enter_context(nc.Block())

        @block.tensor
        def _(eng):
            PE.emit(eng)

        @block.vector
        def _(eng):
            DV.emit(eng)

        @block.scalar
        def _(eng):
            AC.emit(eng)

        @block.gpsimd
        def _(eng):
            PO.emit(eng)

        @block.sync
        def _(eng):
            SP.emit(eng)


def _constants():
    c = np.zeros((128, 944), np.float32)
    c[:, 0:128] = np.eye(128, dtype=np.float32)
    q = np.arange(128)[:, None]
    k = np.arange(256)[None, :]
    c[:, 128:384] = np.where(k > q, -25.0, 0.0)
    c[:, 384:640] = np.where(k > q + 128, -25.0, 0.0)
    i = np.arange(128)
    c[:, 640:768] = np.where(i[:, None] < i[None, :], 1.0, 0.0)
    c[:, 896:944] = np.arange(48)[None, :]
    c[:, 768:896] = np.where(i[:, None] // 16 == i[None, :] // 16, 0.25, 0.0)
    return c


def kernel(**inputs):
    import concourse.bacc as bacc
    from concourse.bass_utils import run_bass_kernel_spmd as run
    a = {k: np.asarray(v) for k, v in inputs.items()}

    def pc(v):
        return v.reshape(-1, 128).T

    def pack(w1, w2, b1):
        w1, w2, b1 = a[w1], a[w2], a[b1]
        return np.concatenate([w1.reshape(8, 2, 128, -1).transpose(0, 2, 1, 3).reshape(8, 128, -1),
                               w2.reshape(8, -1, 128, 256).transpose(0, 2, 1, 3).reshape(8, 128, -1),
                               b1.reshape(8, -1, 128).transpose(0, 2, 1)], axis=2)

    def pad_heads(w):
        z = np.zeros((256, 16, 32), np.float32)
        z[:, :, 0:16] = w.T.reshape(256, 16, 16)
        return z.reshape(256, 512)

    cols = np.concatenate([
        pc(a["L1_xattn_ln_x_w"]), pc(a["L1_xattn_ln_x_b"]), pc(a["L1_xattn_ln_l_w"]), pc(a["L1_xattn_ln_l_b"]),
        pc(np.tile(a["L1_xattn_k_scale"], 2)), pc(np.tile(a["L1_xattn_q_scale"], 2)),
        pc(a["L2_xattn_ln_media_w"]), pc(a["L2_xattn_ln_media_b"]), pc(a["L2_xattn_ln_lat_w"]), pc(a["L2_xattn_ln_lat_b"]),
        pc(a["L1_ffn_b_in"]), pc(a["L3_xattn_wq_b"])], axis=1)
    rows = np.concatenate([
        a["L1_xattn_ln_o_w"], a["L1_xattn_ln_o_b"], a["L1_ffn_b_out"], a["L3_xattn_wk_b"], a["L3_xattn_wv_b"],
        a["L3_xattn_wo_b"], a["L3_xattn_ln_g"], a["L3_xattn_ln_b"], a["L3_ffn_b1"], a["L3_ffn_b2"], a["L2_ffn_bg"]])[None, :]
    data = {
        "x": a["x"].reshape(2048, 256), "ctx": a["ctx_1024"].reshape(2048, 256),
        "mask1": a["mask_BxS2_bk0"].reshape(1, 2048),
        "mask0": a["mask_Bx1xSxS2_bf0"].reshape(2048, 256),
        "cols": cols, "rows": rows, "consts": _constants(),
        "L0wqT": pad_heads(a["L0_xattn_Wq"]), "L0wkT": pad_heads(a["L0_xattn_Wk"]),
        "L0wvT": a["L0_xattn_Wv"].T, "L0woT": a["L0_xattn_Wo"].T,
        "L0gate": a["L0_ffn_gate_w"], "L0pack": pack("L0_ffn_w1", "L0_ffn_w2", "L0_ffn_b1"), "L0b2": a["L0_ffn_b2"],
        "L1Wq": a["L1_xattn_Wq"], "L1Wkv": a["L1_xattn_Wkv"], "L1Wo": a["L1_xattn_Wo"],
        "L1WinT": a["L1_ffn_W_in"].T, "L1Wout": a["L1_ffn_W_out"],
        "L2Wq": a["L2_xattn_Wq"], "L2Wk": a["L2_xattn_Wk"], "L2Wv": a["L2_xattn_Wv"], "L2Wout": a["L2_xattn_Wout"],
        "L2Wg": a["L2_ffn_Wg"], "L2pack": pack("L2_ffn_W1", "L2_ffn_W2", "L2_ffn_b1"), "L2b2": a["L2_ffn_b2"],
        "L3wqT": a["L3_xattn_wq_w"].T, "L3wkT": a["L3_xattn_wk_w"].T, "L3wvT": a["L3_xattn_wv_w"].T,
        "L3woT": a["L3_xattn_wo_w"].T, "L3w1T": a["L3_ffn_w1"].T, "L3w2T": a["L3_ffn_w2"].T,
    }
    nc = bacc.Bacc("TRN2", target_bir_lowering=False, num_devices=1)
    arrays, io = {}, {}
    for name, v in data.items():
        v = np.ascontiguousarray(v)
        arrays["in_" + name] = v
        io[name] = nc.dram_tensor("in_" + name, v.shape, mybir.dt.from_np(v.dtype), kind="ExternalInput").ap()
    out = nc.dram_tensor("out_0", (2048, 256), F32, kind="ExternalOutput").ap()
    build(nc, io, out)
    r = run(nc, [arrays], core_ids=[0])
    return r.results[0]["out_0"].reshape(8, 256, 256)
```

```python
import numpy as np
import concourse.bass as bass
import concourse.mybir as mybir
from contextlib import ExitStack

ACT = mybir.ActivationFunctionType
ALU = mybir.AluOpType
AX = mybir.AxisListType
F32 = mybir.dt.float32
F32R = mybir.dt.float32r
BF16 = mybir.dt.bfloat16
U8 = mybir.dt.uint8

MAGIC = 12582912.0
BIG = float(2.0 ** 123)

COLS = {}
ROWS = {}


def _lay_cols():
    o = 0
    for name, n in (("lxw", 2), ("lxb", 2), ("llw", 2), ("llb", 2), ("ks", 1), ("qs", 1),
                    ("mw", 2), ("mb", 2), ("zw", 2), ("zb", 2), ("bin", 8), ("bq", 2)):
        COLS[name] = (o, n)
        o += n
    return o


def _lay_rows():
    o = 0
    for name, n in (("low", 256), ("lob", 256), ("bout", 256), ("bk", 256), ("bv", 256), ("bo", 256),
                    ("lng", 256), ("lnb", 256), ("fb1", 1024), ("fb2", 256), ("bg", 8)):
        ROWS[name] = (o, n)
        o += n
    return o


NCOL = _lay_cols()
NROW = _lay_rows()


class Mark:

    def __init__(self, queue):
        self.queue, self.used, self.value = queue, False, 0


class Arrival:

    def __init__(self, sem, value):
        self.sem, self.value = sem, value


def flat(after):
    for a in after:
        if a is None:
            continue
        if isinstance(a, (list, tuple)):
            yield from flat(a)
        else:
            yield a


class Queue:

    def __init__(self, sem):
        self.sem, self.items, self.last = sem, [], None

    def do(self, fn, *after):
        after = list(flat(after))
        for a in after:
            if isinstance(a, Mark):
                a.used = True
        m = Mark(self)
        self.items.append((fn, after, m, None))
        self.last = m
        return m

    def dma(self, sem, fn, *after):
        after = list(flat(after))
        for a in after:
            if isinstance(a, Mark):
                a.used = True
        self.items.append((fn, after, None, sem))

    def wait(self, *after):
        after = list(flat(after))
        for a in after:
            if isinstance(a, Mark):
                a.used = True
        self.items.append((None, after, None, None))

    def count(self):
        n = 0
        for _, _, m, _ in self.items:
            if m is not None and m.used:
                n += 1
                m.value = n

    def emit(self, eng):
        seen = {}
        for fn, after, m, dsem in self.items:
            for a in after:
                sem = a.queue.sem if isinstance(a, Mark) else a.sem
                if seen.get(id(sem), 0) < a.value:
                    eng.wait_ge(sem, a.value)
                    seen[id(sem)] = a.value
            if fn is None:
                continue
            ins = fn(eng)
            if dsem is not None:
                ins.then_inc(dsem, 16)
            elif m.used:
                ins.then_inc(self.sem, 1)


class Slot:
    def __init__(self, ap):
        self.ap, self.free = ap, None


class Ring:
    def __init__(self, aps):
        self.slots, self.i = [Slot(a) for a in aps], 0

    def take(self):
        s = self.slots[self.i % len(self.slots)]
        self.i += 1
        return s


def build(nc, io, out):
    ctx = ExitStack()
    with ctx:
        def sb(name, shape, dt=F32):
            return ctx.enter_context(nc.sbuf_tensor(name, shape, dt))

        def sem(name):
            return ctx.enter_context(nc.semaphore(name))

        X = sb("X", [128, 16, 256])
        ctxT = sb("ctxT", [128, 2, 2048])
        HT = sb("HT", [128, 2, 2048])
        WA = sb("WA", [128, 8192])
        WB = sb("WB", [128, 8208])
        cols = sb("cols", [128, NCOL])
        rows = sb("rows", [128, NROW])
        ident = sb("ident", [128, 128])
        identb = sb("identb", [128, 128], BF16)
        identr = sb("identr", [128, 128], F32R)
        diagb = sb("diagb", [128, 128], BF16)
        causb = sb("causb", [128, 2, 256], BF16)
        blk = sb("blk", [128, 128])
        onesf = sb("onesf", [128, 128])
        onesb = sb("onesb", [1, 128], BF16)
        onesbb = sb("onesbb", [128, 128], BF16)
        trib = sb("trib", [128, 128], BF16)
        iota = sb("iota", [128, 48])
        rev = sb("rev", [128, 8])
        nhalf = sb("nhalf", [128, 16])
        st = sb("st", [128, 8, 6])
        mv = sb("mv", [128, 16, 2])
        mv2 = sb("mv2", [128, 16, 2])
        cmv = sb("cmv", [128, 16, 2])
        crs = sb("crs", [128, 16])
        rs = sb("rs", [128, 16])
        small = sb("small", [128, 704])
        banks = [ctx.enter_context(nc.psum_tensor(f"bank{i}", [128, 512], F32)) for i in range(8)]
        bank_slots = [Slot(b[:, :]) for b in banks]

        def ring_of(*ids):
            r = Ring([])
            r.slots = [bank_slots[i] for i in ids]
            return r

        PE, DV, AC, PO, SP = (Queue(sem(f"s_{n}")) for n in ("pe", "dv", "ac", "po", "sp"))

        def load(name, pairs, *after, q=None):
            s = sem(f"d_{name}")
            for o, i in pairs:
                (q or SP).dma(s, lambda e, o=o, i=i: e.dma_start(o, i), *after)
            return Arrival(s, 16 * len(pairs))

        def col(name, j=0):
            o, _ = COLS[name]
            return cols[:, o + j:o + j + 1]

        def row(name):
            o, n = ROWS[name]
            return rows[:, o:o + n]

        def region(base, own=F32):
            state = [0]

            def take(words, dt=own, **dims):
                v = base[:, state[0]:state[0] + words]
                state[0] += words
                assert state[0] <= base.shape[1], (state[0], base.shape)
                if dt is not own:
                    v = v.bitcast(dt)
                if dims:
                    names = list(dims)
                    v = v.rearrange("p (" + " ".join(names) + ") -> p " + " ".join(names),
                                    **{k: dims[k] for k in names[1:]})
                return v
            return take

        def mm(o, l, r, start, stop, *after):
            return PE.do(lambda e: e.matmul(o, l, r, start=start, stop=stop), *after)

        def tr(o, i, idn, *after):
            return PE.do(lambda e: e.transpose(o, i, idn), *after)

        def tt(o, a, b, op, *after, q=None):
            return (q or DV).do(lambda e: e.tensor_tensor(o, a, b, op), *after)

        def ts(o, a, s1, s2, op0, op1, *after, q=None):
            if op1 is None:
                return (q or DV).do(lambda e: e.tensor_scalar(o, a, s1, None, op0), *after)
            return (q or DV).do(lambda e: e.tensor_scalar(o, a, s1, s2, op0, op1), *after)

        def recip(o, a, *after):
            return DV.do(lambda e: e.reciprocal(o, a), *after)

        def cp(o, a, *after, q=None):
            return (q or DV).do(lambda e: e.tensor_copy(o, a), *after)

        def act(o, a, f, *after, **kw):
            return AC.do(lambda e: e.activation(o, a, f, **kw), *after)

        def red(o, a, op, *after, **kw):
            return DV.do(lambda e: e.tensor_reduce(o, a, AX.X, op, **kw), *after)

        a_cst = load("cst", [(ident[:, :], io["consts"][:, 0:128]), 
                             (small[:, 0:640], io["consts"][:, 128:768]), (iota[:, :], io["consts"][:, 896:944]),
                             (blk[:, :], io["consts"][:, 768:896]), (cols[:, :], io["cols"])])
        scope = [None]

        def arena(name, words, dt=F32):
            if scope[0] is None:
                scope[0] = ExitStack()
            return scope[0].enter_context(nc.sbuf_tensor(name, [128, words], dt))

        def leave():
            scope[0].close()
            scope[0] = None

        ctx0 = WB[:, 0:4096].rearrange("p (t d) -> p t d", t=16)
        a_ctx = load("ctx", [(ctx0, io["ctx"].rearrange("(t p) d -> p t d", p=128))], q=AC)
        a_x = load("x", [(X[:, :, :], io["x"].rearrange("(t p) d -> p t d", p=128))])

        sorted_h0, sorted_y0, sorted_h2, sorted_y2 = (
            nc.dram_tensor(n, (k * 128, 256), F32, kind="Internal").ap()
            for n, k in (("sorted_h0", 23), ("sorted_y0", 23), ("sorted_h2", 39), ("sorted_y2", 39)))

        def clear(dram, n, name, *after):
            s = sem("d_" + name)
            for i in range(n):
                PO.dma(s, lambda e, i=i: e.dma_start(dram[i * 1024:min((i + 1) * 1024, dram.shape[0]), :].rearrange(
                    "(k p) n -> p k n", p=128),
                    zero[:, 0:(min((i + 1) * 1024, dram.shape[0]) - i * 1024) * 2].rearrange("p (k n) -> p k n", n=256)), *after)
            return Arrival(s, 16 * n)

        zero = WA[:, 4096:6144]
        m_zero = PO.do(lambda e: e.memset(zero, 0.0))
        cleared0 = clear(sorted_h0, 3, "z0", m_zero)
        cleared2 = clear(sorted_h2, 5, "z2", m_zero)

        def wview(dram):
            return dram.rearrange("(k p) n -> p k n", p=128)

        wt = region(WA)
        wq0, wk0 = wt(512, k=2, n=256), wt(512, k=2, n=256)
        wv0, wo0 = wt(512, k=2, n=256), wt(1024, k=4, n=256)
        a_w0 = load("w0", [(wq0, wview(io["L0wqT"])), (wk0, wview(io["L0wkT"])),
                           (wv0, wview(io["L0wvT"])), (wo0, wview(io["L0woT"]))])
        a_rows = load("rows", [(rows[:, :], io["rows"].to_broadcast([128, NROW]))])

        m_id = [cp(identb[:, :], ident[:, :], a_cst),
                ts(diagb[:, :], ident[:, :], 4000.0, None, ALU.mult, None, a_cst),
                cp(causb[:, :, :], small[:, 0:512].rearrange("p (a b) -> p a b", a=2), a_cst)]
        m_id.append(cp(identr[:, :], ident[:, :], a_cst))
        m_id.append(cp(trib[:, :], small[:, 512:640], a_cst))
        m_rev = ts(rev[:, :], iota[:, 0:8], -1.0, 8.0, ALU.mult, ALU.add, a_cst)
        DV.do(lambda e: e.memset(onesbb[:, :], 1.0))
        m_one = DV.do(lambda e: e.memset(onesf[:, :], 1.0))
        m_oneb = DV.do(lambda e: e.memset(onesb[:, :], 1.0))
        m_nh = DV.do(lambda e: e.memset(nhalf[:, :], -0.5))

        def rstd(dst, var, n, *after, eps=1e-5, op=ALU.add):
            m = ts(dst, var, eps, None, op, None, *after, q=PO)
            return PO.do(lambda e: e.tensor_tensor(dst, dst, nhalf[:, 0:n], ALU.pow), m, m_nh)

        def stats(dst, src, t, *after):
            m = DV.do(lambda e: e.bn_stats(st[:, t % 8, :], src), *after)
            return DV.do(lambda e: e.bn_aggr(dst, st[:, t % 8, :]), m)

        Xm = [a_x] * 16

        known = {}

        def stats_ahead(t):
            known[t] = stats(mv[:, t, :], X[:, t, :], t, Xm[t])

        def norm_T(src, srcm, keep, dst, mvt, ring, evac, *after, second=None, hook=None):
            done = [None] * 16
            tok = [None] * 16
            hs = [None] * 16
            r1, r2 = {}, {}

            def stat(g, dst, source):
                T = range(4 * g, 4 * g + 4)
                if dst is mv and all(t in known for t in T):
                    ms = [known.pop(t) for t in T]
                else:
                    ms = []
                    for t in T:
                        i, k, *dep = source(t)
                        ms.append(DV.do(lambda e, i=i, k=k: e.bn_stats(st[:, k % 8, :], i), dep))
                    ms = [DV.do(lambda e, t=t: e.bn_aggr(dst[:, t, :], st[:, t % 8, :]), m) for t, m in zip(T, ms)]
                return rstd(rs[:, 4 * g:4 * g + 4], dst[:, 4 * g:4 * g + 4, 1], 4, ms[-1], tok[4 * g:4 * g + 4])

            def normalise(g):
                for t in range(4 * g, 4 * g + 4):
                    s = keep.take()
                    tok[t] = ts(s.ap, src[:, t, :], mvt[:, t, 0:1], rs[:, t:t + 1], ALU.subtract, ALU.mult, r1[g], s.free,
                                q=DV)
                    hs[t] = s

            def again(g):
                for t in range(4 * g, 4 * g + 4):
                    tok[t] = ts(hs[t].ap, hs[t].ap, mv2[:, t, 0:1], rs[:, t:t + 1], ALU.subtract, ALU.mult, r2[g])

            def turn(g):
                if hook:
                    for t in range(4 * g, 4 * g + 4):
                        hook(t, hs[t], tok[t])
                for c in range(2):
                    b = ring.take()
                    for j in range(4):
                        s = hs[4 * g + j]
                        m = tr(b.ap[:, j * 128:(j + 1) * 128], s.ap[:, c * 128:(c + 1) * 128], ident[:, :],
                               tok[4 * g + j], b.free, a_cst)
                        if c == 1:
                            s.free = [s.free, m] if hook else m
                    m = evac(dst[:, c, g * 512:(g + 1) * 512], b.ap, c, m)
                    b.free = m
                    for t in range(4 * g, 4 * g + 4):
                        done[t] = [done[t], m]

            for i in range(6):
                if i < 4:
                    r1[i] = stat(i, mvt, lambda t: (src[:, t, :], t, srcm[t], after))
                if 0 <= i - 2 < 4 and second is not None:
                    again(i - 2)
                    turn(i - 2)
                if 0 <= i - 1 < 4:
                    normalise(i - 1)
                    if second is None:
                        turn(i - 1)
                    else:
                        r2[i - 1] = stat(i - 1, mv2, lambda t: (hs[t].ap, t, tok[t]))
            return done, tok

        def evac_copy(o, i, c, *after):
            return (act(o, i, ACT.Copy, *after) if c == 0 else cp(o, i, *after))

        def evac_affine(w, b):
            def f(o, i, c, *after):
                return act(o, i, ACT.Identity, *after, a_cst, scale=col(w, c), bias=col(b, c)) if c == 0 else \
                    ts(o, i, col(w, c), col(b, c), ALU.mult, ALU.add, *after, a_cst)
            return f

        def tiles_ring(buf, n):
            return Ring([buf[:, i, :] for i in range(n)])

        pre = ring_of(0, 1, 2, 3)
        ctx_m = [None] * 16
        for g in range(4):
            for c in range(2):
                b = pre.take()
                for j in range(4):
                    m = tr(b.ap[:, j * 128:(j + 1) * 128], ctx0[:, 4 * g + j, c * 128:(c + 1) * 128], ident[:, :],
                           a_ctx, a_cst, b.free)
                m = evac_copy(ctxT[:, c, g * 512:(g + 1) * 512], b.ap, c, m)
                b.free = m
                for t in range(4 * g, 4 * g + 4):
                    ctx_m[t] = [ctx_m[t], m]
        m_cs = [stats(cmv[:, t, :], ctx0[:, t, :], t, a_ctx) for t in range(16)]
        m_crs = rstd(crs[:, :], cmv[:, :, 1], 16, m_cs)

        def residual(t, src, *after, ahead=True):
            m = Xm[t] = tt(X[:, t, :], src, X[:, t, :], ALU.add, *after, Xm[t])
            if ahead:
                stats_ahead(t)
            return m

        def turns(gens, starts=(0,)):
            left, i = list(zip(starts, gens)), 0
            while left:
                left = [(s, g) for s, g in left if s > i or next(g, left) is not left]
                i += 1

        def spread(hooks, plan):
            for i, (n, make) in plan.items():
                cell = []

                def first(cell=cell, make=make):
                    cell.append(make())
                    next(cell[0], None)
                hooks.setdefault(i, []).append(first)
                for j in range(1, n):
                    hooks.setdefault(i + 0.5 * j, []).append(lambda cell=cell: next(cell[0], None))

        def attention(n, nsub, scores, pv, hooks, Pr, PTr, mx, sums, inv, Sr, Tr):
            info = [dict() for _ in range(n)]
            w = 512 // nsub
            for i in range(n + 4):
                for h in hooks.get(i, ()):
                    h()
                if 0 <= i - 3 < n:
                    u = info[i - 3]
                    u["T"] = Tr.take()
                    for j in range(4):
                        o = (2 * (j % 2) + j // 2) if nsub == 2 else j
                        m = tr(u["T"].ap[:, o * 128:(o + 1) * 128], u["P"].ap[:, j * 128:(j + 1) * 128], ident[:, :],
                               u["nm"], u["T"].free)
                    u["P"].free = m
                    if nsub == 2:
                        q = u["PT"] = PTr.take()
                        u["pt"] = act(q.ap, u["T"].ap, ACT.Copy, m, q.free)
                    else:
                        a = (i - 3) % 2
                        q = u["PT"] = info[i - 4]["PT"] if a else PTr.take()
                        m = act(q.ap.rearrange("p (k n) -> p k n", k=4)[:, :, a * 128:(a + 1) * 128],
                                u["T"].ap.rearrange("p (k n) -> p k n", k=4), ACT.Copy, m, q.free)
                        u["pt"] = [m, info[i - 4]["pt"]] if a else m
                    u["T"].free = m if nsub == 1 else u["pt"]
                if i < n:
                    u = info[i]
                    u["S"] = Sr.take()
                    u["ms"] = scores(i, u["S"])
                    k = (i % 4) * nsub
                    u["mx"] = red(mx[:, k:k + nsub], u["S"].ap.rearrange("p (a b) -> p a b", a=nsub), ALU.max,
                                  u["ms"], info[i - 4]["exp"] if i >= 4 else None, negate=True)
                    p = u["P"] = Pr.take()
                    for j in range(nsub):
                        m = act(p.ap[:, j * w:(j + 1) * w], u["S"].ap[:, j * w:(j + 1) * w], ACT.Exp,
                                u["mx"], p.free, info[i - 4]["rc"] if i >= 4 else None,
                                bias=mx[:, k + j:k + j + 1], accum_out=sums[:, k + j:k + j + 1])
                    u["exp"] = m
                    u["S"].free = m
                if 0 <= i - 1 < n:
                    u = info[i - 1]
                    k = ((i - 1) % 4) * nsub
                    u["rc"] = recip(inv[:, k:k + nsub], sums[:, k:k + nsub], u["exp"], info[i - 5]["nm"] if i >= 5 else None)
                    u["nm"] = []
                    for j in range(nsub):
                        v = u["P"].ap[:, j * w:(j + 1) * w]
                        u["nm"].append(ts(v, v, inv[:, k + j:k + j + 1], None, ALU.mult, None, u["rc"], u["exp"]))
                if 0 <= i - 4 < n and (nsub == 2 or (i - 4) % 2 == 1):
                    u = info[i - 4]
                    u["PT"].free = pv(i - 4, u["PT"].ap, u["pt"])
                for h in hooks.get(i + 0.5, ()):
                    h()

        def layer0_attention():
            RR = region(arena("l0r", 10240, F32R), F32R)
            r2 = region(arena("l0f", 4096))
            f = [PE.last, DV.last, AC.last]
            DV.wait(f)
            AC.wait(f)
            r = region(WB)
            keep = tiles_ring(r(2048, t=8, d=256), 8)
            QS = [RR(2048, c=8, n=256) for _ in range(2)]
            KS = [RR(2048, c=8, n=256) for _ in range(2)]
            V = [r2(1024, t=2, h=16, d=32) for _ in range(2)]
            m_v = [DV.do(lambda e, v=v: e.memset(v[:, :, :, 16:32], 0.0)) for v in V]
            PTr = Ring([r(512) for _ in range(3)])
            tmp = Ring([RR(1024, h=16, w=4, d=16) for _ in range(2)])
            Pr = Ring([r(512) for _ in range(4)])
            OTs = [r2(1024, c=4, n=256) for _ in range(2)]
            sm, rc, mx = small[:, 512:520], small[:, 520:528], small[:, 528:536]
            Sr, Tr, Or, Mr = ring_of(0, 1), ring_of(2, 3), ring_of(4, 5), ring_of(6, 7)
            hm, _ = norm_T(X, Xm, keep, HT, mv, pre, evac_copy)
            proj = {}
            ready = {}

            def project(b):
                s, lo = b % 2, b * 256
                free = proj.get(b - 2)
                done = ready[b] = []
                pieces = []

                def split(src, q, scale):
                    t = tmp.take()
                    i = src.rearrange("p (h o d) -> p h o d", h=16, o=1).to_broadcast([128, 16, 2, 16])
                    hi = t.ap[:, :, 0:2, :] if q else t.ap[:, :, 0:4:2, :]
                    lw = t.ap[:, :, 2:4, :] if q else t.ap[:, :, 1:4:2, :]
                    return t, i, hi, lw

                def keys(t):
                    def first():
                        bk = Mr.take()
                        at = slice(lo + t * 128, lo + t * 128 + 128)
                        for j, W in enumerate((wk0, wv0)):
                            for k in range(2):
                                m = mm(bk.ap[:, j * 256:(j + 1) * 256], ctxT[:, k, at], W[:, k, :], k == 0, k == 1,
                                       ctx_m[2 * b + t], a_w0, bk.free)
                        z, i, hi, lw = split(bk.ap[:, 0:256], False, None)
                        m1 = act(hi, i, ACT.Copy, m, z.free)
                        m3 = act(V[s][:, t, :, 0:16], bk.ap[:, 256:512].rearrange("p (h d) -> p h d", h=16), ACT.Copy, m, free, m_v)
                        m2 = tt(lw, i, hi.bitcast(F32), ALU.subtract, m1, m3, z.free)
                        bk.free = m2
                        done.append(m3)
                        held[t] = (z, [m1, m2])
                    held = {}
                    pieces.append(first)
                    pieces.append(lambda: turn(*held[t], KS[s], t))

                def turn(z, ms, dst, t):
                    for q in range(2):
                        T = Tr.take()
                        for j in range(4):
                            c = 4 * q + j
                            m = tr(T.ap[:, j * 128:(j + 1) * 128].bitcast(F32R),
                                   z.ap[:, 2 * c:2 * c + 2, :, :].rearrange("p h w d -> p (h w d)"), identr[:, :], ms, T.free, m_id)
                        o = dst[:, 4 * q:4 * q + 4, t * 128:(t + 1) * 128]
                        i = T.ap.rearrange("p (c n) -> p c n", c=4)
                        m5 = act(o, i, ACT.Copy, m, free) if q else cp(o, i, m, free)
                        T.free = m5
                        done.append(m5)
                    z.free = m

                def queries(t):
                    def first():
                        bk = Mr.take()
                        at = slice(lo + t * 128, lo + t * 128 + 128)
                        for k in range(2):
                            m = mm(bk.ap[:, 0:256], HT[:, k, at], wq0[:, k, :], k == 0, k == 1, hm[2 * b + t], a_w0, bk.free)
                        z, i, hi, lw = split(bk.ap[:, 0:256], True, 0.0625)
                        m1 = act(hi, i, ACT.Copy, m, z.free, scale=0.0625)
                        q2 = qf[t % 2]
                        m2 = act(q2, bk.ap[:, 0:256], ACT.Copy, m, qfree.get(t % 2), scale=0.0625)
                        m3 = tt(lw, q2.rearrange("p (h o d) -> p h o d", h=16, o=1).to_broadcast([128, 16, 2, 16]),
                                hi.bitcast(F32), ALU.subtract, m1, m2, z.free)
                        qfree[t % 2] = m3
                        bk.free = m2
                        held[t] = (z, [m1, m3])
                    held = {}
                    pieces.append(first)
                    pieces.append(lambda: turn(*held[t], QS[s], t))

                for t in range(2):
                    keys(t)
                    queries(t)
                return pieces

            qf = [r(256) for _ in range(2)]
            qfree = {}

            def scores(i, S):
                b, h = divmod(i, 16)
                s, c, p = b % 2, h // 2, 64 * (h % 2)
                for a in range(2):
                    mm(S.ap[:, a * 256:(a + 1) * 256], QS[s][p:p + 64, c, a * 128:(a + 1) * 128],
                       KS[s][p:p + 64, c, :], True, False, ready[b], S.free)
                    m = mm(S.ap[:, a * 256:(a + 1) * 256], diagb[:, :], causb[:, a, :], False, True, m_id)
                return m

            O = {}
            ot = {}
            otfree = {}

            def pv(i, PT, *after):
                b, h = divmod(i, 16)
                if h % 8 == 0:
                    O[b] = Or.take()
                o = O[b].ap[32 * (h % 4):32 * (h % 4) + 32, (h % 8) // 4 * 256:(h % 8) // 4 * 256 + 256]
                for k in range(2):
                    m = mm(o, V[b % 2][:, k, h, :], PT[:, k * 256:(k + 1) * 256], k == 0, k == 1, after, O[b].free)
                if h % 8 == 7:
                    proj[b] = m
                    c = h // 8 * 2
                    mo = act(OTs[b % 2][:, c:c + 2, :], O[b].ap.rearrange("p (c n) -> p c n", c=2), ACT.Copy, m, otfree.get(b - 2))
                    O[b].free = mo
                    ot[b] = [ot.get(b), mo]
                return m

            def out_proj(b):
                bk = Mr.take()
                for a in range(2):
                    for c in range(4):
                        m = mm(bk.ap[:, a * 256:(a + 1) * 256], OTs[b % 2][:, c, a * 128:(a + 1) * 128], wo0[:, c, :],
                               c == 0, c == 3, ot[b], bk.free)
                otfree[b] = m
                for a in range(2):
                    bk.free = residual(2 * b + a, bk.ap[:, a * 256:(a + 1) * 256], m)

            for q in project(0):
                q()
            hooks = {}
            state = {}
            for b in range(7):
                for j in range(8):
                    def piece(b=b, j=j):
                        if j == 0:
                            state[b] = project(b + 1)
                        state[b][j]()
                    hooks[16 * b + 4 + (3 * j) // 2] = [piece]
            for b in range(7):
                hooks[16 * b + 22] = [lambda b=b: out_proj(b)]
            attention(128, 2, scores, pv, hooks, Pr, PTr, mx, sm, rc, Sr, Tr)
            out_proj(7)
            leave()

        def gates(w_sb, wready, temp, topk, hm, bias, r):
            L = r(128, t=16, e=8)
            G = r(128, t=16, e=8)
            E = r(128, t=16, e=8)
            M = r(128 * topk, c=topk, t=16, e=8)
            S = r(128 * topk, c=topk, t=16, e=8)
            gv = r(16 * topk, c=topk, t=16)
            m1 = r(16)
            d = r(16)
            bk = ring_of(7).take()
            for t in range(16):
                for k in range(2):
                    m = mm(bk.ap[:, t * 8:(t + 1) * 8], HT[:, k, t * 128:(t + 1) * 128], w_sb[:, k, :],
                           k == 0, k == 1, hm[t], bk.free, wready)
            lg = bk.ap[:, 0:128].rearrange("p (t e) -> p t e", e=8)

            def bc(v):
                return v.rearrange("p (t o) -> p t o", o=1).to_broadcast([128, 16, 8])

            revb = rev[:, :].rearrange("p (o e) -> p o e", o=1).to_broadcast([128, 16, 8])
            if bias is not None:
                m = tt(L, lg, bias.rearrange("p (o e) -> p o e", o=1).to_broadcast([128, 16, 8]), ALU.add, m, a_rows)
                bk.free = m
                m = ts(L, L, 1.0 / temp, None, ALU.mult, None, m)
            else:
                m = cp(L, lg, m)
                bk.free = m
            m = red(m1, L, ALU.max, m)
            m = tt(E, L, bc(m1), ALU.subtract, m)
            me = act(E, E, ACT.Exp, m)
            sel = []
            for c in range(topk):
                if c:
                    m = ts(S[:, 0, :, :], M[:, c - 1, :, :], -3.0e38, None, ALU.mult, None, m)
                    m = tt(L, L, S[:, 0, :, :], ALU.add, m)
                    m = red(m1, L, ALU.max, m)
                m = tt(M[:, c, :, :], L, bc(m1), ALU.is_equal, m)
                m = tt(M[:, c, :, :], M[:, c, :, :], revb, ALU.mult, m, m_rev)
                m = red(m1, M[:, c, :, :], ALU.max, m)
                m = tt(M[:, c, :, :], M[:, c, :, :], bc(m1), ALU.is_equal, m)
                sel.append(m)
            md = red(d, E, ALU.add, me)
            md = recip(d, d, md)
            md = tt(E, E, bc(d), ALU.mult, md)
            for c in range(topk):
                md = tt(S[:, c, :, :], E, M[:, c, :, :], ALU.mult, md, sel)
                md = red(gv[:, c, :], S[:, c, :, :], ALU.add, md)
            if topk == 2:
                m = tt(d, gv[:, 0, :], gv[:, 1, :], ALU.add, md)
                m = ts(d, d, 1e-9, None, ALU.add, None, m)
                m = recip(d, d, m)
                for c in range(2):
                    md = tt(gv[:, c, :], gv[:, c, :], d, ALU.mult, m)
                m = tt(S[:, 0, :, :], S[:, 0, :, :], S[:, 1, :, :], ALU.add, md)
                md2 = tt(G, S[:, 0, :, :], bc(d), ALU.mult, m)
            else:
                md2 = cp(G, S[:, 0, :, :], md)
            return G, M, gv, md2, [md2, md], sel

        def route(M, sel, topk, nt, r):
            n = 16 * topk
            selb = r(64 * topk, dt=BF16)
            I = [r(8 * n, t=n, e=8) for _ in range(2)]
            Mf = M.rearrange("p c t e -> p (c t) e")
            nb = [r(8) for _ in range(3)]
            pos = r(n, dt=mybir.dt.int32)
            ex = r(nt, dt=mybir.dt.int32)
            posf = r(n)
            cmpb = r(8 * nt, i=nt, e=8)
            exf = r(nt)
            bk = ring_of(7).take()
            m = cp(selb, Mf.rearrange("p t e -> p (t e)"), sel)
            mm(bk.ap[:, 0:8 * n], trib[:, :], selb, True, True, m, bk.free, m_id)
            m = mm(bk.ap[:, 256:256 + 8 * n], onesbb[:, :], selb, True, True, m_one)
            pre_v = bk.ap[:, 0:8 * n].rearrange("p (t e) -> p t e", e=8)
            tot = bk.ap[:, 256:256 + 8 * n].rearrange("p (t e) -> p t e", e=8)
            m = cp(I[0], tot, m)
            cur, st_ = 0, 1
            while st_ < n:
                o, i = I[1 - cur], I[cur]
                m1 = tt(o[:, st_:n, :], i[:, st_:n, :], i[:, 0:n - st_, :], ALU.add, m)
                m2 = cp(o[:, 0:st_, :], i[:, 0:st_, :], m)
                m = [m1, m2]
                cur, st_ = 1 - cur, st_ * 2
            inc, exc = I[cur], I[1 - cur]
            m = tt(exc, inc, tot, ALU.subtract, m)
            ma = tt(exc, exc, pre_v, ALU.add, m)
            bk.free = ma
            m = ts(nb[0], inc[:, n - 1, :], 63.5, 1.0 / 128, ALU.add, ALU.mult, m)
            m = ts(nb[0], nb[0], MAGIC, MAGIC, ALU.add, ALU.subtract, m)
            m = cp(nb[1], nb[0], m)
            cur, st_ = 1, 1
            while st_ < 8:
                o, i = nb[3 - cur], nb[cur]
                m1 = tt(o[:, st_:8], i[:, st_:8], i[:, 0:8 - st_], ALU.add, m)
                m2 = cp(o[:, 0:st_], i[:, 0:st_], m)
                m = [m1, m2]
                cur, st_ = 3 - cur, st_ * 2
            T = nb[cur]
            mt = m
            m = tt(nb[0], T, nb[0], ALU.subtract, mt)
            m = ts(nb[0], nb[0], 128.0, None, ALU.mult, None, m)
            m = tt(exc, exc, nb[0].rearrange("p (o e) -> p o e", o=1).to_broadcast([128, n, 8]), ALU.add, m, ma)
            m = tt(exc, exc, Mf, ALU.mult, m)
            m = red(posf, exc, ALU.add, m)
            m_pos = cp(pos, posf, m)
            m = tt(cmpb[0:1, :, :], T[0:1, :].rearrange("p (o e) -> p o e", o=1).to_broadcast([1, nt, 8]),
                   iota[0:1, 0:nt].rearrange("p (i o) -> p i o", o=1).to_broadcast([1, nt, 8]), ALU.is_le, mt, a_cst)
            m = red(exf[0:1, :], cmpb[0:1, :, :], ALU.add, m)
            m = ts(ex[0:1, :], exf[0:1, :], 7.0, None, ALU.min, None, m)
            return pos, ex, m_pos, m

        def experts(tag, ff, topk, nt, pack, b2d, gate_d, temp, bias, wbufs, sorted_h, sorted_y, cleared):
            f = fence()
            r = region(arena(tag + "a", 14336))
            Hn = r(4096, t=16, d=256)
            keep = tiles_ring(Hn, 16)
            for s in keep.slots:
                s.free = f
            gw = r(16, k=2, n=8)
            a_g = load(tag + "gw", [(gw, wview(gate_d))], f)
            hm, tok = norm_T(X, Xm, keep, HT, mv, pre, evac_copy)
            nf = ff // 128
            nw = 4 * ff + nf
            G, M, gv, gm, gvm, sel = gates(gw, a_g, temp, topk, hm, bias, r)
            pos, ex, m_pos, m_ex = route(M, sel, topk, nt, r)
            b2 = r(256)
            a_b2 = load(tag + "b2", [(b2[0:8, :], b2d)], f)
            xs = Ring([r(256) for _ in range(3)])
            xT = Ring([r(256, k=2, n=128) for _ in range(2)])
            gb = Ring([r(ff, f=nf, n=128) for _ in range(2)])
            ys = Ring([r(256) for _ in range(3)])
            wbufs = [w for w in wbufs(r)]
            wr = Ring(wbufs)
            for g in (xs, wr, ys):
                for i, s in enumerate(g.slots):
                    s.sem, s.n = sem(f"d_{tag}{'x' if g is xs else 'w' if g is wr else 'y'}{i}"), 0
            s_sc = sem(f"d_{tag}sc")
            for c in range(topk):
                for t in range(16):
                    i = c * 16 + t
                    PO.dma(s_sc, lambda e, i=i, t=t: e.indirect_dma_start(
                        out=sorted_h, out_offset=bass.IndirectOffsetOnAxis(ap=pos[:, i:i + 1], axis=0),
                        in_=Hn[:, t, :], in_offset=None), m_pos, tok[t], cleared)
            scattered = Arrival(s_sc, 256 * topk)

            def arrival(s):
                s.n += 16
                return Arrival(s.sem, s.n)

            regs = {}

            def load_w(i):
                s = wr.take()
                SP.wait(m_ex, f, s.free)

                def fn(e, i=i, s=s):
                    v = e.value_load(ex[0:1, i:i + 1], min_val=0, max_val=7)
                    return e.dma_start(s.ap[:, 0:nw].rearrange("p (o n) -> p o n", o=1),
                                       pack[bass.ds(v, 1), :, :].rearrange("o p n -> p o n"))
                SP.dma(s.sem, fn)
                return s, arrival(s)

            def load_x(i):
                s = xs.take()
                SP.dma(s.sem, lambda e: e.dma_start(s.ap, sorted_h[i * 128:(i + 1) * 128, :]), s.free, scattered, f)
                return s, arrival(s)

            GT = gb.slots[0].ap.rearrange("p f n -> p (f n)")
            Yr = ring_of(4, 5)
            for h in range(0, 16, nf):
                for t in range(h, h + nf):
                    if t % 4 == 0:
                        bk = ring_of(7).take()
                    m = tr(bk.ap[0:8, (t % 4) * 128:(t % 4 + 1) * 128], G[:, t, :], ident[:, :], gm, bk.free)
                    if t % 4 == 3:
                        gtm = cp(GT[0:8, (t - 3 - h) * 128:(t + 1 - h) * 128], bk.ap[0:8, :], m, gb.slots[0].free)
                        bk.free = gtm
                for t in range(h, h + nf, 2):
                    bk = Yr.take()
                    for a in range(2):
                        m = mm(bk.ap[:, a * 256:(a + 1) * 256], GT[0:8, (t + a - h) * 128:(t + a + 1 - h) * 128], b2[0:8, :],
                               True, True, gtm, a_b2, bk.free)
                    gb.slots[0].free = m
                    for a in range(2):
                        bk.free = residual(t + a, bk.ap[:, a * 256:(a + 1) * 256], m, ahead=False)

            Tr, Hr = ring_of(6, 7), ring_of(0, 1, 2, 3)
            lw, lx, xt, gt = {}, {}, {}, {}
            nwb = len(wbufs)
            for i in range(min(nwb, nt)):
                lw[i] = load_w(i)
            for i in range(3):
                lx[i] = load_x(i)

            def turn(i):
                s, a = lx[i]
                T = Tr.take()
                for k in range(2):
                    m = tr(T.ap[:, k * 128:(k + 1) * 128], s.ap[:, k * 128:(k + 1) * 128], ident[:, :], a, T.free)
                s.free = m
                o = xT.take()
                m = cp(o.ap, T.ap[:, 0:256].rearrange("p (k n) -> p k n", k=2), m, o.free)
                T.free = m
                xt[i] = (o, m)
                if i + 3 < nt:
                    lx[i + 3] = load_x(i + 3)

            def up(i):
                o, mx_ = xt[i]
                w, aw = lw[i]
                g = gb.take()
                ms = []
                for q in range(nf // 4):
                    bk = Hr.take()
                    for j in range(4):
                        ft = 4 * q + j
                        for k in range(2):
                            m = mm(bk.ap[:, j * 128:(j + 1) * 128], w.ap[:, k * ff + ft * 128:k * ff + ft * 128 + 128],
                                   o.ap[:, k, :], k == 0, k == 1, aw, mx_, bk.free)
                    for j in range(4):
                        ft = 4 * q + j
                        m2 = act(g.ap[:, ft, :], bk.ap[:, j * 128:(j + 1) * 128], ACT.Gelu, m, g.free,
                                 bias=w.ap[:, 4 * ff + ft:4 * ff + ft + 1])
                        ms.append(m2)
                    bk.free = m2
                o.free = m
                gt[i] = (g, ms)

            def down(i):
                g, ms = gt[i]
                w, aw = lw[i]
                bk = Yr.take()
                for k in range(nf):
                    m = mm(bk.ap[:, 0:256], g.ap[:, k, :], w.ap[:, 2 * ff + k * 256:2 * ff + (k + 1) * 256],
                           k == 0, k == nf - 1, ms[k], bk.free)
                g.free = w.free = m
                y = ys.take()
                m = cp(y.ap, bk.ap[:, 0:256], m, y.free)
                bk.free = m
                if i + nwb < nt:
                    lw[i + nwb] = load_w(i + nwb)
                SP.dma(y.sem, lambda e: e.dma_start(sorted_y[i * 128:(i + 1) * 128, :], y.ap), m)
                y.free = arrival(y)

            turn(0)
            up(0)
            turn(1)
            for i in range(nt):
                if i + 1 < nt:
                    up(i + 1)
                if i + 2 < nt:
                    turn(i + 2)
                down(i)
            stored = [y.free for y in ys.slots]
            back = keep
            for s in back.slots:
                s.free = scattered
            for i, s in enumerate(back.slots):
                s.sem, s.n = sem(f"d_{tag}g{i}"), 0
            for t in range(16):
                for c in range(topk):
                    i = c * 16 + t
                    s = back.take()
                    PO.dma(s.sem, lambda e, i=i, s=s: e.indirect_dma_start(
                        out=s.ap, out_offset=None, in_=sorted_y,
                        in_offset=bass.IndirectOffsetOnAxis(ap=pos[:, i:i + 1], axis=0)), stored, s.free)
                    a = arrival(s)
                    Xm[t] = DV.do(lambda q, t=t, s=s, g=gv[:, c, t:t + 1]: q.scalar_tensor_tensor(
                        out=X[:, t, :], in0=s.ap, scalar=g, in1=X[:, t, :], op0=ALU.mult, op1=ALU.add), a, Xm[t], gvm)
                    s.free = Xm[t]
                if t:
                    stats_ahead(t - 1)
            stats_ahead(15)
            leave()

        def fence():
            f = [PE.last, DV.last, AC.last, PO.last]
            for q in (DV, AC, PO):
                q.wait(f)
            return f

        def layer0_ffn():
            def wbufs(r):
                return [WB[:, 0:4104], WB[:, 4104:8208], r(4104)]
            experts("e0", 1024, 1, 23, io["L0pack"], io["L0b2"], io["L0gate"], 1.0, None, wbufs,
                    sorted_h0, sorted_y0, cleared0)

        def layer2_ffn():
            def wbufs(r):
                return [WB[:, i * 2052:(i + 1) * 2052] for i in range(4)]
            experts("e2", 512, 2, 39, io["L2pack"], io["L2b2"], io["L2Wg"], 5.0, row("bg"), wbufs,
                    sorted_h2, sorted_y2, cleared2)

        def perceiver(which, W, a_w, xw, xb, zw, zb):
            f = fence()
            RR = region(arena(f"p{which}r", 8192, F32R), F32R)
            r = region(arena(f"p{which}f", 6528))
            wb = region(WB[:, 4096:8208])
            keep_v = wb(2048)
            keep = tiles_ring(keep_v.rearrange("p (t d) -> p t d", t=8), 8)
            K = [[RR(1024, c=2, n=512) for _ in range(2)] for _ in range(2)]
            Q = [[RR(1024, c=2, o=2, n=256) for _ in range(2)] for _ in range(2)]
            V = [r(1024, t=4, n=256) for _ in range(2)]
            Pr, PTr = Ring([r(512) for _ in range(4)]), Ring([r(1024) for _ in range(2)])
            xT = [wb(512, c=2, n=256) for _ in range(2)]
            OTs = wb(1024, c=4, n=256)
            r2 = region(keep_v)
            xn = r2(512, t=2, d=256)
            kn = Ring([r2(512) for _ in range(3)])
            sm, rc, mx = small[:, 512:516], small[:, 516:520], small[:, 520:524]
            ss = Ring([small[:, 528 + 8 * k:536 + 8 * k] for k in range(3)])
            qs8 = small[:, 524:525]
            Sr, Tr, Or, Ur, Mr = ring_of(0, 1), ring_of(2, 3), ring_of(4), ring_of(5), ring_of(6, 7)
            wq, wk, wv, wo = W
            m_qs = ts(qs8, col("qs"), 8.0, None, ALU.mult, None, a_cst, f)
            hm, _ = norm_T(X, Xm, keep, HT, mv, pre, evac_affine(zw, zb), second=True)
            m_z = [DV.do(lambda e, v=Q[j][k][64 * (1 - o):64 * (1 - o) + 64, :, o, :].bitcast(F32): e.memset(v, 0.0))
                   for j in range(2) for k in range(2) for o in range(2)]
            f2 = fence()
            SP.wait(f2)
            sx = sem(f"d_x{which}")
            neg = None
            if which == 1:
                nb = r(256, dt=BF16)
                mk = r(128, dt=U8)
                a_mk = load("mk", [(mk[32 * j:32 * j + 1, :], io["mask1"][0:1, 512 * j:512 * j + 512]) for j in range(4)])
                neg = [ts(nb[32 * j:32 * j + 1, :], mk[32 * j:32 * j + 1, :], 1.0, BIG, ALU.subtract, ALU.mult, a_mk)
                       for j in range(4)]

            xm, x_free = {}, {}
            s_last, p_last, ready, o_done, o_free = {}, {}, {}, {}, {}

            def fetch(b):
                SP.dma(sx, lambda e: e.dma_start(xn, io["ctx"][b * 256:(b + 1) * 256, :].rearrange("(t p) d -> p t d", p=128)),
                       x_free.get(b - 1))
                return Arrival(sx, 16 * (b + 1))

            def context(b):
                a = arrived[b]
                ms = [ts(xn[:, t, :], xn[:, t, :], cmv[:, 2 * b + t, 0:1], crs[:, 2 * b + t:2 * b + t + 1], ALU.subtract,
                         ALU.mult, a, m_crs) for t in range(2)]
                yield
                bk = Mr.take()
                for c in range(2):
                    for t in range(2):
                        m = tr(bk.ap[:, (2 * c + t) * 128:(2 * c + t + 1) * 128], xn[:, t, c * 128:(c + 1) * 128], ident[:, :],
                               ms, bk.free)
                x_free[b] = m
                if b < 7:
                    arrived[b + 1] = fetch(b + 1)
                yield
                last = [ready.get(2 * b - 3)]
                for c in range(2):
                    m1 = act(xT[b % 2][:, c, :], bk.ap[:, c * 256:(c + 1) * 256], ACT.Identity, m, last, a_cst,
                             scale=col(xw, c), bias=col(xb, c))
                xm[b] = bk.free = m1

            arrived = {0: fetch(0)}

            def project(g):
                b, hg = divmod(g, 2)
                s = g % 2
                at = slice(hg * 256, hg * 256 + 256)
                done = []
                kfree, vfree = s_last.get(g - 2), p_last.get(g - 2)

                def src(t):
                    if t < 2:
                        return xT[b % 2][:, :, t * 128:(t + 1) * 128], xm[b]
                    return HT[:, :, b * 256 + (t - 2) * 128:b * 256 + (t - 1) * 128], hm[2 * b + t - 2]

                def both(t):
                    if t < 2:
                        return xT[b % 2], xm[b]
                    return HT[:, :, b * 256:b * 256 + 256], [hm[2 * b], hm[2 * b + 1]]

                def split_k(pair, i, sc, m, slot):
                    hi, lo = (K[s][k][:, :, pair * 256:(pair + 1) * 256] for k in range(2))
                    m1 = act(hi, i, ACT.Copy, m, kfree, m_qs, scale=sc)
                    slot.free = DV.do(lambda e: e.scalar_tensor_tensor(out=lo, in0=i, scalar=sc, in1=hi.bitcast(F32),
                                                                       op0=ALU.mult, op1=ALU.subtract), m1, kfree)
                    done.append(slot.free)

                def split_q(i, sc, m, slot):
                    for o in range(2):
                        p = slice(64 * o, 64 * o + 64)
                        hi, lo = (Q[s][k][p, :, o, :] for k in range(2))
                        m = act(hi, i[p], ACT.Copy, m, kfree, m_qs, m_z, scale=sc if isinstance(sc, float) else sc[p])
                    for o in range(2):
                        p = slice(64 * o, 64 * o + 64)
                        hi, lo = (Q[s][k][p, :, o, :] for k in range(2))
                        slot.free = DV.do(lambda e, p=p, hi=hi, lo=lo: e.scalar_tensor_tensor(
                            out=lo, in0=i[p], scalar=sc if isinstance(sc, float) else sc[p], in1=hi.bitcast(F32),
                            op0=ALU.mult, op1=ALU.subtract), m, kfree)
                        done.append(slot.free)

                def value(pair):
                    bk = Mr.take()
                    for j in range(2):
                        sr, dep = src(2 * pair + j)
                        for k in range(2):
                            m = mm(bk.ap[:, j * 256:(j + 1) * 256], sr[:, k, :], wv[:, k, at], k == 0, k == 1, dep, a_w, bk.free)
                    yield
                    m = act(V[s][:, 2 * pair:2 * pair + 2, :], bk.ap.rearrange("p (t n) -> p t n", t=2), ACT.Copy, m, vfree)
                    bk.free = m
                    done.append(m)

                def normed(t, w, name):
                    bk = Mr.take()
                    for j in range(2):
                        sr, dep = src(t + j)
                        for k in range(2):
                            m = mm(bk.ap[:, j * 256:(j + 1) * 256], sr[:, k, :], w[:, k, at], k == 0, k == 1, dep, a_w, bk.free)
                    yield
                    z = kn.take()
                    zv = z.ap.rearrange("p (h d) -> p h d", h=8)
                    m1 = act(z.ap, bk.ap, ACT.Square, m, z.free)
                    v = ss.take()
                    m2 = red(v.ap, zv, ALU.add, m1, v.free)
                    m3 = rstd(v.ap, v.ap, 8, m2, eps=1e-24, op=ALU.max)
                    yield
                    m4 = tt(zv, bk.ap.rearrange("p (h d) -> p h d", h=8),
                            v.ap.rearrange("p (h o) -> p h o", o=1).to_broadcast([128, 8, 64]), ALU.mult, m3)
                    v.free = bk.free = m4
                    yield
                    T = Ur.take()
                    for c in range(2):
                        for j in range(2):
                            m = tr(T.ap[:, (2 * c + j) * 128:(2 * c + j + 1) * 128],
                                   z.ap[:, j * 256 + c * 128:j * 256 + (c + 1) * 128], ident[:, :], m4, T.free)
                    z.free = m
                    yield
                    i = T.ap.rearrange("p (c n) -> p c n", c=2)
                    if name == "q":
                        split_q(i, qs8, m, T)
                    else:
                        split_k(name, i, col("ks"), m, T)

                def plain(t, w, name):
                    bk = Mr.take()
                    sr, dep = both(t)
                    for c in range(2):
                        for k in range(2):
                            m = mm(bk.ap[:, c * 256:(c + 1) * 256], w[:, k, hg * 256 + c * 128:hg * 256 + (c + 1) * 128],
                                   sr[:, k, :], k == 0, k == 1, dep, a_w, bk.free)
                    yield
                    i = bk.ap.rearrange("p (c n) -> p c n", c=2)
                    if name == "q":
                        split_q(i, 0.125, m, bk)
                    else:
                        split_k(name, i, 1.0, m, bk)

                ready[g] = done
                if which == 1:
                    return [normed(0, wk, 0), normed(2, wk, 1), normed(2, wq, "q"), value(0), value(1)]
                return [plain(0, wk, 0), plain(2, wk, 1), plain(2, wq, "q"), value(0), value(1)]

            def scores(i, S):
                g, rest = divmod(i, 8)
                h, a = divmod(rest, 2)
                b = g // 2
                c, o = divmod(h, 2)
                (kh, kl), (qh, ql) = K[g % 2], Q[g % 2]
                q = slice(a * 128, a * 128 + 128)
                mm(S.ap, qh[:, c, o, q], kh[:, c, :], True, False, ready[g], S.free)
                mm(S.ap, qh[:, c, o, q], kl[:, c, :], False, False)
                m = mm(S.ap, ql[:, c, o, q], kh[:, c, :], False, which != 1)
                if which == 1:
                    p = 32 * (b // 2)
                    m = mm(S.ap[:, 0:256], onesbb[p:p + 1, :], nb[p:p + 1, (b % 2) * 256:(b % 2) * 256 + 256], False, True, neg, m_one)
                s_last[g] = m
                return m

            O = {}

            def pv(i, PT, *after):
                g, rest = divmod(i, 8)
                h = rest // 2
                if h == 0:
                    O[g] = Or.take()
                o = O[g].ap[64 * (h % 2):64 * (h % 2) + 64, h // 2 * 256:h // 2 * 256 + 256]
                for k in range(4):
                    m = mm(o, V[g % 2][:, k, h * 64:(h + 1) * 64], PT[:, k * 256:(k + 1) * 256], k == 0, k == 3, after, O[g].free)
                if h == 3:
                    p_last[g] = m
                    b, hg = divmod(g, 2)
                    mo = act(OTs[:, 2 * hg:2 * hg + 2, :], O[g].ap.rearrange("p (c n) -> p c n", c=2), ACT.Copy, m,
                             o_free.get(b - 1))
                    O[g].free = mo
                    o_done[b] = [o_done.get(b), mo]
                return m

            def out_proj(b):
                bk = Mr.take()
                for a in range(2):
                    for c in range(4):
                        m = mm(bk.ap[:, a * 256:(a + 1) * 256], OTs[:, c, a * 128:(a + 1) * 128], wo[:, c, :],
                               c == 0, c == 3, o_done[b], bk.free)
                    yield
                o_free[b] = m
                if which == 2:
                    for a in range(2):
                        bk.free = residual(2 * b + a, bk.ap[:, a * 256:(a + 1) * 256], m)
                    return
                ms = [stats(mv2[:, 2 * b + a, :], bk.ap[:, a * 256:(a + 1) * 256], a, m) for a in range(2)]
                mr = rstd(rs[:, 2 * b:2 * b + 2], mv2[:, 2 * b:2 * b + 2, 1], 2, ms)
                yield
                y = kn.take()
                m1 = [ts(y.ap[:, a * 256:(a + 1) * 256], bk.ap[:, a * 256:(a + 1) * 256], mv2[:, 2 * b + a, 0:1],
                         rs[:, 2 * b + a:2 * b + a + 1], ALU.subtract, ALU.mult, mr, ms, y.free) for a in range(2)]
                bk.free = m1
                yield
                m2 = {}
                for a in range(2):
                    v = y.ap[:, a * 256:(a + 1) * 256]
                    m2[a] = tt(v, v, row("low"), ALU.mult, m1, a_rows, q=PO)
                    m2[a] = tt(v, v, row("lob"), ALU.add, m2[a], q=PO)
                yield
                for a in range(2):
                    y.free = residual(2 * b + a, y.ap[:, a * 256:(a + 1) * 256], m2[a])

            turns([context(0)])
            turns([context(1)])
            steps = ((0, 5), (1, 5), (2, 5), (4, 2), (5, 2)) if which == 1 else ((0, 2), (1, 2), (2, 2), (4, 2), (5, 2))
            turns(project(0), [2 * at for at, _ in steps])
            hooks = {}
            made = {}

            def part(g, j):
                if g not in made:
                    made[g] = project(g)
                return made[g][j]

            for g in range(16):
                if g > 0 and g % 2 == 0:
                    spread(hooks, {8 * g + 6: (6 if which == 1 else 3, lambda g=g: out_proj(g // 2 - 1))})
                if g < 15:
                    for j, (at, n) in enumerate(steps):
                        spread(hooks, {8 * g + at: (n, lambda g=g, j=j: part(g + 1, j))})
                if g % 2 == 1 and g < 13:
                    spread(hooks, {8 * g + 6: (3, lambda g=g: context(g // 2 + 2))})
            attention(128, 1, scores, pv, hooks, Pr, PTr, mx, sm, rc, Sr, Tr)
            turns([out_proj(7)])
            leave()

        def all_max(dst, src, n, ring, *after):
            m = red(dst, src, ALU.max, *after)
            b = ring.take()
            m = tr(b.ap[0:1, 0:128], dst, ident[:, :], m, b.free)
            m = red(dst[0:1, :], b.ap[0:1, 0:128], ALU.max, m)
            m = mm(b.ap[:, 256:257], onesf[0:1, :], dst[0:1, :], True, True, m, m_one)
            m = cp(dst, b.ap[:, 256:257], m)
            b.free = m
            return m

        def layer1_ffn(WI, WO, a_w):
            f = fence()
            AR = arena("f1a", 14336)
            r = region(AR)
            am = small[:, 0:64]
            sc = small[:, 64:72]
            keep = tiles_ring(r(2048, t=8, d=256), 8)
            for s in keep.slots:
                s.free = f
            hid3 = AR[:, 0:12288].rearrange("p (g f n) -> p g f n", g=3, f=8)
            W1 = AR[:, 12288:14336].rearrange("p (k n) -> p k n", k=2)
            hid1 = WB[:, 4096:8192].rearrange("p (f n) -> p f n", f=8)

            def hid(n):
                return hid3[:, n, :, :] if n < 3 else hid1
            aw = small[:, 80:96]
            sw = small[:, 96:112]
            iw = small[:, 112:128]
            wm = []
            for j, Wt in ((0, WI), (8, WO)):
                m = red(aw[:, j:j + 8], Wt, ALU.max, a_w, f, apply_absolute_value=True)
                wm.append(m)
            m = ts(aw, aw, 1e-8, None, ALU.max, None, wm)
            m = recip(sw, aw, m)
            m = ts(sw, sw, 127.0, None, ALU.mult, None, m)
            mi = ts(iw, aw, 1.0 / 127.0, None, ALU.mult, None, m)
            w_ready = []
            for j, Wt in ((0, WI), (8, WO)):
                for k in range(8):
                    m1 = ts(Wt[:, k, :], Wt[:, k, :], sw[:, j + k:j + k + 1], MAGIC, ALU.mult, ALU.add, m, mi)
                    m1 = ts(Wt[:, k, :], Wt[:, k, :], MAGIC, iw[:, j + k:j + k + 1], ALU.subtract, ALU.mult, m1)
                    w_ready.append(m1)
            t1 = []
            rr = ring_of(4, 5)
            for k in range(2):
                for q in range(2):
                    b = rr.take()
                    for j in range(4):
                        m = tr(b.ap[:, j * 128:(j + 1) * 128], WI[:, 4 * q + j, k * 128:(k + 1) * 128], ident[:, :],
                               w_ready, b.free)
                    m = act(W1[:, k, q * 512:(q + 1) * 512], b.ap, ACT.Copy, m, f)
                    b.free = m
                    t1.append(m)

            def hook(t, s, m):
                s.free = red(am[:, t:t + 1], s.ap, ALU.max, m, f, apply_absolute_value=True)

            hm, _ = norm_T(X, Xm, keep, HT, mv, pre, evac_copy, hook=hook)
            m = all_max(sc[:, 0:1], am[:, 0:16], 16, ring_of(7), DV.last)
            m = ts(sc[:, 0:1], sc[:, 0:1], 1e-8, None, ALU.max, None, m)
            m = recip(sc[:, 1:2], sc[:, 0:1], m)
            m = ts(sc[:, 1:2], sc[:, 1:2], 32767.0, None, ALU.mult, None, m)
            m = ts(sc[:, 2:3], sc[:, 0:1], 1.0 / 32767.0, None, ALU.mult, None, m)
            hq = []
            for n in range(4):
                v = HT[:, :, n * 512:(n + 1) * 512]
                m1 = ts(v, v, sc[:, 1:2], MAGIC, ALU.mult, ALU.add, m, hm[4 * n:4 * n + 4])
                hq.append(ts(v, v, MAGIC, sc[:, 2:3], ALU.subtract, ALU.mult, m1))
            f3 = [hm, w_ready, t1]
            Hr, Yr = ring_of(0, 1, 2, 3), ring_of(4, 5, 6)
            gm = []
            for n in range(4):
                for k in range(8):
                    b = Hr.take()
                    for c in range(2):
                        m = mm(b.ap, W1[:, c, k * 128:(k + 1) * 128], HT[:, c, n * 512:(n + 1) * 512], c == 0, c == 1,
                               hq[n], t1, b.free)
                    m = act(hid(n)[:, k, :], b.ap, ACT.Gelu, m, f3, a_cst, bias=col("bin", k))
                    b.free = m
                    u = small[:, 160 + 8 * n + k:161 + 8 * n + k]
                    gm.append(red(u, hid(n)[:, k, :], ALU.max, m, apply_absolute_value=True))
            m = all_max(sc[:, 3:4], small[:, 160:192], 32, ring_of(7), gm)
            m = ts(sc[:, 3:4], sc[:, 3:4], 1e-8, None, ALU.max, None, m)
            m = recip(sc[:, 4:5], sc[:, 3:4], m)
            m = ts(sc[:, 4:5], sc[:, 4:5], 32767.0, None, ALU.mult, None, m)
            ms = ts(sc[:, 5:6], sc[:, 3:4], 1.0 / 32767.0, None, ALU.mult, None, m)
            for n in range(4):
                qs = []
                for k in range(0, 8, 2):
                    v = hid(n)[:, k:k + 2, :]
                    m1 = ts(v, v, sc[:, 4:5], MAGIC, ALU.mult, ALU.add, ms)
                    qs.append(ts(v, v, MAGIC, sc[:, 5:6], ALU.subtract, ALU.mult, m1))
                for j in range(4):
                    t = 4 * n + j
                    b = Yr.take()
                    for k in range(8):
                        m = mm(b.ap[:, 0:256], hid(n)[:, k, j * 128:(j + 1) * 128], WO[:, k, :], k == 0, k == 7,
                               qs, b.free)
                    Xm[t] = tt(X[:, t, :], X[:, t, :], row("bout"), ALU.add, Xm[t], a_rows)
                    b.free = residual(t, b.ap[:, 0:256], m)
            leave()

        def layer3_attention(wq, wk, wv, wo, a_w):
            f = fence()
            r = region(arena("x3a", 14336))
            Hn = r(4096, t=16, d=256)
            keep = tiles_ring(Hn, 16)
            for s in keep.slots:
                s.free = f
            hm, tok = norm_T(X, Xm, keep, HT, mv, pre, evac_copy)
            mk = r(1024, dt=U8, t=16, n=256)
            a_m = load("mask0", [(mk, io["mask0"].rearrange("(t p) n -> p t n", p=128))], f)
            pen = small[:, 0:16]
            m = red(pen, mk, ALU.max, a_m, f)
            m_pen = ts(pen, pen, -3.0e38, 3.0e38, ALU.mult, ALU.mult, m)
            Ks, Vs, Qs, As, Cs = (Ring([r(512, a=2, n=256) for _ in range(2)]) for _ in range(5))
            Qs.slots.append(Slot(r(512, a=2, n=256)))
            ys = Ring([r(256) for _ in range(4)])
            R = ring_of(0, 1, 2, 3, 4, 5, 6, 7)

            def first(b):
                lo = b * 256
                kv = []
                for w, rg, bias in ((wk, Ks, "bk"), (wv, Vs, "bv")):
                    bk = R.take()
                    for a in range(2):
                        for k in range(2):
                            m = mm(bk.ap[:, a * 256:(a + 1) * 256], ctxT[:, k, lo + a * 128:lo + (a + 1) * 128], w[:, k, :],
                                   k == 0, k == 1, a_w, bk.free, ctx_m[2 * b + a])
                    s = rg.take()
                    m = tt(s.ap, bk.ap.rearrange("p (a n) -> p a n", a=2),
                           row(bias).rearrange("p (o n) -> p o n", o=1).to_broadcast([128, 2, 256]), ALU.add, m, s.free, a_rows, f)
                    bk.free = m
                    kv.append((s, m))
                bk = R.take()
                for c in range(2):
                    for k in range(2):
                        m = mm(bk.ap[:, c * 256:(c + 1) * 256], wq[:, k, c * 128:(c + 1) * 128], HT[:, k, lo:lo + 256],
                               k == 0, k == 1, a_w, bk.free, hm[2 * b], hm[2 * b + 1])
                q = Qs.take()
                for c in range(2):
                    m2 = act(q.ap[:, c, :], bk.ap[:, c * 256:(c + 1) * 256], ACT.Identity, m, q.free, a_cst, f, bias=col("bq", c))
                bk.free = m2
                return kv, (q, m2)

            def second(b, kv, q):
                (K, mk_), (V, mv_) = kv
                bk = R.take()
                for c in range(2):
                    for a in range(2):
                        m = mm(bk.ap[:, c * 128:(c + 1) * 128], K.ap[:, a, c * 128:(c + 1) * 128],
                               V.ap[:, a, c * 128:(c + 1) * 128], a == 0, a == 1, mk_, mv_, bk.free)
                K.free = V.free = m
                A = As.take()
                m = tt(A.ap[:, 0, :].rearrange("p (c n) -> p c n", c=2), bk.ap[:, 0:256].rearrange("p (c n) -> p c n", c=2),
                       blk[:, :].rearrange("p (o n) -> p o n", o=1).to_broadcast([128, 2, 128]), ALU.mult, m, A.free, a_cst, f)
                bk.free = m
                return A, m

            def third(b, q, A, am_):
                bk = R.take()
                for c in range(2):
                    m = mm(bk.ap[:, c * 256:(c + 1) * 256], A.ap[:, 0, c * 128:(c + 1) * 128], q[0].ap[:, c, :], True, True,
                           am_, q[1], bk.free)
                q[0].free = A.free = m
                C = Cs.take()
                m = act(C.ap, bk.ap.rearrange("p (c n) -> p c n", c=2), ACT.Copy, m, C.free, f)
                bk.free = m
                return C, m

            def fourth(b, C, cm):
                bk = R.take()
                for a in range(2):
                    for c in range(2):
                        m = mm(bk.ap[:, a * 256:(a + 1) * 256], C.ap[:, c, a * 128:(a + 1) * 128], wo[:, c, :],
                               c == 0, c == 1, cm, bk.free)
                C.free = m
                mms = []
                yy = []
                for a in range(2):
                    t = 2 * b + a
                    y = ys.take()
                    m1 = tt(y.ap, bk.ap[:, a * 256:(a + 1) * 256], row("bo"), ALU.add, m, y.free, a_rows, f)
                    bk.free = m1
                    m1 = DV.do(lambda e, y=y, t=t: e.scalar_tensor_tensor(out=y.ap, in0=Hn[:, t, :], scalar=pen[:, t:t + 1],
                               in1=y.ap, op0=ALU.add, op1=ALU.add), m1, m_pen, tok[t])
                    mms.append(stats(mv2[:, t, :], y.ap, t, m1))
                    yy.append(y)
                mr = rstd(rs[:, 2 * b:2 * b + 2], mv2[:, 2 * b:2 * b + 2, 1], 2, mms, tok[2 * b], tok[2 * b + 1])
                for a in range(2):
                    t = 2 * b + a
                    y = yy[a]
                    m1 = ts(y.ap, y.ap, mv2[:, t, 0:1], rs[:, t:t + 1], ALU.subtract, ALU.mult, mr, mms)
                    m1 = tt(y.ap, y.ap, row("lng"), ALU.mult, m1, q=PO)
                    m1 = tt(y.ap, y.ap, row("lnb"), ALU.add, m1, q=PO)
                    y.free = residual(t, y.ap, m1)

            s1, s2, s3 = {}, {}, {}
            for i in range(8 + 3):
                if i < 8:
                    s1[i] = first(i)
                if 0 <= i - 1 < 8:
                    s2[i - 1] = second(i - 1, *s1[i - 1])
                if 0 <= i - 2 < 8:
                    s3[i - 2] = third(i - 2, s1[i - 2][1], *s2[i - 2])
                if 0 <= i - 3 < 8:
                    fourth(i - 3, *s3[i - 3])
            leave()

        def layer3_ffn(w1, w2, a_w):
            f = fence()
            r = region(arena("f3a", 10240))
            rb = region(WB)
            wq1 = r(1024, dt=BF16, k=2, n=1024)
            wq2 = r(1024, dt=BF16, k=8, n=256)
            sc = small[:, 0:8]
            hs, scr = Ring([rb(1024) for _ in range(4)]), Ring([rb(1024) for _ in range(3)])
            hb = Ring([r(512, dt=BF16) for _ in range(3)])
            hT = Ring([r(512, dt=BF16, k=8, n=128) for _ in range(3)])
            xs = Ring([r(256) for _ in range(4)])
            xb = Ring([r(128, dt=BF16) for _ in range(3)])
            xT = Ring([r(128, dt=BF16, k=2, n=128) for _ in range(3)])
            ys = Ring([r(256) for _ in range(3)])
            stt = small[:, 128:128 + 16 * 16].rearrange("p (t s) -> p t s", t=16)
            Hr, Tr, Yr = ring_of(0, 1, 2, 3), ring_of(4, 5), ring_of(6, 7)
            iws = [sc[:, 2:3], sc[:, 6:7]]
            wr = [[], []]

            def weight(j, w, wq):
                v, s, i = (sc[:, 4 * j + k:4 * j + k + 1] for k in range(3))
                m = red(v, w.rearrange("p k n -> p (k n)"), ALU.add, a_w, f, apply_absolute_value=True)
                yield
                b = Yr.take()
                m = mm(b.ap[:, 0:1], onesf[:, :], v, True, True, m, b.free, m_one)
                yield
                m = ts(i, b.ap[:, 0:1], 1.0 / 262144.0, 1e-5, ALU.mult, ALU.max, m)
                b.free = m
                m = recip(s, i, m)
                yield
                m = ts(w, w, s, MAGIC, ALU.mult, ALU.add, m)
                yield
                m = ts(w, w, MAGIC, 1.0, ALU.subtract, ALU.min, m)
                yield
                wr[j].append(ts(wq, w, -1.0, None, ALU.max, None, m))

            def quant(t, src, srcm, n, base, ring, wi, out_):
                c = [stt[:, t, base + k:base + k + 1] for k in range(4)]
                q = scr.take()
                m1 = act(q.ap[:, 0:n], src, ACT.Square, srcm, q.free, f, accum_out=c[0])
                q.free = m1
                m2 = red(c[1], src, ALU.max, srcm, f, apply_absolute_value=True)
                yield
                m3 = ts(c[0], c[0], 1.0 / n, 1e-5, ALU.mult, ALU.add, m1, q=PO)
                m3 = PO.do(lambda e: e.tensor_tensor(c[0], c[0], nhalf[:, 0:1], ALU.pow), m3, m_nh)
                yield
                m4 = ts(c[1], c[1], c[0], 1e-5, ALU.mult, ALU.max, m3, m2)
                ma = act(src, src, ACT.Copy, m3, m2, m1, scale=c[0])
                yield
                m5 = recip(c[2], c[1], m4)
                m7 = ts(c[3], c[1], iws[wi], 1.0 / 127.0, ALU.mult, ALU.mult, m4, wr[wi])
                yield
                m6 = ts(c[2], c[2], 127.0, None, ALU.mult, None, m5)
                yield
                m8 = ts(src, src, c[2], MAGIC, ALU.mult, ALU.add, m6, ma)
                yield
                d = ring.take()
                m9 = act(d.ap, src, ACT.Copy, m8, d.free, f, bias=-MAGIC)
                out_.extend([d, m9, m7, c[3]])

            turns([weight(0, w1, wq1)])
            rs_m = []
            for g in range(4):
                ms = [known.pop(t) for t in range(4 * g, 4 * g + 4)]
                rs_m.append(rstd(rs[:, 4 * g:4 * g + 4], mv[:, 4 * g:4 * g + 4, 1], 4, ms, f))

            def tile(t):
                x = xs.take()
                m = ts(x.ap, X[:, t, :], mv[:, t, 0:1], rs[:, t:t + 1], ALU.subtract, ALU.mult, rs_m[t // 4], x.free, Xm[t])
                yield
                o = []
                yield from quant(t, x.ap, m, 256, 0, xb, 0, o)
                d, md, ms, sx = o
                x.free = md
                yield
                T = Tr.take()
                tv = T.ap.bitcast(BF16)
                for k in range(2):
                    m = tr(tv[:, k * 128:(k + 1) * 128], d.ap[:, k * 128:(k + 1) * 128], identb[:, :], md, T.free, m_id)
                d.free = m
                yield
                xt = xT.take()
                m = T.free = act(xt.ap, tv[:, 0:256].rearrange("p (k n) -> p k n", k=2), ACT.Copy, m, xt.free, f)
                yield
                bs = [Hr.take() for _ in range(2)]
                mp = []
                for q in range(2):
                    for k in range(2):
                        m1 = mm(bs[q].ap, xt.ap[:, k, :], wq1[:, k, q * 512:(q + 1) * 512], k == 0, k == 1, m, wr[0], bs[q].free)
                    mp.append(m1)
                xt.free = m1
                yield
                h = hs.take()
                for q in range(2):
                    fb = row("fb1")[:, q * 512:(q + 1) * 512]
                    bs[q].free = DV.do(lambda e, q=q, fb=fb: e.scalar_tensor_tensor(
                        out=h.ap[:, q * 512:(q + 1) * 512], in0=bs[q].ap, scalar=sx, in1=fb, op0=ALU.mult, op1=ALU.add),
                        mp[q], ms, h.free, a_rows, f)
                yield
                m = act(h.ap, h.ap, ACT.Gelu, bs[0].free, bs[1].free)
                yield
                o2 = []
                yield from quant(t, h.ap, m, 1024, 8, hb, 1, o2)
                d2, md2, ms2, sx2 = o2
                h.free = md2
                yield
                T2 = Tr.take()
                tw = T2.ap.bitcast(BF16)
                for k in range(8):
                    m = tr(tw[:, k * 128:(k + 1) * 128], d2.ap[:, k * 128:(k + 1) * 128], identb[:, :], md2, T2.free)
                d2.free = m
                yield
                xt2 = hT.take()
                m = T2.free = act(xt2.ap, tw.rearrange("p (k n) -> p k n", k=8), ACT.Copy, m, xt2.free, f)
                yield
                b = Yr.take()
                for k in range(8):
                    mp2 = mm(b.ap[:, 0:256], xt2.ap[:, k, :], wq2[:, k, :], k == 0, k == 7, m, wr[1], b.free)
                xt2.free = mp2
                yield
                y = ys.take()
                m = DV.do(lambda e: e.scalar_tensor_tensor(out=y.ap, in0=b.ap[:, 0:256], scalar=sx2, in1=row("fb2"),
                                                           op0=ALU.mult, op1=ALU.add), mp2, ms2, y.free, a_rows, f)
                b.free = m
                yield
                m = tt(X[:, t, :], X[:, t, :], y.ap, ALU.add, m, Xm[t], q=PO)
                y.free = m
                Xm[t] = m

            turns([weight(1, w2, wq2)] + [tile(t) for t in range(16)], [0] + [3 * t for t in range(16)])
            leave()

        layer0_attention()
        e0 = PE.last
        wt = region(WA)
        W1 = (wt(1024, k=2, n=512), wt(1024, k=2, n=512), wt(1024, k=2, n=512), wt(1024, k=4, n=256))
        WI, WO = wt(2048, f=8, n=256), wt(2048, f=8, n=256)
        e0 = [e0, cleared0, cleared2]
        a_w1 = load("w1", [(W1[0], wview(io["L1Wq"])), (W1[1], wview(io["L1Wkv"])[:, :, 0:512]),
                           (W1[2], wview(io["L1Wkv"])[:, :, 512:1024]), (W1[3], wview(io["L1Wo"]))], e0)
        a_wf1 = load("wf1", [(WI, wview(io["L1WinT"])), (WO, wview(io["L1Wout"]))], e0)
        layer0_ffn()
        e1 = PE.last
        wt = region(WB)
        W2 = (wt(1024, k=2, n=512), wt(1024, k=2, n=512), wt(1024, k=2, n=512), wt(1024, k=4, n=256))
        a_w2 = load("w2", [(W2[0], wview(io["L2Wq"])), (W2[1], wview(io["L2Wk"])),
                           (W2[2], wview(io["L2Wv"])), (W2[3], wview(io["L2Wout"]))], e1)
        perceiver(1, W1, a_w1, "lxw", "lxb", "llw", "llb")
        layer1_ffn(WI, WO, a_wf1)
        e3 = PE.last
        wt = region(WA)
        W3 = [wt(512, k=2, n=256) for _ in range(4)]
        F1, F2 = wt(2048, k=2, n=1024), wt(2048, k=8, n=256)
        a_w3 = load("w3", [(W3[0], wview(io["L3wqT"])), (W3[1], wview(io["L3wkT"])),
                           (W3[2], wview(io["L3wvT"])), (W3[3], wview(io["L3woT"]))], e3)
        a_f3 = load("f3", [(F1, wview(io["L3w1T"])), (F2, wview(io["L3w2T"]))], e3)
        perceiver(2, W2, a_w2, "mw", "mb", "zw", "zb")
        layer2_ffn()
        layer3_attention(*W3, a_w3)
        layer3_ffn(F1, F2, a_f3)
        s_out = sem("s_out")
        ov = out.rearrange("(t p) d -> p t d", p=128)
        for g in range(4):
            SP.dma(s_out, lambda e, g=g: e.dma_start(ov[:, 4 * g:4 * g + 4, :], X[:, 4 * g:4 * g + 4, :]),
                   Xm[4 * g:4 * g + 4])
        SP.wait(Arrival(s_out, 64))

        for q in (PE, DV, AC, PO, SP):
            q.count()
        block = ctx.enter_context(nc.Block())

        @block.tensor
        def _(eng):
            PE.emit(eng)

        @block.vector
        def _(eng):
            DV.emit(eng)

        @block.scalar
        def _(eng):
            AC.emit(eng)

        @block.gpsimd
        def _(eng):
            PO.emit(eng)

        @block.sync
        def _(eng):
            SP.emit(eng)


def _constants():
    c = np.zeros((128, 944), np.float32)
    c[:, 0:128] = np.eye(128, dtype=np.float32)
    q = np.arange(128)[:, None]
    k = np.arange(256)[None, :]
    c[:, 128:384] = np.where(k > q, -25.0, 0.0)
    c[:, 384:640] = np.where(k > q + 128, -25.0, 0.0)
    i = np.arange(128)
    c[:, 640:768] = np.where(i[:, None] < i[None, :], 1.0, 0.0)
    c[:, 896:944] = np.arange(48)[None, :]
    c[:, 768:896] = np.where(i[:, None] // 16 == i[None, :] // 16, 0.25, 0.0)
    return c


def kernel(**inputs):
    import concourse.bacc as bacc
    from concourse.bass_utils import run_bass_kernel_spmd as run
    a = {k: np.asarray(v) for k, v in inputs.items()}

    def pc(v):
        return v.reshape(-1, 128).T

    def wide(w):
        z = np.zeros((16, 32, 256), np.float32)
        z[:, 0:16, :] = w.reshape(16, 16, 256)
        return z.reshape(512, 256)

    def pack(w1, w2, b1):
        w1, w2, b1 = a[w1], a[w2], a[b1]
        return np.concatenate([w1.reshape(8, 2, 128, -1).transpose(0, 2, 1, 3).reshape(8, 128, -1),
                               w2.reshape(8, -1, 128, 256).transpose(0, 2, 1, 3).reshape(8, 128, -1),
                               b1.reshape(8, -1, 128).transpose(0, 2, 1)], axis=2)

    cols = np.concatenate([
        pc(a["L1_xattn_ln_x_w"]), pc(a["L1_xattn_ln_x_b"]), pc(a["L1_xattn_ln_l_w"]), pc(a["L1_xattn_ln_l_b"]),
        pc(np.tile(a["L1_xattn_k_scale"], 2)), pc(np.tile(a["L1_xattn_q_scale"], 2)),
        pc(a["L2_xattn_ln_media_w"]), pc(a["L2_xattn_ln_media_b"]), pc(a["L2_xattn_ln_lat_w"]), pc(a["L2_xattn_ln_lat_b"]),
        pc(a["L1_ffn_b_in"]), pc(a["L3_xattn_wq_b"])], axis=1)
    rows = np.concatenate([
        a["L1_xattn_ln_o_w"], a["L1_xattn_ln_o_b"], a["L1_ffn_b_out"], a["L3_xattn_wk_b"], a["L3_xattn_wv_b"],
        a["L3_xattn_wo_b"], a["L3_xattn_ln_g"], a["L3_xattn_ln_b"], a["L3_ffn_b1"], a["L3_ffn_b2"], a["L2_ffn_bg"]])[None, :]
    data = {
        "x": a["x"].reshape(2048, 256), "ctx": a["ctx_1024"].reshape(2048, 256),
        "mask1": a["mask_BxS2_bk0"].reshape(1, 2048),
        "mask0": a["mask_Bx1xSxS2_bf0"].reshape(2048, 256),
        "cols": cols, "rows": rows, "consts": _constants(),
        "L0wqT": a["L0_xattn_Wq"].T, "L0wkT": a["L0_xattn_Wk"].T,
        "L0wvT": a["L0_xattn_Wv"].T, "L0woT": wide(a["L0_xattn_Wo"].T),
        "L0gate": a["L0_ffn_gate_w"], "L0pack": pack("L0_ffn_w1", "L0_ffn_w2", "L0_ffn_b1"), "L0b2": a["L0_ffn_b2"],
        "L1Wq": a["L1_xattn_Wq"], "L1Wkv": a["L1_xattn_Wkv"], "L1Wo": a["L1_xattn_Wo"],
        "L1WinT": a["L1_ffn_W_in"].T, "L1Wout": a["L1_ffn_W_out"],
        "L2Wq": a["L2_xattn_Wq"], "L2Wk": a["L2_xattn_Wk"], "L2Wv": a["L2_xattn_Wv"], "L2Wout": a["L2_xattn_Wout"],
        "L2Wg": a["L2_ffn_Wg"], "L2pack": pack("L2_ffn_W1", "L2_ffn_W2", "L2_ffn_b1"), "L2b2": a["L2_ffn_b2"],
        "L3wqT": a["L3_xattn_wq_w"].T, "L3wkT": a["L3_xattn_wk_w"].T, "L3wvT": a["L3_xattn_wv_w"].T,
        "L3woT": a["L3_xattn_wo_w"].T, "L3w1T": a["L3_ffn_w1"].T, "L3w2T": a["L3_ffn_w2"].T,
    }
    nc = bacc.Bacc("TRN2", target_bir_lowering=False, num_devices=1)
    arrays, io = {}, {}
    for name, v in data.items():
        v = np.ascontiguousarray(v)
        arrays["in_" + name] = v
        io[name] = nc.dram_tensor("in_" + name, v.shape, mybir.dt.from_np(v.dtype), kind="ExternalInput").ap()
    out = nc.dram_tensor("out_0", (2048, 256), F32, kind="ExternalOutput").ap()
    build(nc, io, out)
    r = run(nc, [arrays], core_ids=[0])
    return r.results[0]["out_0"].reshape(8, 256, 256)
```
